# Optimizing a Trainium2 kernel written in Bass

```python
import numpy as np
import jax
import jax.numpy as jnp

def _softmax(x, axis=-1):
    return jax.nn.softmax(x, axis=axis)

def _gelu(x):
    return jax.nn.gelu(x, approximate=True)

def _silu(x):
    return jax.nn.silu(x)

def _sigmoid(x):
    return jax.nn.sigmoid(x)

def _layernorm(x, axis=-1, eps=1e-05):
    m = jnp.mean(x, axis=axis, keepdims=True)
    v = jnp.var(x, axis=axis, keepdims=True)
    return (x - m) / jnp.sqrt(v + eps)

def _scatter_add(tgt, idx, src, axis=0):
    return tgt.at[idx].add(src)

def _segment_sum(src, seg, n):
    return jax.ops.segment_sum(src, seg, n)
kernel_name = 'mk_adaln_d1_jaxref_r4_1d4b77'

def setup_inputs(seed: int=0):
    np.random.seed(seed)
    _w = jnp.asarray

    def _L0_attn_setup():
        import math
        import jax, jax.numpy as jnp
        import numpy as np
        B, T, D_MODEL, N_HEADS = (2, 512, 256, 16)
        HEAD_DIM = D_MODEL // N_HEADS

        def _alibi_slopes(n_heads: int) -> np.ndarray:

            def pow2(n):
                start = 2.0 ** (-(8.0 / n))
                return [start * start ** i for i in range(n)]
            if math.log2(n_heads).is_integer():
                s = pow2(n_heads)
            else:
                cp = 2 ** math.floor(math.log2(n_heads))
                base = pow2(cp)
                extra = pow2(2 * cp)[1::2]
                s = base + extra[:n_heads - cp]
            return np.asarray(s, dtype=np.float32)
        SLOPES = jnp.asarray(_alibi_slopes(N_HEADS))
        key = jax.random.key(seed)
        k1, k2, k3 = jax.random.split(key, 3)
        x = jax.random.normal(k1, (B, T, D_MODEL), dtype=jnp.float32)
        Wqkv = jax.random.normal(k2, (D_MODEL, 3 * D_MODEL), dtype=jnp.float32) * 0.02
        Wout = jax.random.normal(k3, (D_MODEL, D_MODEL), dtype=jnp.float32) * 0.02
        return {'x': x, 'Wqkv': Wqkv, 'Wout': Wout}
    _L0_attn_in = _L0_attn_setup()

    def _L0_ffn_setup():
        import jax, jax.numpy as jnp
        import numpy as np
        LN_EPS = 1e-05

        def layer_norm(x, g, b):
            mu = jnp.mean(x, axis=-1, keepdims=True)
            var = jnp.mean(jnp.square(x - mu), axis=-1, keepdims=True)
            return (x - mu) * jax.lax.rsqrt(var + LN_EPS) * g + b

        def ternary_quant(w):
            scale = 1.0 / jnp.clip(jnp.mean(jnp.abs(w)), 1e-05)
            wq = jnp.clip(jnp.round(w * scale), -1.0, 1.0) / scale
            return w + jax.lax.stop_gradient(wq - w)
        key = jax.random.key(seed)
        ks = jax.random.split(key, 3)
        dim, hidden = (256, 1024)
        B, S = (8, 256)
        x = jax.random.normal(ks[0], (B, S, dim), dtype=jnp.float32)
        w1 = jax.random.normal(ks[1], (hidden, dim), dtype=jnp.float32) * 0.02
        w2 = jax.random.normal(ks[2], (dim, hidden), dtype=jnp.float32) * 0.02
        return {'x': x, 'ln1_g': jnp.ones((dim,), jnp.float32), 'ln1_b': jnp.zeros((dim,), jnp.float32), 'w1': w1, 'b1': jnp.zeros((hidden,), jnp.float32), 'ln2_g': jnp.ones((hidden,), jnp.float32), 'ln2_b': jnp.zeros((hidden,), jnp.float32), 'w2': w2, 'b2': jnp.zeros((dim,), jnp.float32)}
    _L0_ffn_in = _L0_ffn_setup()
    _L0_c = _w((lambda *s: np.random.randn(*s).astype(np.float32) * 0.05)(32, 256))
    _L0_wmod = _w((lambda *s: np.random.randn(*s).astype(np.float32) * 0.05)(256, 6 * 256) * 256 ** (-0.5))
    _d = {'L0_attn_x': _L0_attn_in['x'], 'L0_attn_Wqkv': _L0_attn_in['Wqkv'], 'L0_attn_Wout': _L0_attn_in['Wout'], 'L0_ffn_ln1_g': _L0_ffn_in['ln1_g'], 'L0_ffn_ln1_b': _L0_ffn_in['ln1_b'], 'L0_ffn_w1': _L0_ffn_in['w1'], 'L0_ffn_b1': _L0_ffn_in['b1'], 'L0_ffn_ln2_g': _L0_ffn_in['ln2_g'], 'L0_ffn_ln2_b': _L0_ffn_in['ln2_b'], 'L0_ffn_w2': _L0_ffn_in['w2'], 'L0_ffn_b2': _L0_ffn_in['b2'], 'L0_c': _L0_c, 'L0_wmod': _L0_wmod}
    _x0 = _d['L0_attn_x']
    _d['L0_attn_x'] = jax.random.normal(jax.random.fold_in(jax.random.key(seed), 1), (32, 512, 256), dtype=_x0.dtype)
    del _x0
    return _d

def reference(L0_attn_x, L0_attn_Wqkv, L0_attn_Wout, L0_ffn_ln1_g, L0_ffn_ln1_b, L0_ffn_w1, L0_ffn_b1, L0_ffn_ln2_g, L0_ffn_ln2_b, L0_ffn_w2, L0_ffn_b2, L0_c, L0_wmod):

    def _L0_attn_ref(x, Wqkv, Wout):
        import math
        import jax, jax.numpy as jnp
        import numpy as np
        B, T, D_MODEL, N_HEADS = (2, 512, 256, 16)
        HEAD_DIM = D_MODEL // N_HEADS

        def _alibi_slopes(n_heads: int) -> np.ndarray:

            def pow2(n):
                start = 2.0 ** (-(8.0 / n))
                return [start * start ** i for i in range(n)]
            if math.log2(n_heads).is_integer():
                s = pow2(n_heads)
            else:
                cp = 2 ** math.floor(math.log2(n_heads))
                base = pow2(cp)
                extra = pow2(2 * cp)[1::2]
                s = base + extra[:n_heads - cp]
            return np.asarray(s, dtype=np.float32)
        SLOPES = jnp.asarray(_alibi_slopes(N_HEADS))
        Bc, Tc, Dc = x.shape
        qkv = x @ Wqkv
        q, k, v = jnp.split(qkv, 3, axis=-1)
        q = q.reshape(Bc, Tc, N_HEADS, HEAD_DIM)
        k = k.reshape(Bc, Tc, N_HEADS, HEAD_DIM)
        v = v.reshape(Bc, Tc, N_HEADS, HEAD_DIM)
        scale = 1.0 / math.sqrt(HEAD_DIM)
        logits = jnp.einsum('bihd,bjhd->bhij', q, k) * scale
        pos = jnp.arange(Tc, dtype=jnp.float32)
        rel = pos[None, :] - pos[:, None]
        logits = logits + SLOPES[None, :, None, None] * rel[None, None, :, :]
        causal = pos[:, None] >= pos[None, :]
        logits = jnp.where(causal[None, None, :, :], logits, -jnp.inf)
        attn = jax.nn.softmax(logits, axis=-1)
        out = jnp.einsum('bhij,bjhd->bihd', attn, v).reshape(Bc, Tc, Dc)
        return out @ Wout

    def _L0_ffn_ref(x, ln1_g, ln1_b, w1, b1, ln2_g, ln2_b, w2, b2):
        import jax, jax.numpy as jnp
        import numpy as np
        LN_EPS = 1e-05

        def layer_norm(x, g, b):
            mu = jnp.mean(x, axis=-1, keepdims=True)
            var = jnp.mean(jnp.square(x - mu), axis=-1, keepdims=True)
            return (x - mu) * jax.lax.rsqrt(var + LN_EPS) * g + b

        def ternary_quant(w):
            scale = 1.0 / jnp.clip(jnp.mean(jnp.abs(w)), 1e-05)
            wq = jnp.clip(jnp.round(w * scale), -1.0, 1.0) / scale
            return w + jax.lax.stop_gradient(wq - w)
        h = layer_norm(x, ln1_g, ln1_b)
        h = jnp.einsum('bsd,hd->bsh', h, ternary_quant(w1)) + b1
        h = jax.nn.gelu(h, approximate=False)
        h = layer_norm(h, ln2_g, ln2_b)
        out = jnp.einsum('bsh,dh->bsd', h, ternary_quant(w2)) + b2
        return out
    x = L0_attn_x
    mod = (_silu(L0_c) @ L0_wmod).reshape(L0_c.shape[0], 6, 1, -1)
    sa, ca, ga, sb, cb, gb = (mod[:, 0], mod[:, 1], mod[:, 2], mod[:, 3], mod[:, 4], mod[:, 5])
    ga = (2 * (ga >= 0) - 1) * jnp.maximum(jnp.abs(ga), 0.25)
    gb = (2 * (gb >= 0) - 1) * jnp.maximum(jnp.abs(gb), 0.25)
    h = _layernorm(x, axis=-1) * (1 + ca) + sa
    x = x + ga * _L0_attn_ref(h, L0_attn_Wqkv, L0_attn_Wout)
    h = _layernorm(x, axis=-1) * (1 + cb) + sb
    x = x + gb * _L0_ffn_ref(h, L0_ffn_ln1_g, L0_ffn_ln1_b, L0_ffn_w1, L0_ffn_b1, L0_ffn_ln2_g, L0_ffn_ln2_b, L0_ffn_w2, L0_ffn_b2)
    return x

_drawn_inputs = setup_inputs


def setup_inputs(seed=0):
    import zlib

    import numpy as np

    out = dict(_drawn_inputs(seed))
    spreads = {'L0_ffn_ln1_g': (1.0, 0.6),
     'L0_ffn_ln1_b': (0.0, 0.787),
     'L0_ffn_b1': (0.0, 0.1),
     'L0_ffn_ln2_g': (1.0, 0.6),
     'L0_ffn_ln2_b': (0.0, 0.743),
     'L0_ffn_b2': (0.0, 0.332)}
    factors = {'L0_attn_Wqkv': 7.767, 'L0_attn_Wout': 7.791}
    for name, (base, spread) in spreads.items():
        noise = np.random.default_rng([zlib.crc32(name.encode()), seed]).standard_normal(out[name].shape)
        drawn = base * np.exp(spread * noise) if base else spread * noise
        out[name] = jnp.asarray(drawn.astype(out[name].dtype))
    for name, factor in factors.items():
        out[name] = (out[name] * factor).astype(out[name].dtype)
    return out
```

```python
import numpy as np
import concourse.bass as bass
from concourse import mybir
from contextlib import ExitStack

F32 = mybir.dt.float32
F32R = mybir.dt.float32r
BF16 = mybir.dt.bfloat16
ALU = mybir.AluOpType
ACT = mybir.ActivationFunctionType
AX = mybir.AxisListType

P = 128
T = 512
NT = T // P
C = 256
KC = C // P
HEADS = 16
HD = C // HEADS
HG = 4
GROUPS = HEADS // HG
PAIRS = HEADS // 2
UNITS = 10
HID = 1024
KH = HID // P
EPS = 1e-5
MASKED = -1e30
MODS = 6 * C
M_ROW = 63

MISC_USES = (4, 6, 6, 4)
MISC_BEFORE = (0, 2, 5, 8)
MISC_PER_BATCH = 10


def wait(eng, sem, count):
    if isinstance(count, int) and count <= 0:
        return
    eng.wait_ge(sem, count)


def wait_apart(eng, sem, count, passed):
    wait(eng, sem, count)
    eng.sem_inc(passed, 1)


def misc_uses_before(b, slot, order):
    return (b + 1) * MISC_PER_BATCH + MISC_BEFORE[slot] + order // 2


def head_of(group, half, side):
    return HG * group + 2 * half + side


def setup_phase(nc, io, keep, ctx):
    def sb(name, shape, dt=F32):
        return ctx.enter_context(nc.sbuf_tensor(name, shape, dt))

    def sem(name):
        return ctx.enter_context(nc.semaphore(name))

    NB = io["x"].shape[0]
    w_mod = sb("w_mod", [P, KC, MODS])
    c_t = sb("c_t", [P, KC, NB])
    e_t = sb("e_t", [P, KC, NB])
    d_t = sb("d_t", [P, KC, NB])
    silu = sb("silu", [P, KC, NB])
    rows = sb("rows", [NB, MODS])
    sign = sb("sign", [NB, C])
    neg = sb("neg", [NB, C])
    mag = sb("mag", [NB, C])
    col_ps = ctx.enter_context(nc.psum_tensor("col_ps", [P, 12, NB], F32))
    row_ps = [ctx.enter_context(nc.psum_tensor(f"row_ps{i}", [NB, 512], F32)) for i in range(3)]
    loaded, exp_done, silu_done, mod_done, rows_done, rows_out, chain = (
        sem(n) for n in ("s_loaded", "s_exp", "s_silu", "s_mod", "s_rows", "s_rows_out", "s_chain"))
    mod_cols = keep["mod_cols"]
    with nc.Block() as block:
        @block.sync
        def _(sp):
            sp.dma_start(c_t[:, :, :], io["c_t"].rearrange("(k p) b -> p k b", p=P)).then_inc(loaded, 16)
            sp.dma_start(w_mod[:, :, :], io["w_mod"].rearrange("(k p) n -> p k n", p=P)).then_inc(loaded, 16)
            sp.wait_ge(rows_done, 1)
            sp.dma_start(io["mod_rows"], rows[:, :]).then_inc(rows_out, 16)
            sp.wait_ge(rows_out, 16)

        @block.scalar
        def _(act):
            act.wait_ge(loaded, 32)
            act.activation(e_t[:, :, :], c_t[:, :, :], ACT.Exp, scale=-1.0).then_inc(exp_done, 1)

        @block.vector
        def _(dve):
            n = 0

            def link(ins):
                nonlocal n
                n += 1
                ins.then_inc(chain, 1)
                dve.wait_ge(chain, n)

            dve.wait_ge(exp_done, 1)
            link(dve.tensor_scalar_add(d_t[:, :, :], e_t[:, :, :], 1.0))
            link(dve.reciprocal(e_t[:, :, :], d_t[:, :, :]))
            dve.tensor_tensor(silu[:, :, :], c_t[:, :, :], e_t[:, :, :], ALU.mult).then_inc(silu_done, 1)
            dve.wait_ge(mod_done, 1)
            dve.tensor_copy(mod_cols[:, 0:2, :], col_ps[:, 0:2, :])
            dve.tensor_scalar_add(mod_cols[:, 2:4, :], col_ps[:, 2:4, :], 1.0)
            for i in range(3):
                ins = dve.tensor_copy(rows[:, 512 * i:512 * i + 512], row_ps[i][:, :])
            link(ins)
            link(dve.tensor_scalar_add(rows[:, 4 * C:5 * C], rows[:, 4 * C:5 * C], 1.0))
            for gate in (2, 5):
                g = rows[:, gate * C:gate * C + C]
                link(dve.tensor_scalar(sign[:, :], g, 0.0, 2.0, ALU.is_ge, ALU.mult))
                link(dve.tensor_scalar(neg[:, :], g, -1.0, None, ALU.mult))
                link(dve.tensor_tensor(mag[:, :], g, neg[:, :], ALU.max))
                link(dve.tensor_scalar(neg[:, :], mag[:, :], 0.25, None, ALU.max))
                link(dve.tensor_scalar(mag[:, :], sign[:, :], 1.0, None, ALU.subtract))
                link(dve.tensor_tensor(g, mag[:, :], neg[:, :], ALU.mult))
            dve.tensor_copy(sign[:, :], neg[:, :]).then_inc(rows_done, 1)

        @block.tensor
        def _(pe):
            pe.wait_ge(loaded, 32)
            pe.wait_ge(silu_done, 1)
            for j in range(4):
                for k in range(KC):
                    pe.matmul(col_ps[:, j, :], w_mod[:, k, j * P:j * P + P], silu[:, k, :],
                              start=(k == 0), stop=(k == KC - 1))
            for i in range(3):
                for k in range(KC):
                    ins = pe.matmul(row_ps[i][:, :], silu[:, k, :], w_mod[:, k, 512 * i:512 * i + 512],
                                    start=(k == 0), stop=(k == KC - 1))
            ins.then_inc(mod_done, 1)


def attention_phase(nc, io, keep, ctx):
    def sb(name, shape, dt=F32):
        return ctx.enter_context(nc.sbuf_tensor(name, shape, dt))

    def pb(name):
        return ctx.enter_context(nc.psum_tensor(name, [P, 512], F32))

    def sem(name):
        return ctx.enter_context(nc.semaphore(name))

    NB = io["x"].shape[0]
    mod_cols, ident = keep["mod_cols"], keep["ident"]
    w_qkv = sb("w_qkv", [P, KC, 3 * C])
    w_out = sb("w_out", [P, KC, C])
    w_gated = sb("w_gated", [P, KC, C])
    gate = [sb(f"gate{i}", [P, C]) for i in range(2)]
    mask_f = sb("mask_f", [P, 2, P])
    masks = sb("masks", [P, 2, P], BF16)
    mask, mask_t = masks[:, 0, :], masks[:, 1, :]
    ident_b = sb("ident_b", [P, P], BF16)
    half_pow = sb("half_pow", [P, NT])
    x = [sb(f"x{i}", [P, NT, C]) for i in range(2)]
    stats = sb("stats", [P, NT, 6])
    mean_var = sb("mean_var", [P, NT, 2])
    var_eps = sb("var_eps", [P, NT])
    rstd = sb("rstd", [P, NT])
    h_t = [sb(f"h_t{k}", [P, T]) for k in range(KC)]
    dense = {n: sb(f"dense_{n}", [P, 2, T], F32R) for n in ("q_hi", "q_lo", "k_hi", "k_lo")}
    q_st = [sb(f"q_st{i}", [P, PAIRS, T], F32R) for i in range(2)]
    k_st = [sb(f"k_st{i}", [P, PAIRS, T], F32R) for i in range(2)]
    v_ones = [sb(f"v_ones{i}", [P, NT, HEADS, 32]) for i in range(2)]
    probs = [sb(f"probs{i}", [P, UNITS, 512]) for i in range(2)]
    row_max = [sb(f"row_max{i}", [P, 2, 2, NT]) for i in range(2)]
    neg_max = [sb(f"neg_max{i}", [16, P], F32R) for i in range(2)]
    o_sum = [sb(f"o_sum{i}", [P, T]) for i in range(2)]
    recip = sb("recip", [P, 16])
    attn = [sb(f"attn{i}", [P, NT, C]) for i in range(2)]
    attn_t = [sb(f"attn_t{k}", [P, T]) for k in range(KC)]
    res = [sb(f"res{i}", [P, NT, C]) for i in range(2)]

    mx_bank = [pb(f"mx_bank{i}") for i in range(2)]
    ex_bank = [pb(f"ex_bank{i}") for i in range(2)]
    pv_bank = [pb(f"pv_bank{i}") for i in range(2)]
    misc = [pb(f"misc{i}") for i in range(2)]

    const_in, const_ok, dve_const = sem("const_in"), sem("const_ok"), sem("dve_const")
    x_in = [sem(f"x_in{i}") for i in range(2)]
    res_in = [sem(f"res_in{i}") for i in range(2)]
    gate_in = [sem(f"gate_in{i}") for i in range(2)]
    x1_out = [sem(f"x1_out{i}") for i in range(2)]
    stacked = [sem(f"stacked{i}") for i in range(2)]
    max_in = [sem(f"max_in{i}") for i in range(2)]
    stats_ok, aggr_ok, var_ok, rstd_ok, xhat_ok = (sem(n) for n in ("stats_ok", "aggr_ok", "var_ok", "rstd_ok", "xhat_ok"))
    xt_ps, qk_ps, v_ps, mx_ps, ex_ps, pv_ps, ot_ps, mt_ps, at_ps, wo_ps = (
        sem(n) for n in ("xt_ps", "qk_ps", "v_ps", "mx_ps", "ex_ps", "pv_ps", "ot_ps", "mt_ps", "at_ps", "wo_ps"))
    hi_ok, exp_ok, osum_ok = sem("hi_ok"), sem("exp_ok"), sem("osum_ok")
    max_ok, recip_ok = sem("max_ok"), sem("recip_ok")
    gated_ok = sem("gated_ok")
    passed = [sem(f"passed_{e}") for e in ("pool", "dve")]
    misc_ok = [sem(f"misc_ok{i}") for i in range(2)]

    x_d = io["x"].rearrange("b (t p) c -> b p t c", p=P)
    x1_d = io["x1"].rearrange("b (t p) c -> b p t c", p=P)
    mod_rows = io["mod_rows"]
    FIRST, LAST = 4, NB - 2

    def there(n):
        return not isinstance(n, int) or 0 <= n < NB

    def iterations(eng, body, start):
        for b in range(start, FIRST):
            body(b, b // 2, b % 2)
        with eng.Fori(0, (LAST - FIRST) // 2) as i:
            for par in range(2):
                body(i * 2 + (FIRST + par), i + FIRST // 2, par)
        for b in range(LAST, NB + 2):
            body(b, b // 2, b % 2)

    EXACT = ((-1, 2), (-1, 3), (0, 0), (0, 1))
    VALUE = ((-1, 1), (-1, 2), (-1, 3), (0, 0))
    MAXT = ((-1, 3), (0, 0), (0, 1), (0, 2))

    with nc.Block() as block:
        @block.sync
        def _(sp):
            sp.dma_start(w_qkv[:, :, :], io["w_qkv"].rearrange("(k p) n -> p k n", p=P)).then_inc(const_in, 16)
            sp.dma_start(w_out[:, :, :], io["w_out"].rearrange("(k p) n -> p k n", p=P)).then_inc(const_in, 16)
            sp.dma_start(mask_f[:, :, :], io["mask"]).then_inc(const_in, 16)
            for i, n in enumerate(("q_rows", "k_rows")):
                sp.dma_start(probs[i][:, 0:PAIRS, :], io[n]).then_inc(const_in, 16)

            def body(b, hb, par):
                if there(b + 2):
                    wait(sp, xt_ps, KC * (b + 1))
                    sp.dma_start(x[par][:, :, :], x_d[b + 2]).then_inc(x_in[par], 16)
                n = b - 1
                if there(n):
                    q, half = (par + 1) % 2, hb + (par - 1) // 2
                    wait(sp, x1_out[q], 16 * half)
                    sp.dma_start(res[q][:, :, :], x_d[n]).then_inc(res_in[q], 16)
                    wait(sp, gated_ok, n - 1)
                    sp.dma_start(gate[q][:, :], mod_rows[n, 2 * C:3 * C].partition_broadcast(P)).then_inc(gate_in[q], 16)
                n = b + 1
                if there(n):
                    q = (par + 1) % 2
                    wait(sp, ex_ps, GROUPS * UNITS * (n - 1))
                    if isinstance(n, int) and n < 2:
                        sp.wait_ge(const_ok, 1)
                    for tile in range(2):
                        for bank in range(2):
                            sp.wait_ge(misc_ok[bank], misc_uses_before(b, 1 + tile, 2 + bank) + 1)
                        for p in range(4):
                            for st, hi, lo, lo_row in ((q_st, "q_hi", "q_lo", 1), (k_st, "k_hi", "k_lo", 2)):
                                for row in range(3):
                                    src = dense[lo if row == lo_row else hi]
                                    sp.dma_start(st[q][row:P:4, 4 * tile + p, :].bitcast(F32),
                                                 src[32 * p:32 * p + 32, tile, :].bitcast(F32)).then_inc(stacked[tile], 16)
                n = b - 2
                if there(n):
                    for bank in range(2):
                        sp.wait_ge(misc_ok[bank], misc_uses_before(b, 2, 4 + bank) + 1)
                    sp.dma_start(x1_d[n], res[par][:, :, :]).then_inc(x1_out[par], 16)

            iterations(sp, body, -2)
            for i in range(2):
                sp.wait_ge(x1_out[i], 16 * (NB // 2))

        @block.gpsimd
        def _(pool):
            pool.memset(half_pow[:, :], -0.5)
            for i in range(2):
                pool.memset(v_ones[i][:, :, :, :], 1.0)

            def body(b, hb, par):
                n = b - 2
                if there(n):
                    wait(pool, gate_in[par], 16 * hb)
                    wait(pool, wo_ps, 2 * n)
                    if isinstance(n, int) and n == 0:
                        pool.wait_ge(const_in, 16 * 5)
                    for k in range(KC):
                        ins = pool.tensor_tensor(w_gated[:, k, :], w_out[:, k, :], gate[par][:, :], ALU.mult)
                    ins.then_inc(gated_ok, 1)
                for s in range(4):
                    m, mg = MAXT[s]
                    if there(b + m):
                        pool.wait_ge(misc_ok[0], misc_uses_before(b, s, 0) + 1)
                        wait_apart(pool, ex_ps, GROUPS * UNITS * (b + m - 1), passed[0])
                        for half in range(2):
                            pool.dma_start(q_st[(par + m) % 2][M_ROW:P:64, 2 * mg + half, :].bitcast(F32),
                                           neg_max[mg % 2][8 * half:8 * half + 8, :].bitcast(F32)).then_inc(max_in[mg % 2], 16)
                    if s == 3 and there(b + 2):
                        pool.wait_ge(aggr_ok, b + 3)
                        wait_apart(pool, xhat_ok, b + 2, passed[0])
                        pool.tensor_scalar(var_eps[:, :], mean_var[:, :, 1], EPS, None, ALU.add).then_inc(var_ok, 1)
                        pool.wait_ge(var_ok, b + 3)
                        pool.tensor_tensor(rstd[:, :], var_eps[:, :], half_pow[:, :], ALU.pow).then_inc(rstd_ok, 1)

            iterations(pool, body, -2)

        @block.scalar
        def _(act):
            def body(b, hb, par):
                prep = there(b + 1)
                for s in range(4):
                    e, g = EXACT[s]
                    n = b + e
                    v, vg = VALUE[s]
                    for u in range(UNITS):
                        if there(n):
                            act.wait_ge(ex_ps, GROUPS * UNITS * n + UNITS * g + u + 1)
                            if u == 0:
                                wait(act, pv_ps, GROUPS * n + g - 1)
                            act.activation(probs[g % 2][:, u, :], ex_bank[u % 2][:, :], ACT.Exp).then_inc(exp_ok, 1)
                        if s == 0 and u in (6, 8) and prep:
                            k = (u - 6) // 2
                            act.wait_ge(xt_ps, KC * (b + 1) + k + 1)
                            if k == 0:
                                wait(act, v_ps, 2 * (b + 1))
                            act.activation(h_t[k][:, :], misc[k][:, :], ACT.Identity,
                                           bias=mod_cols[:, k, bass.ds(b + 1, 1)],
                                           scale=mod_cols[:, 2 + k, bass.ds(b + 1, 1)]).then_inc(misc_ok[k], 1)
                        if s in (1, 2) and u in (4, 6) and prep:
                            which = "q_hi" if u == 4 else "k_hi"
                            use = 4 * (b + 1) + 2 * (s - 1) + (u - 4) // 2
                            act.wait_ge(qk_ps, use + 1)
                            if u == 4:
                                wait(act, stacked[s - 1], 24 * 16 * (b + 1))
                            act.activation(dense[which][:, s - 1, :], misc[(u - 4) // 2][:, :], ACT.Copy).then_inc(hi_ok, 1)
                        if s == 1 and u >= 8 and there(b - 2):
                            k = u - 8
                            act.wait_ge(at_ps, 2 * (b - 2) + k + 1)
                            wait(act, wo_ps, 2 * (b - 2))
                            act.activation(attn_t[k][:, :], misc[k][:, :], ACT.Copy).then_inc(misc_ok[k], 1)
                        if s == 3 and u in (5, 7) and prep:
                            j = (u - 5) // 2
                            act.wait_ge(v_ps, 2 * (b + 1) + j + 1)
                            wait(act, pv_ps, GROUPS * b)
                            if isinstance(b, int) and b < 1:
                                act.wait_ge(const_ok, 1)
                            for t in range(2):
                                ins = act.activation(v_ones[(par + 1) % 2][:, 2 * j + t, :, 0:HD],
                                                     misc[j][:, C * t:C * t + C].rearrange("p (h d) -> p h d", d=HD),
                                                     ACT.Copy)
                            ins.then_inc(misc_ok[j], 1)
                        if u == 9 and there(b + v):
                            n_pv = GROUPS * (b + v) + vg
                            act.wait_ge(pv_ps, n_pv + 1)
                            wait(act, ot_ps, n_pv - 1)
                            act.activation(o_sum[vg % 2][:, :], pv_bank[vg % 2][:, :], ACT.Copy).then_inc(osum_ok, 1)

            iterations(act, body, -1)

        @block.vector
        def _(dve):
            dve.wait_ge(const_in, 16 * 5)
            dve.tensor_scalar(w_qkv[:, :, 0:C], w_qkv[:, :, 0:C], HD ** -0.5, None, ALU.mult)
            dve.tensor_copy(masks[:, :, :], mask_f[:, :, :])
            dve.tensor_copy(ident_b[:, :], ident[:, :])
            for i in range(2):
                dve.tensor_copy(q_st[i][:, :, :], probs[0][:, 0:PAIRS, :])
                ins = dve.tensor_copy(k_st[i][:, :, :], probs[1][:, 0:PAIRS, :])
            ins.then_inc(dve_const, 1)
            dve.wait_ge(dve_const, 1)
            dve.sem_inc(const_ok, 1)

            def normalise_x(n, q):
                dve.wait_ge(rstd_ok, n + 1)
                for t in range(NT):
                    ins = dve.tensor_scalar(x[q][:, t, :], x[q][:, t, :], mean_var[:, t, 0:1], rstd[:, t:t + 1],
                                            ALU.subtract, ALU.mult)
                ins.then_inc(xhat_ok, 1)

            def statistics(n, half, q):
                dve.wait_ge(x_in[q], 16 * (half + 1))
                wait(dve, xhat_ok, n)
                wait(dve, aggr_ok, n)
                for t in range(NT):
                    ins = dve.bn_stats(stats[:, t, :], x[q][:, t, :])
                ins.then_inc(stats_ok, 1)
                wait_apart(dve, stats_ok, n + 1, passed[1])
                for t in range(NT):
                    ins = dve.bn_aggr(mean_var[:, t, :], stats[:, t, :])
                ins.then_inc(aggr_ok, 1)

            def body(b, hb, par):
                prep = there(b + 1)
                for s in range(4):
                    m, mg = MAXT[s]
                    for u in range(UNITS):
                        if s == 0 and u == 1 and prep:
                            normalise_x(b + 1, (par + 1) % 2)
                        if there(b):
                            side, v = u % 2, u // 2
                            dve.wait_ge(mx_ps, GROUPS * UNITS * b + UNITS * s + u + 1)
                            if u == 0:
                                wait(dve, mt_ps, GROUPS * b + s - 1)
                            bank, out = mx_bank[u % 2], row_max[s % 2]
                            if v in (0, 2):
                                ins = dve.reduce_max(out[:, v // 2, side, 3:4], bank[:, :], AX.X)
                            elif v in (1, 3):
                                dve.reduce_max(out[:, v // 2, side, 0:1], bank[:, 0:P], AX.X)
                                ins = dve.reduce_max(out[:, v // 2, side, 2:3], bank[:, P:512], AX.X)
                            else:
                                ins = dve.reduce_max(out[:, :, side, 1], bank[:, :].rearrange("p (h j) -> p h j", h=2), AX.X)
                            ins.then_inc(max_ok, 1)
                        if u == 2 and there(b + m):
                            n_mt = GROUPS * (b + m) + mg
                            dve.wait_ge(mt_ps, n_mt + 1)
                            wait(dve, max_in[mg % 2], 32 * (2 * (b + m) + mg // 2))
                            dve.tensor_scalar(neg_max[mg % 2][:, :], misc[0][0:16, 0:P], -1.0, None,
                                              ALU.mult).then_inc(misc_ok[0], 1)
                        if u == (4 if s == 0 else 3) and there(b - 1):
                            n_ot = GROUPS * (b - 1) + s
                            dve.wait_ge(ot_ps, n_ot + 1)
                            wait(dve, misc_ok[1], misc_uses_before(b - 1, 3, 1) + 1 if s == 0 else misc_uses_before(b, s - 1, 1) + 1)
                            ot = misc[1][:, :].rearrange("p (a c) -> p a c", c=32)
                            dve.reciprocal(recip[:, :], ot[:, :, HD]).then_inc(recip_ok, 1)
                            dve.wait_ge(recip_ok, n_ot + 1)
                            wait(dve, at_ps, 2 * (b - 2))
                            dve.tensor_tensor(
                                attn[(par + 1) % 2][:, :, 64 * s:64 * s + 64].rearrange("p i (h d) -> p i h d", d=HD),
                                ot[:, :, 0:HD].rearrange("p (i h) d -> p i h d", h=HG),
                                recip[:, :].rearrange("p (i h) -> p i h", h=HG).unsqueeze(3).to_broadcast([P, NT, HG, HD]),
                                ALU.mult).then_inc(misc_ok[1], 1)
                        if s in (1, 2) and u in (5, 7) and prep:
                            hi, lo = ("q_hi", "q_lo") if u == 5 else ("k_hi", "k_lo")
                            use = 4 * (b + 1) + 2 * (s - 1) + (u - 5) // 2
                            dve.wait_ge(hi_ok, use + 1)
                            wait(dve, stacked[s - 1], 24 * 16 * (b + 1))
                            dve.tensor_tensor(dense[lo][:, s - 1, :], misc[(u - 5) // 2][:, :],
                                              dense[hi][:, s - 1, :].bitcast(F32), ALU.subtract).then_inc(misc_ok[(u - 5) // 2], 1)
                        if s == 3 and u < 2 and there(b - 2):
                            n, j = b - 2, u
                            dve.wait_ge(wo_ps, 2 * n + j + 1)
                            wait(dve, res_in[par], 16 * hb)
                            dve.tensor_tensor(res[par][:, 2 * j:2 * j + 2, :], res[par][:, 2 * j:2 * j + 2, :],
                                              misc[j][:, :].rearrange("p (t c) -> p t c", t=2), ALU.add).then_inc(misc_ok[j], 1)
                        if s == 3 and u == 4 and there(b + 2):
                            statistics(b + 2, hb + 1, par)

            iterations(dve, body, -2)

        @block.tensor
        def _(pe):
            pe.wait_ge(const_ok, 1)

            def misc_free(b, s, order):
                wait(pe, misc_ok[order % 2], misc_uses_before(b, s, order))
                return misc[order % 2]

            def misc_skip(b, s, order):
                wait(pe, misc_ok[order % 2], misc_uses_before(b, s, order))
                pe.sem_inc(misc_ok[order % 2], 1)

            def max_unit(n, g, u, q):
                side, v, bank = u % 2, u // 2, mx_bank[u % 2]
                rows = slice(64 * side, 64 * side + M_ROW)
                unit = GROUPS * UNITS * n + UNITS * g + u
                if u == 0 and g % 2 == 0:
                    pe.wait_ge(stacked[g // 2], 24 * 16 * (n + 1))
                wait(pe, max_ok, unit - 1)

                def scores(pair, block_, keys, at):
                    pe.matmul(bank[:, at:at + keys], q_st[q][rows, pair, P * block_:P * block_ + P],
                              k_st[q][rows, pair, 0:keys], start=True, stop=False)

                def add_mask(at):
                    return pe.matmul(bank[:, at:at + P], ident_b[:, :], mask, start=False, stop=True)

                pair = 2 * g + v // 2
                if v in (0, 2):
                    scores(pair, 3, 512, 0)
                    ins = add_mask(384)
                elif v in (1, 3):
                    scores(pair, 0, 256, 0)
                    add_mask(0)
                    scores(pair, 2, 384, P)
                    ins = add_mask(384)
                else:
                    for half in range(2):
                        scores(2 * g + half, 1, 256, 256 * half)
                        ins = add_mask(256 * half + P)
                ins.then_inc(mx_ps, 1)

            def exact_unit(n, g, u, q):
                side, v, bank = (u + 1) % 2, u // 2, ex_bank[u % 2]
                rows = slice(64 * side, 64 * side + 64)
                unit = GROUPS * UNITS * n + UNITS * g + u
                if u == 0:
                    pe.wait_ge(max_in[g % 2], 32 * (2 * n + g // 2 + 1))
                wait(pe, exp_ok, unit - 1)

                def scores(pair, keys, first, at):
                    pe.matmul(bank[:, at:at + T - first], k_st[q][rows, pair, P * keys:P * keys + P],
                              q_st[q][rows, pair, first:T], start=True, stop=False)

                def add_mask(at):
                    return pe.matmul(bank[:, at:at + P], ident_b[:, :], mask_t, start=False, stop=True)

                pair = 2 * g + v // 2
                if v in (0, 2):
                    scores(pair, 0, 0, 0)
                    ins = add_mask(0)
                elif v in (1, 3):
                    scores(pair, 3, 256, 256)
                    add_mask(384)
                    scores(pair, 1, P, 0)
                    ins = add_mask(0)
                else:
                    for half in range(2):
                        scores(2 * g + half, 2, 256, 256 * half)
                        ins = add_mask(256 * half)
                ins.then_inc(ex_ps, 1)

            def values(n, g, q, keys):
                if keys == 0:
                    pe.wait_ge(exp_ok, GROUPS * UNITS * n + UNITS * (g + 1))
                    wait(pe, osum_ok, GROUPS * n + g - 1)
                for hh in range(HG):
                    half, side = hh // 2, hh % 2
                    odd = 1 - side
                    if keys == 0:
                        moving = probs[g % 2][:, 4 * half + odd, :]
                    elif keys == 1:
                        moving = probs[g % 2][:, 4 * half + 2 + odd, 0:384]
                    elif keys == 3:
                        moving = probs[g % 2][:, 4 * half + 2 + odd, 384:512]
                    else:
                        moving = probs[g % 2][:, 8 + odd, 256 * half:256 * half + 256]
                    ins = pe.matmul(pv_bank[g % 2][32 * hh:32 * hh + 32, P * keys:T],
                                    v_ones[q][:, keys, HG * g + hh, :], moving, start=(keys == 0), stop=(keys == NT - 1))
                if keys == NT - 1:
                    ins.then_inc(pv_ps, 1)

            def body(b, hb, par):
                prep = there(b + 1)
                for s in range(4):
                    e, eg = EXACT[s]
                    v, vg = VALUE[s]
                    m, mg = MAXT[s]
                    for u in range(UNITS):
                        if there(b):
                            max_unit(b, s, u, par)
                        if there(b + e):
                            exact_unit(b + e, eg, u, (par + e) % 2)
                        if u in (1, 3, 5, 7) and there(b + v):
                            values(b + v, vg, (par + v) % 2, (u - 1) // 2)
                        if u == 1:
                            if there(b + m):
                                bank = misc_free(b, s, 0)
                                pe.wait_ge(max_ok, (GROUPS * (b + m) + mg + 1) * UNITS)
                                pe.matmul(bank[0:16, 0:P], row_max[mg % 2][:, :, :, :].rearrange("p a b c -> p (a b c)"),
                                          ident[:, :], start=True, stop=True).then_inc(mt_ps, 1)
                            else:
                                misc_skip(b, s, 0)
                        if u == (3 if s == 0 else 2):
                            if there(b - 1):
                                bank = misc_free(b, s, 1)
                                pe.wait_ge(osum_ok, GROUPS * (b - 1) + s + 1)
                                for i in range(NT):
                                    ins = pe.transpose(bank[:, P * i:P * i + P], o_sum[s % 2][:, P * i:P * i + P], ident[:, :])
                                ins.then_inc(ot_ps, 1)
                            else:
                                misc_skip(b, s, 1)
                        if s == 0 and u in (5, 7):
                            k = (u - 5) // 2
                            if prep:
                                bank = misc_free(b, s, 2 + k)
                                pe.wait_ge(xhat_ok, b + 2)
                                for t in range(NT):
                                    ins = pe.transpose(bank[:, P * t:P * t + P], x[(par + 1) % 2][:, t, P * k:P * k + P], ident[:, :])
                                ins.then_inc(xt_ps, 1)
                            else:
                                misc_skip(b, s, 2 + k)
                        if s in (1, 2) and u in (3, 5):
                            j = (u - 3) // 2
                            if prep:
                                bank = misc_free(b, s, 2 + j)
                                for i in range(KC):
                                    pe.wait_ge(misc_ok[i], misc_uses_before(b, 0, 2 + i) + 1)
                                col = C * j + P * (s - 1)
                                for k in range(KC):
                                    ins = pe.matmul(bank[:, :], w_qkv[:, k, col:col + P], h_t[k][:, :],
                                                    start=(k == 0), stop=(k == KC - 1))
                                ins.then_inc(qk_ps, 1)
                            else:
                                misc_skip(b, s, 2 + j)
                        if s == 1 and u in (7, 8):
                            k = u - 7
                            if there(b - 2):
                                bank = misc_free(b, s, 4 + k)
                                pe.wait_ge(misc_ok[1], misc_uses_before(b - 1, 3, 1) + 1)
                                for t in range(NT):
                                    ins = pe.transpose(bank[:, P * t:P * t + P], attn[par][:, t, P * k:P * k + P], ident[:, :])
                                ins.then_inc(at_ps, 1)
                            else:
                                misc_skip(b, s, 4 + k)
                        if s == 2 and u in (7, 8):
                            j = u - 7
                            if there(b - 2):
                                bank = misc_free(b, s, 4 + j)
                                for i in range(KC):
                                    pe.wait_ge(misc_ok[i], misc_uses_before(b, 1, 4 + i) + 1)
                                pe.wait_ge(gated_ok, b - 1)
                                for t in range(2):
                                    for k in range(KC):
                                        tok = P * (2 * j + t)
                                        ins = pe.matmul(bank[:, C * t:C * t + C], attn_t[k][:, tok:tok + P], w_gated[:, k, :],
                                                        start=(k == 0), stop=(k == KC - 1))
                                ins.then_inc(wo_ps, 1)
                            else:
                                misc_skip(b, s, 4 + j)
                        if s == 3 and u in (4, 6):
                            j = (u - 4) // 2
                            if prep:
                                bank = misc_free(b, s, 2 + j)
                                for t in range(2):
                                    for k in range(KC):
                                        tok = P * (2 * j + t)
                                        ins = pe.matmul(bank[:, C * t:C * t + C], h_t[k][:, tok:tok + P], w_qkv[:, k, 2 * C:3 * C],
                                                        start=(k == 0), stop=(k == KC - 1))
                                ins.then_inc(v_ps, 1)
                            else:
                                misc_skip(b, s, 2 + j)

            iterations(pe, body, -1)


def ternary_phase(nc, io, keep, ctx):
    def sb(name, shape, dt=F32):
        return ctx.enter_context(nc.sbuf_tensor(name, shape, dt))

    def sem(name):
        return ctx.enter_context(nc.semaphore(name))

    ident = keep["ident"]
    raw = [sb("raw1", [P, KC * HID]), sb("raw2", [P, KH * C])]
    over = sb("over", [P, HID * KC])
    under = sb("under", [P, HID * KC])
    tern2_f = sb("tern2_f", [P, KH * C])
    absw = sb("absw", [P, HID * KC])
    part = sb("part", [P, 2])
    mean = sb("mean", [P, 2])
    clipped = sb("clipped", [P, 2])
    scale = sb("scale", [P, 2])
    ones = sb("ones", [P, P])
    b1_two = sb("b1_two", [2, HID])
    b1_s = sb("b1_s", [2, HID])
    b1_hi = sb("b1_hi", [2, HID], F32R)
    minus_row1 = sb("minus_row1", [2, 1])
    g2 = sb("g2", [P, HID])
    ln2_b = sb("ln2_b", [P, KH])
    b2_all = sb("b2_all", [P, C])
    shift_l = sb("shift_l", [P, KH, P])
    tmp_c = sb("tmp_c", [P, C])
    sum_ps = ctx.enter_context(nc.psum_tensor("sum_ps", [P, 2], F32))
    const_ps = ctx.enter_context(nc.psum_tensor("const_ps", [P, C], F32))
    loaded, abs_ok, ones_ok, sum_ok, chain, tern_ok, const_ok = (
        sem(n) for n in ("t_loaded", "t_abs", "t_ones", "t_sum", "t_chain", "t_tern", "t_const"))
    count = 1.0 / (HID * C)
    n_loads = 8
    with nc.Block() as block:
        @block.sync
        def _(sp):
            sp.dma_start(raw[0][:, :].rearrange("p (k n) -> p k n", k=KC), io["w1"].rearrange("(k p) n -> p k n", p=P)).then_inc(loaded, 16)
            sp.dma_start(raw[1][:, :].rearrange("p (k n) -> p k n", k=KH), io["w2"].rearrange("(k p) n -> p k n", p=P)).then_inc(loaded, 16)
            sp.dma_start(b1_two[:, :], io["b1"].partition_broadcast(2)).then_inc(loaded, 16)
            sp.dma_start(g2[:, :], io["ln2_g"].partition_broadcast(P)).then_inc(loaded, 16)
            sp.dma_start(b2_all[:, :], io["b2"].partition_broadcast(P)).then_inc(loaded, 16)
            sp.dma_start(ln2_b[:, :], io["ln2_b"]).then_inc(loaded, 16)
            sp.dma_start(keep["ln1_g"][:, :], io["ln1_g"]).then_inc(loaded, 16)
            sp.dma_start(keep["ln1_b"][:, :], io["ln1_b"]).then_inc(loaded, 16)
            sp.wait_ge(loaded, 16 * n_loads)

        @block.scalar
        def _(act):
            act.wait_ge(loaded, 16 * n_loads)
            act.activation(absw[:, :], raw[0][:, :], ACT.Abs, accum_out=part[:, 0:1]).then_inc(abs_ok, 1)
            act.wait_ge(abs_ok, 1)
            act.activation(absw[:, :], raw[1][:, :], ACT.Abs, accum_out=part[:, 1:2]).then_inc(abs_ok, 1)

        @block.tensor
        def _(pe):
            pe.wait_ge(ones_ok, 1)
            pe.wait_ge(abs_ok, 2)
            pe.matmul(sum_ps[:, :], ones[:, :], part[:, :], start=True, stop=True).then_inc(sum_ok, 1)
            pe.wait_ge(tern_ok, 1)
            for k in range(KH):
                ins = pe.matmul(const_ps[:, :], shift_l[:, k, :], tern2_f[:, C * k:C * k + C], start=(k == 0), stop=(k == KH - 1))
            ins.then_inc(const_ok, 1)

        @block.vector
        def _(dve):
            n = 0

            def link(ins):
                nonlocal n
                n += 1
                ins.then_inc(chain, 1)
                dve.wait_ge(chain, n)

            dve.memset(ones[:, :], 1.0).then_inc(ones_ok, 1)
            dve.wait_ge(ones_ok, 1)
            dve.tensor_copy(keep["ones2"][:, :], ones[0:2, :])
            dve.wait_ge(loaded, 16 * n_loads)
            dve.wait_ge(sum_ok, 1)
            link(dve.tensor_scalar(mean[:, :], sum_ps[:, :], count, None, ALU.mult))
            link(dve.tensor_scalar(clipped[:, :], mean[:, :], 1e-5, None, ALU.max))
            link(dve.reciprocal(scale[:, :], clipped[:, :]))
            link(dve.reciprocal(keep["inv_scale"][:, :], scale[:, :]))
            for i in range(2):
                link(dve.tensor_scalar(over[:, :], raw[i][:, :], scale[:, i:i + 1], 0.5, ALU.mult, ALU.is_gt))
                link(dve.tensor_scalar(under[:, :], raw[i][:, :], scale[:, i:i + 1], -0.5, ALU.mult, ALU.is_lt))
                link(dve.tensor_tensor(keep["tern1"][:, :] if i == 0 else tern2_f[:, :], over[:, :], under[:, :], ALU.subtract))
            link(dve.tensor_copy(keep["tern2"][:, :], tern2_f[:, :]))
            link(dve.tensor_scalar(b1_s[:, :], b1_two[:, :], scale[0:2, 0:1], None, ALU.mult))
            link(dve.tensor_copy(b1_hi[:, :], b1_s[:, :]))
            link(dve.tensor_scalar(minus_row1[:, :], ident[0:2, 1:2], -1.0, None, ALU.mult))
            link(dve.scalar_tensor_tensor(out=keep["bias1"][:, :], in0=b1_hi[:, :].bitcast(F32), scalar=minus_row1[:, 0:1],
                                          in1=b1_s[:, :], op0=ALU.mult, op1=ALU.add))
            link(dve.tensor_scalar(keep["gain2"][:, :], g2[:, :], keep["inv_scale"][:, 1:2], None, ALU.mult))
            link(dve.tensor_copy(shift_l[:, :, :], ln2_b[:, :].unsqueeze(2).to_broadcast([P, KH, P])))
            dve.tensor_copy(over[:, 0:P], shift_l[:, 0, :]).then_inc(tern_ok, 1)
            dve.wait_ge(const_ok, 1)
            link(dve.tensor_scalar(tmp_c[:, :], const_ps[:, :], keep["inv_scale"][:, 1:2], None, ALU.mult))
            link(dve.tensor_tensor(keep["const_row"][:, :], tmp_c[:, :], b2_all[:, :], ALU.add))


def ffn_phase(nc, io, keep, ctx):
    def sb(name, shape, dt=F32):
        return ctx.enter_context(nc.sbuf_tensor(name, shape, dt))

    def pb(name, n):
        return ctx.enter_context(nc.psum_tensor(name, [P, n], F32))

    def sem(name):
        return ctx.enter_context(nc.semaphore(name))

    NB = io["x"].shape[0]
    ident = keep["ident"]
    half_pow = sb("f_half_pow", [P, NT])
    x1 = [sb(f"f_x1{i}", [P, NT, C]) for i in range(2)]
    base = [sb(f"f_base{i}", [P, NT, C]) for i in range(2)]
    shift_scale = [sb(f"f_ss{i}", [P, 2, C]) for i in range(2)]
    gate = [sb(f"f_gate{i}", [P, C]) for i in range(2)]
    gated_const = sb("f_gc", [P, C])
    xh = sb("f_xh", [P, NT, C])
    h0 = sb("f_h0", [P, NT, C])
    h1 = sb("f_h1", [P, NT, C])
    hf = [sb(f"f_hf{i}", [P, KC, 2 * P]) for i in range(2)]
    h_hi = [sb(f"f_hhi{i}", [P, KC, T], F32R) for i in range(2)]
    h_lo = [sb(f"f_hlo{i}", [P, KC, T], F32R) for i in range(2)]
    stats = sb("f_stats", [P, NT, 6])
    mv = [sb(f"f_mv{i}", [P, NT, 2]) for i in range(2)]
    ve = [sb(f"f_ve{i}", [P, NT]) for i in range(2)]
    rs = [sb(f"f_rs{i}", [P, NT]) for i in range(2)]
    ustats = sb("f_ustats", [P, 2, 6])
    umv = [sb(f"f_umv{i}", [P, 2]) for i in range(2)]
    uve = [sb(f"f_uve{i}", [P, 1]) for i in range(2)]
    urs = [sb(f"f_urs{i}", [P, 1]) for i in range(2)]
    u_act = [sb(f"f_u{i}", [P, HID]) for i in range(2)]
    u_c = [sb(f"f_uc{i}", [P, HID]) for i in range(2)]
    u_hi = [sb(f"f_uhi{i}", [P, HID], F32R) for i in range(2)]
    u_lo = [sb(f"f_ulo{i}", [P, HID], F32R) for i in range(2)]
    y = [sb(f"f_y{i}", [P, C]) for i in range(2)]
    up_ps = [pb(f"up_ps{i}", 2 * 512) for i in range(2)]
    ut_ps = pb("ut_ps", 2 * 512)
    down_ps = pb("down_ps", 2 * C)
    xt_ps = pb("xt_ps_f", 512)

    passed = [sem(f"f_passed_{e}") for e in ("pool", "dve")]
    x1_in = [sem(f"f_x1_in{i}") for i in range(2)]
    ss_in = [sem(f"f_ss_in{i}") for i in range(2)]
    gate_in = [sem(f"f_gate_in{i}") for i in range(2)]
    out_left = [sem(f"f_out{i}") for i in range(2)]
    st_ok = [sem(f"f_st{i}") for i in range(2)]
    ag_ok = [sem(f"f_ag{i}") for i in range(2)]
    ve_ok = [sem(f"f_ve_ok{i}") for i in range(2)]
    rs_ok = [sem(f"f_rs_ok{i}") for i in range(2)]
    xh_ok, scaled_ok, h0_ok, h1_ok, gc_ok, base_ok = (sem("f_" + n) for n in ("xh", "scaled", "h0", "h1", "gc", "base"))
    xt_ok, hf_ok, hhi_ok, hlo_ok = (sem("f_" + n) for n in ("xt", "hf_ok", "hhi_ok", "hlo_ok"))
    up_ok, gelu_ok, ust_ok, uag_ok, uve_ok, urs_ok, uc_ok, ut_ok, uhi_ok, ulo_ok, down_ok, y_ok, out_ok, pow_ok = (
        sem("f_" + n) for n in ("up", "gelu", "ust", "uag", "uve_ok", "urs_ok", "uc", "ut", "uhi_ok", "ulo_ok", "down", "y_ok", "out_ok", "pow"))

    x1_d = io["x1"].rearrange("b (t p) c -> b p t c", p=P)
    out_d = io["out"].rearrange("b (t p) c -> b p t c", p=P)
    mod_rows = io["mod_rows"]
    FIRST, LAST = 4, NB - 2

    def there(n):
        return not isinstance(n, int) or 0 <= n < NB

    def iterations(eng, body):
        for b in range(-2, FIRST):
            body(b, b // 2, b % 2)
        with eng.Fori(0, (LAST - FIRST) // 2) as i:
            for par in range(2):
                body(i * 2 + (FIRST + par), i + FIRST // 2, par)
        for b in range(LAST, NB + 1):
            body(b, b // 2, b % 2)

    def previous(b, t):
        return (b, t - 1) if t else (b - 1, NT - 1)

    with nc.Block() as block:
        @block.sync
        def _(sp):
            def body(b, hb, par):
                odd = 1 - par
                if there(b + 2):
                    wait(sp, base_ok, b + 1)
                    sp.dma_start(x1[par][:, :, :], x1_d[b + 2]).then_inc(x1_in[par], 16)
                    wait(sp, h0_ok, b + 1)
                    sp.dma_start(shift_scale[par][:, :, :],
                                 mod_rows[b + 2, 3 * C:5 * C].rearrange("(a c) -> a c", a=2).partition_broadcast(P)).then_inc(ss_in[par], 16)
                if there(b + 1):
                    wait(sp, y_ok, NT * b)
                    sp.dma_start(gate[odd][:, :], mod_rows[b + 1, 5 * C:6 * C].partition_broadcast(P)).then_inc(gate_in[odd], 16)
                if there(b - 1):
                    sp.wait_ge(out_ok, NT * b)
                    sp.dma_start(out_d[b - 1], base[odd][:, :, :]).then_inc(out_left[odd], 16)

            iterations(sp, body)
            for i in range(2):
                sp.wait_ge(out_left[i], 16 * (NB // 2))

        @block.gpsimd
        def _(pool):
            pool.memset(half_pow[:, :], -0.5).then_inc(pow_ok, 1)
            pool.wait_ge(pow_ok, 1)

            def rstd(i, n):
                pool.wait_ge(ag_ok[i], n + 1)
                wait_apart(pool, (xh_ok, h1_ok)[i], n, passed[0])
                pool.tensor_scalar(ve[i][:, :], mv[i][:, :, 1], EPS, None, ALU.add).then_inc(ve_ok[i], 1)
                pool.wait_ge(ve_ok[i], n + 1)
                pool.tensor_tensor(rs[i][:, :], ve[i][:, :], half_pow[:, :], ALU.pow).then_inc(rs_ok[i], 1)

            def body(b, hb, par):
                odd = 1 - par
                for t in range(NT):
                    if there(b):
                        tile = NT * b + t
                        pool.wait_ge(uag_ok, tile + 1)
                        wait_apart(pool, y_ok, tile - 1, passed[0])
                        pool.tensor_scalar(uve[t % 2][:, :], umv[t % 2][:, 1:2], EPS, None, ALU.add).then_inc(uve_ok, 1)
                        pool.wait_ge(uve_ok, tile + 1)
                        pool.tensor_tensor(urs[t % 2][:, :], uve[t % 2][:, :], half_pow[:, 0:1], ALU.pow).then_inc(urs_ok, 1)
                    pb_, pt = previous(b, t)
                    if there(pb_):
                        q = par if t else odd
                        tile = NT * pb_ + pt
                        pool.wait_ge(y_ok, tile + 1)
                        pool.tensor_tensor(base[q][:, pt, :], base[q][:, pt, :], y[pt % 2][:, :], ALU.add).then_inc(out_ok, 1)
                    n = b + 1
                    if there(n) and t == 0:
                        pool.wait_ge(xh_ok, n + 1)
                        wait(pool, ss_in[odd], 16 * (hb + (par + 1) // 2 + 1))
                        wait(pool, h1_ok, n)
                        ss = shift_scale[odd]
                        pool.tensor_tensor(h0[:, :, :], xh[:, :, :], ss[:, 1, :].unsqueeze(1).to_broadcast([P, NT, C]),
                                           ALU.mult).then_inc(scaled_ok, 1)
                        pool.wait_ge(scaled_ok, n + 1)
                        pool.tensor_tensor(h0[:, :, :], h0[:, :, :], ss[:, 0, :].unsqueeze(1).to_broadcast([P, NT, C]),
                                           ALU.add).then_inc(h0_ok, 1)
                    if there(n) and t == 1:
                        rstd(1, n)
                    if there(n) and t == 2:
                        wait(pool, gate_in[odd], 16 * (hb + (par + 1) // 2 + 1))
                        wait(pool, base_ok, n)
                        pool.tensor_tensor(gated_const[:, :], gate[odd][:, :], keep["const_row"][:, :], ALU.mult).then_inc(gc_ok, 1)
                        pool.wait_ge(gc_ok, n + 1)
                        wait(pool, out_left[odd], 16 * (hb + (par + 1) // 2))
                        pool.tensor_tensor(base[odd][:, :, :], x1[odd][:, :, :],
                                           gated_const[:, :].unsqueeze(1).to_broadcast([P, NT, C]), ALU.add).then_inc(base_ok, 1)
                    if there(n) and t == 3:
                        for j in range(2):
                            use = 2 * n + j
                            pool.wait_ge(hhi_ok, use + 1)
                            wait(pool, up_ok, NT * (n - 1))
                            pool.tensor_tensor(h_lo[odd][:, :, 2 * P * j:2 * P * j + 2 * P], hf[j][:, :, :],
                                               h_hi[odd][:, :, 2 * P * j:2 * P * j + 2 * P].bitcast(F32),
                                               ALU.subtract).then_inc(hlo_ok, 1)
                    if there(b + 2) and t == 3:
                        rstd(0, b + 2)

            iterations(pool, body)

        @block.scalar
        def _(act):
            def body(b, hb, par):
                odd = 1 - par
                n = b + 1
                for t in range(NT):
                    if t == 3 and there(n):
                        for j in range(2):
                            use = 2 * n + j
                            act.wait_ge(xt_ok, use + 1)
                            wait(act, hlo_ok, 2 * (n - 1) + j + 1)
                            for k in range(KC):
                                ins = act.activation(hf[j][:, k, :].rearrange("p (t c) -> p t c", t=2),
                                                     xt_ps[:, :].rearrange("p (t k c) -> p k t c", t=2, k=KC)[:, k],
                                                     ACT.Identity, bias=keep["ln1_b"][:, k:k + 1], scale=keep["ln1_g"][:, k:k + 1])
                            ins.then_inc(hf_ok, 1)
                    pb_, pt = previous(b, t)
                    if there(pb_):
                        tile = NT * pb_ + pt
                        act.wait_ge(ut_ok, tile + 1)
                        wait(act, down_ok, tile - 1)
                        act.activation(u_hi[pt % 2][:, :], ut_ps[:, :], ACT.Copy).then_inc(uhi_ok, 1)
                    if there(b):
                        tile = NT * b + t
                        act.wait_ge(up_ok, tile + 1)
                        wait(act, uc_ok, tile - 1)
                        act.activation(u_act[t % 2][:, :], up_ps[t % 2][:, :], ACT.Gelu,
                                       scale=keep["inv_scale"][:, 0:1]).then_inc(gelu_ok, 1)

            iterations(act, body)

        @block.vector
        def _(dve):
            def statistics(i, n, src):
                wait(dve, ag_ok[i], n)
                for t in range(NT):
                    ins = dve.bn_stats(stats[:, t, :], src[:, t, :])
                ins.then_inc(st_ok[i], 1)
                wait_apart(dve, st_ok[i], n + 1, passed[1])
                for t in range(NT):
                    ins = dve.bn_aggr(mv[i][:, t, :], stats[:, t, :])
                ins.then_inc(ag_ok[i], 1)

            def normalise(i, n, dst, src, done):
                dve.wait_ge(rs_ok[i], n + 1)
                for t in range(NT):
                    ins = dve.tensor_scalar(dst[:, t, :], src[:, t, :], mv[i][:, t, 0:1], rs[i][:, t:t + 1], ALU.subtract, ALU.mult)
                ins.then_inc(done, 1)

            def body(b, hb, par):
                odd = 1 - par
                n = b + 1
                for t in range(NT):
                    if there(n) and t == 0:
                        wait(dve, scaled_ok, n)
                        normalise(0, n, xh, x1[odd], xh_ok)
                    if there(n) and t == 1:
                        dve.wait_ge(h0_ok, n + 1)
                        if not isinstance(n, int) or n > 0:
                            dve.wait_ge(h1_ok, n)
                            dve.wait_ge(ag_ok[0], n + 1)
                        statistics(1, n, h0)
                    if there(n) and t == 2:
                        wait(dve, xt_ok, 2 * n)
                        normalise(1, n, h1, h0, h1_ok)
                    pb_, pt = previous(b, t)
                    if there(pb_):
                        q = par if t else odd
                        tile = NT * pb_ + pt
                        dve.wait_ge(uhi_ok, tile + 1)
                        wait(dve, down_ok, tile - 1)
                        dve.tensor_tensor(u_lo[pt % 2][:, :], ut_ps[:, :], u_hi[pt % 2][:, :].bitcast(F32),
                                          ALU.subtract).then_inc(ulo_ok, 1)
                    if there(n) and t == 3:
                        for j in range(2):
                            dve.wait_ge(hf_ok, 2 * n + j + 1)
                            wait(dve, up_ok, NT * (n - 1))
                            dve.tensor_copy(h_hi[odd][:, :, 2 * P * j:2 * P * j + 2 * P], hf[j][:, :, :]).then_inc(hhi_ok, 1)
                    if there(b):
                        tile = NT * b + t
                        dve.wait_ge(gelu_ok, tile + 1)
                        wait(dve, uag_ok, tile)
                        wait(dve, urs_ok, tile - 1)
                        for i in range(2):
                            ins = dve.bn_stats(ustats[:, i, :], u_act[t % 2][:, 512 * i:512 * i + 512])
                        ins.then_inc(ust_ok, 1)
                        wait_apart(dve, ust_ok, tile + 1, passed[1])
                        dve.bn_aggr(umv[t % 2][:, :], ustats[:, :, :]).then_inc(uag_ok, 1)
                        dve.wait_ge(uag_ok, tile + 1)
                        wait(dve, ut_ok, tile - 1)
                        dve.scalar_tensor_tensor(out=u_c[t % 2][:, :], in0=u_act[t % 2][:, :], scalar=umv[t % 2][:, 0:1],
                                                 in1=keep["gain2"][:, :], op0=ALU.subtract, op1=ALU.mult).then_inc(uc_ok, 1)
                    if there(pb_):
                        dve.wait_ge(down_ok, tile_of(pb_, pt) + 1)
                        dve.wait_ge(urs_ok, tile_of(pb_, pt) + 1)
                        wait(dve, gate_in[q], 16 * (hb + 1) if t else 16 * (hb + (par - 1) // 2 + 1))
                        wait(dve, out_ok, tile_of(pb_, pt) - 1)
                        dve.scalar_tensor_tensor(out=y[pt % 2][:, :], in0=down_ps[:, C * (pt % 2):C * (pt % 2) + C],
                                                 scalar=urs[pt % 2][:, 0:1], in1=gate[q][:, :],
                                                 op0=ALU.mult, op1=ALU.mult).then_inc(y_ok, 1)
                    if there(b + 2) and t == 3:
                        dve.wait_ge(x1_in[par], 16 * (hb + 2))
                        wait(dve, xh_ok, b + 2)
                        wait(dve, ag_ok[1], b + 2)
                        statistics(0, b + 2, x1[par])

            def tile_of(batch, t):
                return NT * batch + t

            iterations(dve, body)

        @block.tensor
        def _(pe):
            tern1, tern2 = keep["tern1"], keep["tern2"]

            def body(b, hb, par):
                odd = 1 - par
                n = b + 1
                for t in range(NT):
                    if t == 3 and there(n):
                        pe.wait_ge(h1_ok, n + 1)
                        for j in range(2):
                            wait(pe, hf_ok, 2 * n + j)
                            for tt in range(2):
                                for k in range(KC):
                                    ins = pe.transpose(xt_ps[:, P * (KC * tt + k):P * (KC * tt + k) + P],
                                                       h1[:, 2 * j + tt, P * k:P * k + P], ident[:, :])
                            ins.then_inc(xt_ok, 1)
                    pb_, pt = previous(b, t)
                    if there(pb_):
                        tile = NT * pb_ + pt
                        pe.wait_ge(uc_ok, tile + 1)
                        wait(pe, ulo_ok, tile)
                        for i in range(KH):
                            ins = pe.transpose(ut_ps[:, P * i:P * i + P], u_c[pt % 2][:, P * i:P * i + P], ident[:, :])
                        ins.then_inc(ut_ok, 1)
                    if there(b):
                        tile = NT * b + t
                        pe.wait_ge(hlo_ok, 2 * b + t // 2 + 1)
                        wait(pe, gelu_ok, tile - 1)
                        tok = slice(P * t, P * t + P)
                        for half in range(2):
                            out = up_ps[t % 2][:, 512 * half:512 * half + 512]
                            pe.matmul(out, keep["ones2"][:, :], keep["bias1"][:, 512 * half:512 * half + 512], start=True, stop=False)
                            for k in range(KC):
                                w = tern1[:, HID * k + 512 * half:HID * k + 512 * half + 512]
                                pe.matmul(out, h_lo[par][:, k, tok], w, start=False, stop=False)
                                ins = pe.matmul(out, h_hi[par][:, k, tok], w, start=False, stop=(k == KC - 1))
                        ins.then_inc(up_ok, 1)
                    if there(pb_):
                        tile = NT * pb_ + pt
                        pe.wait_ge(ulo_ok, tile + 1)
                        wait(pe, y_ok, tile - 1)
                        out = down_ps[:, C * (pt % 2):C * (pt % 2) + C]
                        for i in range(KH):
                            w = tern2[:, C * i:C * i + C]
                            pe.matmul(out, u_lo[pt % 2][:, P * i:P * i + P], w, start=(i == 0), stop=False)
                            ins = pe.matmul(out, u_hi[pt % 2][:, P * i:P * i + P], w, start=False, stop=(i == KH - 1))
                        ins.then_inc(down_ok, 1)

            iterations(pe, body)


def adaln_block(nc, io):
    NB = io["x"].shape[0]
    io["mod_rows"] = nc.dram_tensor("mod_rows", [NB, MODS], F32, kind="Internal").ap()
    io["x1"] = nc.dram_tensor("x1_rows", [NB, T, C], F32, kind="Internal").ap()
    with ExitStack() as whole:
        def sb(name, shape, dt=F32):
            return whole.enter_context(nc.sbuf_tensor(name, shape, dt))

        keep = {"mod_cols": sb("mod_cols", [P, 4, NB]), "ident": sb("ident", [P, P])}
        ident_in = whole.enter_context(nc.semaphore("ident_in"))
        with nc.Block() as block:
            @block.sync
            def _(sp):
                sp.dma_start(keep["ident"][:, :], io["ident"]).then_inc(ident_in, 16)
                sp.wait_ge(ident_in, 16)
        with ExitStack() as ctx:
            setup_phase(nc, io, keep, ctx)
        with ExitStack() as ctx:
            attention_phase(nc, io, keep, ctx)
        keep.update({
            "tern1": sb("tern1", [P, KC * HID], F32R), "tern2": sb("tern2", [P, KH * C], F32R),
            "inv_scale": sb("inv_scale", [P, 2]), "bias1": sb("bias1", [2, HID], F32R), "ones2": sb("ones2", [2, P], F32R),
            "gain2": sb("gain2", [P, HID]), "const_row": sb("const_row", [P, C]),
            "ln1_g": sb("ln1_g", [P, KC]), "ln1_b": sb("ln1_b", [P, KC])})
        with ExitStack() as ctx:
            ternary_phase(nc, io, keep, ctx)
        with ExitStack() as ctx:
            ffn_phase(nc, io, keep, ctx)


def round_12(a):
    m, e = np.frexp(a)
    return np.ldexp(np.rint(np.ldexp(m, 12)), e - 12)


def alibi_rows():
    start = 2.0 ** (-8.0 / HEADS)
    slopes = np.asarray([start * start ** i for i in range(HEADS)], np.float32).astype(np.float64)
    pos = np.arange(T, dtype=np.float64)
    q = np.zeros((P, PAIRS, T))
    k = np.zeros((P, PAIRS, T))
    for head, slope in enumerate(slopes):
        base, pair = 64 * (head % 2), head // 2
        hi = round_12(slope)
        left = -slope * pos
        terms = [(hi + 0 * pos, pos), (slope - hi + 0 * pos, pos)]
        for _ in range(3):
            piece = round_12(left)
            terms.append((piece, 1 + 0 * pos))
            left = left - piece
        for row, (a, b) in enumerate(terms):
            q[base + 4 * row + 3, pair], k[base + 4 * row + 3, pair] = a, b
        k[base + M_ROW, pair] = 1.0
    return q.astype(np.float32), k.astype(np.float32)


def constants():
    q, k = alibi_rows()
    mask = np.where(np.arange(P)[None, :] > np.arange(P)[:, None], MASKED, 0.0).astype(np.float32)
    return {"q_rows": q, "k_rows": k, "mask": np.stack([mask, mask.T], 1), "ident": np.eye(P, dtype=np.float32)}


def by_partition(vector):
    return np.asarray(vector).reshape(-1, P).T


def arrays_of(L0_attn_x, L0_attn_Wqkv, L0_attn_Wout, L0_ffn_ln1_g, L0_ffn_ln1_b, L0_ffn_w1, L0_ffn_b1,
              L0_ffn_ln2_g, L0_ffn_ln2_b, L0_ffn_w2, L0_ffn_b2, L0_c, L0_wmod):
    a = {"x": L0_attn_x, "w_qkv": L0_attn_Wqkv, "w_out": L0_attn_Wout, "ln1_g": by_partition(L0_ffn_ln1_g), "ln1_b": by_partition(L0_ffn_ln1_b),
         "w1": np.asarray(L0_ffn_w1).T, "b1": L0_ffn_b1, "ln2_g": L0_ffn_ln2_g, "ln2_b": by_partition(L0_ffn_ln2_b),
         "w2": np.asarray(L0_ffn_w2).T, "b2": L0_ffn_b2, "c_t": np.asarray(L0_c).T, "w_mod": L0_wmod}
    a = {n: np.ascontiguousarray(v) for n, v in a.items()}
    a.update(constants())
    return a


def kernel(**inputs):
    import concourse.bacc as bacc
    from concourse.bass_utils import run_bass_kernel_spmd

    nc = bacc.Bacc("TRN2", target_bir_lowering=False, num_devices=1)
    arrays = arrays_of(**inputs)
    io = {n: nc.dram_tensor(f"in_{n}", a.shape, mybir.dt.from_np(a.dtype), kind="ExternalInput").ap()
          for n, a in arrays.items()}
    io["out"] = nc.dram_tensor("out", arrays["x"].shape, F32, kind="ExternalOutput").ap()
    adaln_block(nc, io)
    result = run_bass_kernel_spmd(nc, [{f"in_{n}": a for n, a in arrays.items()}], core_ids=[0])
    return result.results[0]["out"]
```

```python
import numpy as np
import concourse.bass as bass
from concourse import mybir
from contextlib import ExitStack

F32 = mybir.dt.float32
F32R = mybir.dt.float32r
BF16 = mybir.dt.bfloat16
ALU = mybir.AluOpType
ACT = mybir.ActivationFunctionType
AX = mybir.AxisListType

P = 128
T = 512
NT = T // P
C = 256
KC = C // P
HEADS = 16
HD = C // HEADS
HG = 4
GROUPS = HEADS // HG
PAIRS = HEADS // 2
UNITS = 10
HID = 1024
KH = HID // P
EPS = 1e-5
MASKED = -1e30
MODS = 6 * C
M_ROW = 63

MISC_USES = (4, 6, 6, 4)
MISC_BEFORE = (0, 2, 5, 8)
MISC_PER_BATCH = 10


def wait(eng, sem, count):
    if isinstance(count, int) and count <= 0:
        return
    eng.wait_ge(sem, count)


def wait_apart(eng, sem, count, passed):
    wait(eng, sem, count)
    eng.sem_inc(passed, 1)


def misc_uses_before(b, slot, order):
    return (b + 1) * MISC_PER_BATCH + MISC_BEFORE[slot] + order // 2


def head_of(group, half, side):
    return HG * group + 2 * half + side


def setup_phase(nc, io, keep, ctx):
    def sb(name, shape, dt=F32):
        return ctx.enter_context(nc.sbuf_tensor(name, shape, dt))

    def sem(name):
        return ctx.enter_context(nc.semaphore(name))

    NB = io["x"].shape[0]
    w_mod = sb("w_mod", [P, KC, MODS])
    c_t = sb("c_t", [P, KC, NB])
    e_t = sb("e_t", [P, KC, NB])
    d_t = sb("d_t", [P, KC, NB])
    silu = sb("silu", [P, KC, NB])
    rows = sb("rows", [NB, MODS])
    sign = sb("sign", [NB, C])
    neg = sb("neg", [NB, C])
    mag = sb("mag", [NB, C])
    col_ps = ctx.enter_context(nc.psum_tensor("col_ps", [P, 12, NB], F32))
    row_ps = [ctx.enter_context(nc.psum_tensor(f"row_ps{i}", [NB, 512], F32)) for i in range(3)]
    loaded, exp_done, silu_done, mod_done, rows_done, rows_out, chain = (
        sem(n) for n in ("s_loaded", "s_exp", "s_silu", "s_mod", "s_rows", "s_rows_out", "s_chain"))
    mod_cols = keep["mod_cols"]
    with nc.Block() as block:
        @block.sync
        def _(sp):
            sp.dma_start(c_t[:, :, :], io["c_t"].rearrange("(k p) b -> p k b", p=P)).then_inc(loaded, 16)
            sp.dma_start(w_mod[:, :, :], io["w_mod"].rearrange("(k p) n -> p k n", p=P)).then_inc(loaded, 16)
            sp.wait_ge(rows_done, 1)
            sp.dma_start(io["mod_rows"], rows[:, :]).then_inc(rows_out, 16)
            sp.wait_ge(rows_out, 16)

        @block.scalar
        def _(act):
            act.wait_ge(loaded, 32)
            act.activation(e_t[:, :, :], c_t[:, :, :], ACT.Exp, scale=-1.0).then_inc(exp_done, 1)

        @block.vector
        def _(dve):
            n = 0

            def link(ins):
                nonlocal n
                n += 1
                ins.then_inc(chain, 1)
                dve.wait_ge(chain, n)

            dve.wait_ge(exp_done, 1)
            link(dve.tensor_scalar_add(d_t[:, :, :], e_t[:, :, :], 1.0))
            link(dve.reciprocal(e_t[:, :, :], d_t[:, :, :]))
            dve.tensor_tensor(silu[:, :, :], c_t[:, :, :], e_t[:, :, :], ALU.mult).then_inc(silu_done, 1)
            dve.wait_ge(mod_done, 1)
            dve.tensor_copy(mod_cols[:, 0:2, :], col_ps[:, 0:2, :])
            dve.tensor_scalar_add(mod_cols[:, 2:4, :], col_ps[:, 2:4, :], 1.0)
            for i in range(3):
                ins = dve.tensor_copy(rows[:, 512 * i:512 * i + 512], row_ps[i][:, :])
            link(ins)
            link(dve.tensor_scalar_add(rows[:, 4 * C:5 * C], rows[:, 4 * C:5 * C], 1.0))
            for gate in (2, 5):
                g = rows[:, gate * C:gate * C + C]
                link(dve.tensor_scalar(sign[:, :], g, 0.0, 2.0, ALU.is_ge, ALU.mult))
                link(dve.tensor_scalar(neg[:, :], g, -1.0, None, ALU.mult))
                link(dve.tensor_tensor(mag[:, :], g, neg[:, :], ALU.max))
                link(dve.tensor_scalar(neg[:, :], mag[:, :], 0.25, None, ALU.max))
                link(dve.tensor_scalar(mag[:, :], sign[:, :], 1.0, None, ALU.subtract))
                link(dve.tensor_tensor(g, mag[:, :], neg[:, :], ALU.mult))
            dve.tensor_copy(sign[:, :], neg[:, :]).then_inc(rows_done, 1)

        @block.tensor
        def _(pe):
            pe.wait_ge(loaded, 32)
            pe.wait_ge(silu_done, 1)
            for j in range(4):
                for k in range(KC):
                    pe.matmul(col_ps[:, j, :], w_mod[:, k, j * P:j * P + P], silu[:, k, :],
                              start=(k == 0), stop=(k == KC - 1))
            for i in range(3):
                for k in range(KC):
                    ins = pe.matmul(row_ps[i][:, :], silu[:, k, :], w_mod[:, k, 512 * i:512 * i + 512],
                                    start=(k == 0), stop=(k == KC - 1))
            ins.then_inc(mod_done, 1)


def attention_phase(nc, io, keep, ctx):
    def sb(name, shape, dt=F32):
        return ctx.enter_context(nc.sbuf_tensor(name, shape, dt))

    def pb(name):
        return ctx.enter_context(nc.psum_tensor(name, [P, 512], F32))

    def sem(name):
        return ctx.enter_context(nc.semaphore(name))

    NB = io["x"].shape[0]
    mod_cols, ident = keep["mod_cols"], keep["ident"]
    w_qkv_hi = sb("w_qkv_hi", [P, KC, 3 * C], F32R)
    w_qkv_lo = sb("w_qkv_lo", [P, KC, 3 * C], F32R)
    w_out = sb("w_out", [P, KC, C])
    w_gated = sb("w_gated", [P, C])
    w_gated_hi = sb("w_gated_hi", [P, KC, C], F32R)
    w_gated_lo = sb("w_gated_lo", [P, KC, C], F32R)
    gate = [sb(f"gate{i}", [P, C]) for i in range(2)]
    masks = sb("masks", [P, 2, P], BF16)
    mask, mask_t = masks[:, 0, :], masks[:, 1, :]
    ident_b = sb("ident_b", [P, P], BF16)
    half_pow = sb("half_pow", [P, NT])
    x = [sb(f"x{i}", [P, NT, C]) for i in range(2)]
    stats = sb("stats", [P, NT, 6])
    mean_var = sb("mean_var", [P, NT, 2])
    var_eps = sb("var_eps", [P, NT])
    rstd = sb("rstd", [P, NT])
    h_hi = [sb(f"h_hi{k}", [P, T], F32R) for k in range(KC)]
    h_lo = [sb(f"h_lo{k}", [P, T], F32R) for k in range(KC)]
    dense = {n: sb(f"dense_{n}", [P, 2, T], F32R) for n in ("q_hi", "q_lo", "k_hi", "k_lo")}
    q_st = [sb(f"q_st{i}", [P, PAIRS, T], F32R) for i in range(2)]
    k_st = [sb(f"k_st{i}", [P, PAIRS, T], F32R) for i in range(2)]
    v_ones = [sb(f"v_ones{i}", [P, NT, HEADS, 32]) for i in range(2)]
    probs = [sb(f"probs{i}", [P, UNITS, 512]) for i in range(2)]
    row_max = [sb(f"row_max{i}", [P, 2, 2, NT]) for i in range(2)]
    neg_max = [sb(f"neg_max{i}", [16, P], F32R) for i in range(2)]
    o_sum = [sb(f"o_sum{i}", [P, T]) for i in range(2)]
    recip = sb("recip", [P, 16])
    attn = [sb(f"attn{i}", [P, NT, C]) for i in range(2)]
    attn_hi = [sb(f"attn_hi{k}", [P, T], F32R) for k in range(KC)]
    attn_lo = [sb(f"attn_lo{k}", [P, T], F32R) for k in range(KC)]
    res = [sb(f"res{i}", [P, NT, C]) for i in range(2)]

    mx_bank = [pb(f"mx_bank{i}") for i in range(2)]
    ex_bank = [pb(f"ex_bank{i}") for i in range(2)]
    pv_bank = [pb(f"pv_bank{i}") for i in range(2)]
    misc = [pb(f"misc{i}") for i in range(2)]

    const_in, const_ok, dve_const = sem("const_in"), sem("const_ok"), sem("dve_const")
    x_in = [sem(f"x_in{i}") for i in range(2)]
    res_in = [sem(f"res_in{i}") for i in range(2)]
    gate_in = [sem(f"gate_in{i}") for i in range(2)]
    x1_out = [sem(f"x1_out{i}") for i in range(2)]
    stacked = [sem(f"stacked{i}") for i in range(2)]
    max_in = [sem(f"max_in{i}") for i in range(2)]
    stats_ok, aggr_ok, var_ok, rstd_ok, xhat_ok = (sem(n) for n in ("stats_ok", "aggr_ok", "var_ok", "rstd_ok", "xhat_ok"))
    xt_ps, qk_ps, v_ps, mx_ps, ex_ps, pv_ps, ot_ps, mt_ps, at_ps, wo_ps = (
        sem(n) for n in ("xt_ps", "qk_ps", "v_ps", "mx_ps", "ex_ps", "pv_ps", "ot_ps", "mt_ps", "at_ps", "wo_ps"))
    hi_ok, exp_ok, osum_ok = sem("hi_ok"), sem("exp_ok"), sem("osum_ok")
    max_ok, recip_ok = sem("max_ok"), sem("recip_ok")
    hhi_ok, hlo_ok, athi_ok = sem("hhi_ok"), sem("hlo_ok"), sem("athi_ok")
    product_ok, ghi_ok, gated_ok = sem("product_ok"), sem("ghi_ok"), sem("gated_ok")
    passed = [sem(f"passed_{e}") for e in ("pool", "dve")]
    misc_ok = [sem(f"misc_ok{i}") for i in range(2)]

    x_d = io["x"].rearrange("b (t p) c -> b p t c", p=P)
    x1_d = io["x1"].rearrange("b (t p) c -> b p t c", p=P)
    mod_rows = io["mod_rows"]
    FIRST, LAST = 4, NB - 2

    def there(n):
        return not isinstance(n, int) or 0 <= n < NB

    def iterations(eng, body, start):
        for b in range(start, FIRST):
            body(b, b // 2, b % 2)
        with eng.Fori(0, (LAST - FIRST) // 2) as i:
            for par in range(2):
                body(i * 2 + (FIRST + par), i + FIRST // 2, par)
        for b in range(LAST, NB + 2):
            body(b, b // 2, b % 2)

    mask_in = attn[0][:, 0, :].rearrange("p (a j) -> p a j", a=2)

    def h_t(q, k):
        return x[q][:, :, P * k:P * k + P]

    def tiles_of(a):
        return a[:, :].rearrange("p (t j) -> p t j", j=P)

    def w_qkv_in(k):
        return probs[k][:, PAIRS:UNITS, :].rearrange("p u n -> p (u n)")[:, 0:3 * C]

    EXACT = ((-1, 2), (-1, 3), (0, 0), (0, 1))
    VALUE = ((-1, 1), (-1, 2), (-1, 3), (0, 0))
    MAXT = ((-1, 3), (0, 0), (0, 1), (0, 2))

    with nc.Block() as block:
        @block.sync
        def _(sp):
            for k in range(KC):
                sp.dma_start(w_qkv_in(k), io["w_qkv"][P * k:P * k + P, :]).then_inc(const_in, 16)
            sp.dma_start(w_out[:, :, :], io["w_out"].rearrange("(k p) n -> p k n", p=P)).then_inc(const_in, 16)
            sp.dma_start(mask_in, io["mask"]).then_inc(const_in, 16)
            for i, n in enumerate(("q_rows", "k_rows")):
                sp.dma_start(probs[i][:, 0:PAIRS, :], io[n]).then_inc(const_in, 16)

            def body(b, hb, par):
                if there(b + 2):
                    wait(sp, hlo_ok, KC * (b + 1))
                    sp.dma_start(x[par][:, :, :], x_d[b + 2]).then_inc(x_in[par], 16)
                n = b - 1
                if there(n):
                    q, half = (par + 1) % 2, hb + (par - 1) // 2
                    wait(sp, x1_out[q], 16 * half)
                    sp.dma_start(res[q][:, :, :], x_d[n]).then_inc(res_in[q], 16)
                    wait(sp, gated_ok, KC * (n - 1))
                    sp.dma_start(gate[q][:, :], mod_rows[n, 2 * C:3 * C].partition_broadcast(P)).then_inc(gate_in[q], 16)
                n = b + 1
                if there(n):
                    q = (par + 1) % 2
                    wait(sp, ex_ps, GROUPS * UNITS * (n - 1))
                    if isinstance(n, int) and n < 2:
                        sp.wait_ge(const_ok, 1)
                    for tile in range(2):
                        for bank in range(2):
                            sp.wait_ge(misc_ok[bank], misc_uses_before(b, 1 + tile, 2 + bank) + 1)
                        for p in range(4):
                            for st, hi, lo, lo_row in ((q_st, "q_hi", "q_lo", 1), (k_st, "k_hi", "k_lo", 2)):
                                for row in range(3):
                                    src = dense[lo if row == lo_row else hi]
                                    sp.dma_start(st[q][row:P:4, 4 * tile + p, :].bitcast(F32),
                                                 src[32 * p:32 * p + 32, tile, :].bitcast(F32)).then_inc(stacked[tile], 16)
                n = b - 2
                if there(n):
                    for bank in range(2):
                        sp.wait_ge(misc_ok[bank], misc_uses_before(b, 2, 4 + bank) + 1)
                    sp.dma_start(x1_d[n], res[par][:, :, :]).then_inc(x1_out[par], 16)

            iterations(sp, body, -2)
            for i in range(2):
                sp.wait_ge(x1_out[i], 16 * (NB // 2))

        @block.gpsimd
        def _(pool):
            pool.memset(half_pow[:, :], -0.5)
            for i in range(2):
                pool.memset(v_ones[i][:, :, :, :], 1.0)

            def body(b, hb, par):
                n = b - 2
                if there(n):
                    wait(pool, gate_in[par], 16 * hb)
                    wait(pool, wo_ps, 2 * n)
                    if isinstance(n, int) and n == 0:
                        pool.wait_ge(const_in, 16 * 6)
                    for k in range(KC):
                        wait(pool, gated_ok, KC * n + k)
                        pool.tensor_tensor(w_gated[:, :], w_out[:, k, :], gate[par][:, :], ALU.mult).then_inc(product_ok, 1)
                        pool.tensor_tensor(w_gated_hi[:, k, :], w_out[:, k, :], gate[par][:, :], ALU.mult).then_inc(ghi_ok, 1)
                        pool.wait_ge(product_ok, KC * n + k + 1)
                        pool.wait_ge(ghi_ok, KC * n + k + 1)
                        pool.tensor_tensor(w_gated_lo[:, k, :], w_gated[:, :], w_gated_hi[:, k, :].bitcast(F32),
                                           ALU.subtract).then_inc(gated_ok, 1)
                for s in range(4):
                    m, mg = MAXT[s]
                    if there(b + m):
                        pool.wait_ge(misc_ok[0], misc_uses_before(b, s, 0) + 1)
                        wait_apart(pool, ex_ps, GROUPS * UNITS * (b + m - 1), passed[0])
                        for half in range(2):
                            pool.dma_start(q_st[(par + m) % 2][M_ROW:P:64, 2 * mg + half, :].bitcast(F32),
                                           neg_max[mg % 2][8 * half:8 * half + 8, :].bitcast(F32)).then_inc(max_in[mg % 2], 16)
                    if s == 0 and there(b + 1):
                        for k in range(KC):
                            pool.wait_ge(hhi_ok, KC * (b + 1) + k + 1)
                            wait(pool, v_ps, 2 * (b + 1))
                            pool.tensor_tensor(tiles_of(h_lo[k]), h_t((par + 1) % 2, k), tiles_of(h_hi[k]).bitcast(F32),
                                               ALU.subtract).then_inc(hlo_ok, 1)
                    if s == 3 and there(b + 2):
                        pool.wait_ge(aggr_ok, b + 3)
                        wait_apart(pool, xhat_ok, b + 2, passed[0])
                        pool.tensor_scalar(var_eps[:, :], mean_var[:, :, 1], EPS, None, ALU.add).then_inc(var_ok, 1)
                        pool.wait_ge(var_ok, b + 3)
                        pool.tensor_tensor(rstd[:, :], var_eps[:, :], half_pow[:, :], ALU.pow).then_inc(rstd_ok, 1)

            iterations(pool, body, -2)

        @block.scalar
        def _(act):
            def body(b, hb, par):
                prep = there(b + 1)
                for s in range(4):
                    e, g = EXACT[s]
                    n = b + e
                    v, vg = VALUE[s]
                    for u in range(UNITS):
                        if there(n):
                            act.wait_ge(ex_ps, GROUPS * UNITS * n + UNITS * g + u + 1)
                            if u == 0:
                                wait(act, pv_ps, GROUPS * n + g - 1)
                            act.activation(probs[g % 2][:, u, :], ex_bank[u % 2][:, :], ACT.Exp).then_inc(exp_ok, 1)
                        if s == 0 and u in (6, 8) and prep:
                            k = (u - 6) // 2
                            act.wait_ge(xt_ps, KC * (b + 1) + k + 1)
                            act.activation(h_t((par + 1) % 2, k), tiles_of(misc[k]), ACT.Identity,
                                           bias=mod_cols[:, k, bass.ds(b + 1, 1)],
                                           scale=mod_cols[:, 2 + k, bass.ds(b + 1, 1)]).then_inc(misc_ok[k], 1)
                        if s in (1, 2) and u in (4, 6) and prep:
                            which = "q_hi" if u == 4 else "k_hi"
                            use = 4 * (b + 1) + 2 * (s - 1) + (u - 4) // 2
                            act.wait_ge(qk_ps, use + 1)
                            if u == 4:
                                wait(act, stacked[s - 1], 24 * 16 * (b + 1))
                            act.activation(dense[which][:, s - 1, :], misc[(u - 4) // 2][:, :], ACT.Copy).then_inc(hi_ok, 1)
                        if s == 1 and u >= 8 and there(b - 2):
                            k = u - 8
                            act.wait_ge(at_ps, 2 * (b - 2) + k + 1)
                            wait(act, wo_ps, 2 * (b - 2))
                            act.activation(attn_hi[k][:, :], misc[k][:, :], ACT.Copy).then_inc(athi_ok, 1)
                        if s == 3 and u in (5, 7) and prep:
                            j = (u - 5) // 2
                            act.wait_ge(v_ps, 2 * (b + 1) + j + 1)
                            wait(act, pv_ps, GROUPS * b)
                            if isinstance(b, int) and b < 1:
                                act.wait_ge(const_ok, 1)
                            for t in range(2):
                                ins = act.activation(v_ones[(par + 1) % 2][:, 2 * j + t, :, 0:HD],
                                                     misc[j][:, C * t:C * t + C].rearrange("p (h d) -> p h d", d=HD),
                                                     ACT.Copy)
                            ins.then_inc(misc_ok[j], 1)
                        if u == 9 and there(b + v):
                            n_pv = GROUPS * (b + v) + vg
                            act.wait_ge(pv_ps, n_pv + 1)
                            wait(act, ot_ps, n_pv - 1)
                            act.activation(o_sum[vg % 2][:, :], pv_bank[vg % 2][:, :], ACT.Copy).then_inc(osum_ok, 1)

            iterations(act, body, -1)

        @block.vector
        def _(dve):
            dve.wait_ge(const_in, 16 * 6)
            for k in range(KC):
                dve.tensor_scalar(w_qkv_hi[:, k, 0:C], w_qkv_in(k)[:, 0:C], HD ** -0.5, None, ALU.mult)
                dve.tensor_copy(w_qkv_hi[:, k, C:3 * C], w_qkv_in(k)[:, C:3 * C]).then_inc(dve_const, 1)
                dve.wait_ge(dve_const, k + 1)
                dve.scalar_tensor_tensor(out=w_qkv_lo[:, k, 0:C], in0=w_qkv_in(k)[:, 0:C], scalar=HD ** -0.5,
                                         in1=w_qkv_hi[:, k, 0:C].bitcast(F32), op0=ALU.mult, op1=ALU.subtract)
                dve.tensor_tensor(w_qkv_lo[:, k, C:3 * C], w_qkv_in(k)[:, C:3 * C],
                                  w_qkv_hi[:, k, C:3 * C].bitcast(F32), ALU.subtract)
            dve.tensor_copy(masks[:, :, :], mask_in)
            dve.tensor_copy(ident_b[:, :], ident[:, :])
            for i in range(2):
                dve.tensor_copy(q_st[i][:, :, :], probs[0][:, 0:PAIRS, :])
                ins = dve.tensor_copy(k_st[i][:, :, :], probs[1][:, 0:PAIRS, :])
            ins.then_inc(dve_const, 1)
            dve.wait_ge(dve_const, KC + 1)
            dve.sem_inc(const_ok, 1)

            def normalise_x(n, q):
                dve.wait_ge(rstd_ok, n + 1)
                for t in range(NT):
                    ins = dve.tensor_scalar(x[q][:, t, :], x[q][:, t, :], mean_var[:, t, 0:1], rstd[:, t:t + 1],
                                            ALU.subtract, ALU.mult)
                ins.then_inc(xhat_ok, 1)

            def statistics(n, half, q):
                dve.wait_ge(x_in[q], 16 * (half + 1))
                wait(dve, xhat_ok, n)
                wait(dve, aggr_ok, n)
                for t in range(NT):
                    ins = dve.bn_stats(stats[:, t, :], x[q][:, t, :])
                ins.then_inc(stats_ok, 1)
                wait_apart(dve, stats_ok, n + 1, passed[1])
                for t in range(NT):
                    ins = dve.bn_aggr(mean_var[:, t, :], stats[:, t, :])
                ins.then_inc(aggr_ok, 1)

            def body(b, hb, par):
                prep = there(b + 1)
                for s in range(4):
                    m, mg = MAXT[s]
                    for u in range(UNITS):
                        if s == 0 and u == 1 and prep:
                            normalise_x(b + 1, (par + 1) % 2)
                        if there(b):
                            side, v = u % 2, u // 2
                            dve.wait_ge(mx_ps, GROUPS * UNITS * b + UNITS * s + u + 1)
                            if u == 0:
                                wait(dve, mt_ps, GROUPS * b + s - 1)
                            bank, out = mx_bank[u % 2], row_max[s % 2]
                            if v in (0, 2):
                                ins = dve.reduce_max(out[:, v // 2, side, 3:4], bank[:, :], AX.X)
                            elif v in (1, 3):
                                dve.reduce_max(out[:, v // 2, side, 0:1], bank[:, 0:P], AX.X)
                                ins = dve.reduce_max(out[:, v // 2, side, 2:3], bank[:, P:512], AX.X)
                            else:
                                ins = dve.reduce_max(out[:, :, side, 1], bank[:, :].rearrange("p (h j) -> p h j", h=2), AX.X)
                            ins.then_inc(max_ok, 1)
                        if u == 2 and there(b + m):
                            n_mt = GROUPS * (b + m) + mg
                            dve.wait_ge(mt_ps, n_mt + 1)
                            wait(dve, max_in[mg % 2], 32 * (2 * (b + m) + mg // 2))
                            dve.tensor_scalar(neg_max[mg % 2][:, :], misc[0][0:16, 0:P], -1.0, None,
                                              ALU.mult).then_inc(misc_ok[0], 1)
                        if u == (4 if s == 0 else 3) and there(b - 1):
                            n_ot = GROUPS * (b - 1) + s
                            dve.wait_ge(ot_ps, n_ot + 1)
                            wait(dve, misc_ok[1], misc_uses_before(b - 1, 3, 1) + 1 if s == 0 else misc_uses_before(b, s - 1, 1) + 1)
                            ot = misc[1][:, :].rearrange("p (a c) -> p a c", c=32)
                            dve.reciprocal(recip[:, :], ot[:, :, HD]).then_inc(recip_ok, 1)
                            dve.wait_ge(recip_ok, n_ot + 1)
                            wait(dve, at_ps, 2 * (b - 2))
                            dve.tensor_tensor(
                                attn[(par + 1) % 2][:, :, 64 * s:64 * s + 64].rearrange("p i (h d) -> p i h d", d=HD),
                                ot[:, :, 0:HD].rearrange("p (i h) d -> p i h d", h=HG),
                                recip[:, :].rearrange("p (i h) -> p i h", h=HG).unsqueeze(3).to_broadcast([P, NT, HG, HD]),
                                ALU.mult).then_inc(misc_ok[1], 1)
                        if s == 0 and u in (7, 9) and prep:
                            k = (u - 7) // 2
                            dve.wait_ge(misc_ok[k], misc_uses_before(b, 0, 2 + k) + 1)
                            wait(dve, v_ps, 2 * (b + 1))
                            dve.tensor_copy(tiles_of(h_hi[k]), h_t((par + 1) % 2, k)).then_inc(hhi_ok, 1)
                        if (s, u) in ((1, 9), (2, 0)) and there(b - 2):
                            k = s - 1
                            dve.wait_ge(athi_ok, KC * (b - 2) + k + 1)
                            dve.tensor_tensor(attn_lo[k][:, :], misc[k][:, :], attn_hi[k][:, :].bitcast(F32),
                                              ALU.subtract).then_inc(misc_ok[k], 1)
                        if s in (1, 2) and u in (5, 7) and prep:
                            hi, lo = ("q_hi", "q_lo") if u == 5 else ("k_hi", "k_lo")
                            use = 4 * (b + 1) + 2 * (s - 1) + (u - 5) // 2
                            dve.wait_ge(hi_ok, use + 1)
                            wait(dve, stacked[s - 1], 24 * 16 * (b + 1))
                            dve.tensor_tensor(dense[lo][:, s - 1, :], misc[(u - 5) // 2][:, :],
                                              dense[hi][:, s - 1, :].bitcast(F32), ALU.subtract).then_inc(misc_ok[(u - 5) // 2], 1)
                        if s == 3 and u < 2 and there(b - 2):
                            n, j = b - 2, u
                            dve.wait_ge(wo_ps, 2 * n + j + 1)
                            wait(dve, res_in[par], 16 * hb)
                            dve.tensor_tensor(res[par][:, 2 * j:2 * j + 2, :], res[par][:, 2 * j:2 * j + 2, :],
                                              misc[j][:, :].rearrange("p (t c) -> p t c", t=2), ALU.add).then_inc(misc_ok[j], 1)
                        if s == 3 and u == 4 and there(b + 2):
                            statistics(b + 2, hb + 1, par)

            iterations(dve, body, -2)

        @block.tensor
        def _(pe):
            pe.wait_ge(const_ok, 1)

            def misc_free(b, s, order):
                wait(pe, misc_ok[order % 2], misc_uses_before(b, s, order))
                return misc[order % 2]

            def misc_skip(b, s, order):
                wait(pe, misc_ok[order % 2], misc_uses_before(b, s, order))
                pe.sem_inc(misc_ok[order % 2], 1)

            def product(out, hi, lo, w_hi, w_lo, k):
                pe.matmul(out, lo, w_hi, start=(k == 0), stop=False)
                pe.matmul(out, hi, w_lo, start=False, stop=False)
                return pe.matmul(out, hi, w_hi, start=False, stop=(k == KC - 1))


            def steps(u):
                return 2 if u // 2 in (1, 3) else 1

            def max_scores(n, g, u, q, step):
                side, v, bank = u % 2, u // 2, mx_bank[u % 2]
                rows = slice(64 * side, 64 * side + M_ROW)
                if step == 0:
                    if u == 0 and g % 2 == 0:
                        pe.wait_ge(stacked[g // 2], 24 * 16 * (n + 1))
                    wait(pe, max_ok, GROUPS * UNITS * n + UNITS * g + u - 1)
                for half in range(2 if v == 4 else 1):
                    pair = 2 * g + (half if v == 4 else v // 2)
                    block_, keys, at = {0: (3, 512, 0), 1: ((0, 256, 0), (2, 384, P))[step], 2: (1, 256, 256 * half)}[
                        2 if v == 4 else v % 2]
                    pe.matmul(bank[:, at:at + keys], q_st[q][rows, pair, P * block_:P * block_ + P],
                              k_st[q][rows, pair, 0:keys], start=(half == 0), stop=False)

            def max_masks(u, step):
                v, bank = u // 2, mx_bank[u % 2]
                if v == 4:
                    ins = add_masks(bank, mask, P, 384)
                else:
                    ins = add_masks(bank, mask, 384 if v % 2 == 0 or step else 0)
                if step == steps(u) - 1:
                    ins.then_inc(mx_ps, 1)

            def exact_scores(n, g, u, q, step):
                side, v, bank = (u + 1) % 2, u // 2, ex_bank[u % 2]
                rows = slice(64 * side, 64 * side + 64)
                if step == 0:
                    if u == 0:
                        pe.wait_ge(max_in[g % 2], 32 * (2 * n + g // 2 + 1))
                    wait(pe, exp_ok, GROUPS * UNITS * n + UNITS * g + u - 1)
                for half in range(2 if v == 4 else 1):
                    pair = 2 * g + (half if v == 4 else v // 2)
                    keys, first, at = {0: (0, 0, 0), 1: ((3, 256, 256), (1, P, 0))[step], 2: (2, 256, 256 * half)}[
                        2 if v == 4 else v % 2]
                    pe.matmul(bank[:, at:at + T - first], k_st[q][rows, pair, P * keys:P * keys + P],
                              q_st[q][rows, pair, first:T], start=(half == 0), stop=False)

            def exact_masks(u, step):
                v, bank = u // 2, ex_bank[u % 2]
                if v == 4:
                    ins = add_masks(bank, mask_t, 0, 256)
                else:
                    ins = add_masks(bank, mask_t, 384 if v % 2 and step == 0 else 0)
                if step == steps(u) - 1:
                    ins.then_inc(ex_ps, 1)

            def add_masks(bank, mask_, first, last=None):
                if last is None:
                    return pe.matmul(bank[:, first:first + P], ident_b[:, :], mask_, start=False, stop=True)
                blocks = bank[:, :].rearrange("p (a j) -> p a j", j=P)[:, first // P:last // P + 1:(last - first) // P]
                return pe.matmul(blocks, ident_b[:, :], mask_.unsqueeze(1).to_broadcast([P, 2, P]), start=False, stop=True)

            def values(n, g, q, keys):
                if keys == 0:
                    pe.wait_ge(exp_ok, GROUPS * UNITS * n + UNITS * (g + 1))
                    wait(pe, osum_ok, GROUPS * n + g - 1)
                for hh in range(HG):
                    half, side = hh // 2, hh % 2
                    odd = 1 - side
                    if keys == 0:
                        moving = probs[g % 2][:, 4 * half + odd, :]
                    elif keys == 1:
                        moving = probs[g % 2][:, 4 * half + 2 + odd, 0:384]
                    elif keys == 3:
                        moving = probs[g % 2][:, 4 * half + 2 + odd, 384:512]
                    else:
                        moving = probs[g % 2][:, 8 + odd, 256 * half:256 * half + 256]
                    ins = pe.matmul(pv_bank[g % 2][32 * hh:32 * hh + 32, P * keys:T],
                                    v_ones[q][:, keys, HG * g + hh, :], moving, start=(keys == 0), stop=(keys == NT - 1))
                if keys == NT - 1:
                    ins.then_inc(pv_ps, 1)

            def body(b, hb, par):
                prep = there(b + 1)
                for s in range(4):
                    e, eg = EXACT[s]
                    v, vg = VALUE[s]
                    m, mg = MAXT[s]
                    for u in range(UNITS):
                        for step in range(steps(u)):
                            if there(b):
                                max_scores(b, s, u, par, step)
                            if there(b + e):
                                exact_scores(b + e, eg, u, (par + e) % 2, step)
                            if there(b):
                                max_masks(u, step)
                            if there(b + e):
                                exact_masks(u, step)
                        if u in (1, 3, 5, 7) and there(b + v):
                            values(b + v, vg, (par + v) % 2, (u - 1) // 2)
                        if u == 1:
                            if there(b + m):
                                bank = misc_free(b, s, 0)
                                pe.wait_ge(max_ok, (GROUPS * (b + m) + mg + 1) * UNITS)
                                pe.matmul(bank[0:16, 0:P], row_max[mg % 2][:, :, :, :].rearrange("p a b c -> p (a b c)"),
                                          ident[:, :], start=True, stop=True).then_inc(mt_ps, 1)
                            else:
                                misc_skip(b, s, 0)
                        if u == (3 if s == 0 else 2):
                            if there(b - 1):
                                bank = misc_free(b, s, 1)
                                pe.wait_ge(osum_ok, GROUPS * (b - 1) + s + 1)
                                for i in range(NT):
                                    ins = pe.transpose(bank[:, P * i:P * i + P], o_sum[s % 2][:, P * i:P * i + P], ident[:, :])
                                ins.then_inc(ot_ps, 1)
                            else:
                                misc_skip(b, s, 1)
                        if s == 0 and u in (5, 7):
                            k = (u - 5) // 2
                            if prep:
                                bank = misc_free(b, s, 2 + k)
                                pe.wait_ge(xhat_ok, b + 2)
                                for t in range(NT):
                                    ins = pe.transpose(bank[:, P * t:P * t + P], x[(par + 1) % 2][:, t, P * k:P * k + P], ident[:, :])
                                ins.then_inc(xt_ps, 1)
                            else:
                                misc_skip(b, s, 2 + k)
                        if s in (1, 2) and u in (3, 5):
                            j = (u - 3) // 2
                            if prep:
                                bank = misc_free(b, s, 2 + j)
                                pe.wait_ge(hlo_ok, KC * (b + 2))
                                col = C * j + P * (s - 1)
                                for k in range(KC):
                                    pe.matmul(bank[:, :], w_qkv_lo[:, k, col:col + P], h_hi[k][:, :], start=(k == 0), stop=False)
                                    pe.matmul(bank[:, :], w_qkv_hi[:, k, col:col + P], h_lo[k][:, :], start=False, stop=False)
                                    ins = pe.matmul(bank[:, :], w_qkv_hi[:, k, col:col + P], h_hi[k][:, :],
                                                    start=False, stop=(k == KC - 1))
                                ins.then_inc(qk_ps, 1)
                            else:
                                misc_skip(b, s, 2 + j)
                        if s == 1 and u in (7, 8):
                            k = u - 7
                            if there(b - 2):
                                bank = misc_free(b, s, 4 + k)
                                pe.wait_ge(misc_ok[1], misc_uses_before(b - 1, 3, 1) + 1)
                                for t in range(NT):
                                    ins = pe.transpose(bank[:, P * t:P * t + P], attn[par][:, t, P * k:P * k + P], ident[:, :])
                                ins.then_inc(at_ps, 1)
                            else:
                                misc_skip(b, s, 4 + k)
                        if s == 2 and u in (7, 8):
                            j = u - 7
                            if there(b - 2):
                                bank = misc_free(b, s, 4 + j)
                                for i in range(KC):
                                    pe.wait_ge(misc_ok[i], misc_uses_before(b, 1, 4 + i) + 1)
                                pe.wait_ge(gated_ok, KC * (b - 1))
                                for t in range(2):
                                    for k in range(KC):
                                        tok = P * (2 * j + t)
                                        ins = product(bank[:, C * t:C * t + C], attn_hi[k][:, tok:tok + P], attn_lo[k][:, tok:tok + P],
                                                      w_gated_hi[:, k, :], w_gated_lo[:, k, :], k)
                                ins.then_inc(wo_ps, 1)
                            else:
                                misc_skip(b, s, 4 + j)
                        if s == 3 and u in (4, 6):
                            j = (u - 4) // 2
                            if prep:
                                bank = misc_free(b, s, 2 + j)
                                for t in range(2):
                                    for k in range(KC):
                                        tok = P * (2 * j + t)
                                        ins = product(bank[:, C * t:C * t + C], h_hi[k][:, tok:tok + P], h_lo[k][:, tok:tok + P],
                                                      w_qkv_hi[:, k, 2 * C:3 * C], w_qkv_lo[:, k, 2 * C:3 * C], k)
                                ins.then_inc(v_ps, 1)
                            else:
                                misc_skip(b, s, 2 + j)

            iterations(pe, body, -1)


def ternary_phase(nc, io, keep, ctx):
    def sb(name, shape, dt=F32):
        return ctx.enter_context(nc.sbuf_tensor(name, shape, dt))

    def sem(name):
        return ctx.enter_context(nc.semaphore(name))

    ident = keep["ident"]
    raw = [sb("raw1", [P, KC * HID]), sb("raw2", [P, KH * C])]
    over = sb("over", [P, HID * KC])
    under = sb("under", [P, HID * KC])
    tern2_f = sb("tern2_f", [P, KH * C])
    absw = sb("absw", [P, HID * KC])
    part = sb("part", [P, 2])
    mean = sb("mean", [P, 2])
    clipped = sb("clipped", [P, 2])
    scale = sb("scale", [P, 2])
    ones = sb("ones", [P, P])
    b1_two = sb("b1_two", [2, HID])
    b1_s = sb("b1_s", [2, HID])
    b1_hi = sb("b1_hi", [2, HID], F32R)
    minus_row1 = sb("minus_row1", [2, 1])
    g2 = sb("g2", [P, HID])
    ln2_b = sb("ln2_b", [P, KH])
    b2_all = sb("b2_all", [P, C])
    shift_l = sb("shift_l", [P, KH, P])
    tmp_c = sb("tmp_c", [P, C])
    sum_ps = ctx.enter_context(nc.psum_tensor("sum_ps", [P, 2], F32))
    const_ps = ctx.enter_context(nc.psum_tensor("const_ps", [P, C], F32))
    loaded, abs_ok, ones_ok, sum_ok, chain, tern_ok, const_ok = (
        sem(n) for n in ("t_loaded", "t_abs", "t_ones", "t_sum", "t_chain", "t_tern", "t_const"))
    count = 1.0 / (HID * C)
    n_loads = 8
    with nc.Block() as block:
        @block.sync
        def _(sp):
            sp.dma_start(raw[0][:, :].rearrange("p (k n) -> p k n", k=KC), io["w1"].rearrange("(k p) n -> p k n", p=P)).then_inc(loaded, 16)
            sp.dma_start(raw[1][:, :].rearrange("p (k n) -> p k n", k=KH), io["w2"].rearrange("(k p) n -> p k n", p=P)).then_inc(loaded, 16)
            sp.dma_start(b1_two[:, :], io["b1"].partition_broadcast(2)).then_inc(loaded, 16)
            sp.dma_start(g2[:, :], io["ln2_g"].partition_broadcast(P)).then_inc(loaded, 16)
            sp.dma_start(b2_all[:, :], io["b2"].partition_broadcast(P)).then_inc(loaded, 16)
            sp.dma_start(ln2_b[:, :], io["ln2_b"]).then_inc(loaded, 16)
            sp.dma_start(keep["ln1_g"][:, :], io["ln1_g"]).then_inc(loaded, 16)
            sp.dma_start(keep["ln1_b"][:, :], io["ln1_b"]).then_inc(loaded, 16)
            sp.wait_ge(loaded, 16 * n_loads)

        @block.scalar
        def _(act):
            act.wait_ge(loaded, 16 * n_loads)
            act.activation(absw[:, :], raw[0][:, :], ACT.Abs, accum_out=part[:, 0:1]).then_inc(abs_ok, 1)
            act.wait_ge(abs_ok, 1)
            act.activation(absw[:, :], raw[1][:, :], ACT.Abs, accum_out=part[:, 1:2]).then_inc(abs_ok, 1)

        @block.tensor
        def _(pe):
            pe.wait_ge(ones_ok, 1)
            pe.wait_ge(abs_ok, 2)
            pe.matmul(sum_ps[:, :], ones[:, :], part[:, :], start=True, stop=True).then_inc(sum_ok, 1)
            pe.wait_ge(tern_ok, 1)
            for k in range(KH):
                ins = pe.matmul(const_ps[:, :], shift_l[:, k, :], tern2_f[:, C * k:C * k + C], start=(k == 0), stop=(k == KH - 1))
            ins.then_inc(const_ok, 1)

        @block.vector
        def _(dve):
            n = 0

            def link(ins):
                nonlocal n
                n += 1
                ins.then_inc(chain, 1)
                dve.wait_ge(chain, n)

            dve.memset(ones[:, :], 1.0).then_inc(ones_ok, 1)
            dve.wait_ge(ones_ok, 1)
            dve.tensor_copy(keep["ones2"][:, :], ones[0:2, :])
            dve.wait_ge(loaded, 16 * n_loads)
            dve.wait_ge(sum_ok, 1)
            link(dve.tensor_scalar(mean[:, :], sum_ps[:, :], count, None, ALU.mult))
            link(dve.tensor_scalar(clipped[:, :], mean[:, :], 1e-5, None, ALU.max))
            link(dve.reciprocal(scale[:, :], clipped[:, :]))
            link(dve.reciprocal(keep["inv_scale"][:, :], scale[:, :]))
            for i in range(2):
                link(dve.tensor_scalar(over[:, :], raw[i][:, :], scale[:, i:i + 1], 0.5, ALU.mult, ALU.is_gt))
                link(dve.tensor_scalar(under[:, :], raw[i][:, :], scale[:, i:i + 1], -0.5, ALU.mult, ALU.is_lt))
                link(dve.tensor_tensor(keep["tern1"][:, :] if i == 0 else tern2_f[:, :], over[:, :], under[:, :], ALU.subtract))
            link(dve.tensor_copy(keep["tern2"][:, :], tern2_f[:, :]))
            link(dve.tensor_scalar(b1_s[:, :], b1_two[:, :], scale[0:2, 0:1], None, ALU.mult))
            link(dve.tensor_copy(b1_hi[:, :], b1_s[:, :]))
            link(dve.tensor_scalar(minus_row1[:, :], ident[0:2, 1:2], -1.0, None, ALU.mult))
            link(dve.scalar_tensor_tensor(out=keep["bias1"][:, :], in0=b1_hi[:, :].bitcast(F32), scalar=minus_row1[:, 0:1],
                                          in1=b1_s[:, :], op0=ALU.mult, op1=ALU.add))
            link(dve.tensor_scalar(keep["gain2"][:, :], g2[:, :], keep["inv_scale"][:, 1:2], None, ALU.mult))
            link(dve.tensor_copy(shift_l[:, :, :], ln2_b[:, :].unsqueeze(2).to_broadcast([P, KH, P])))
            dve.tensor_copy(over[:, 0:P], shift_l[:, 0, :]).then_inc(tern_ok, 1)
            dve.wait_ge(const_ok, 1)
            link(dve.tensor_scalar(tmp_c[:, :], const_ps[:, :], keep["inv_scale"][:, 1:2], None, ALU.mult))
            link(dve.tensor_tensor(keep["const_row"][:, :], tmp_c[:, :], b2_all[:, :], ALU.add))


def ffn_phase(nc, io, keep, ctx):
    def sb(name, shape, dt=F32):
        return ctx.enter_context(nc.sbuf_tensor(name, shape, dt))

    def pb(name, n):
        return ctx.enter_context(nc.psum_tensor(name, [P, n], F32))

    def sem(name):
        return ctx.enter_context(nc.semaphore(name))

    NB = io["x"].shape[0]
    ident = keep["ident"]
    half_pow = sb("f_half_pow", [P, NT])
    x1 = [sb(f"f_x1{i}", [P, NT, C]) for i in range(2)]
    base = [sb(f"f_base{i}", [P, NT, C]) for i in range(2)]
    shift_scale = [sb(f"f_ss{i}", [P, 2, C]) for i in range(2)]
    gate = [sb(f"f_gate{i}", [P, C]) for i in range(2)]
    gated_const = sb("f_gc", [P, C])
    xh = sb("f_xh", [P, NT, C])
    h0 = sb("f_h0", [P, NT, C])
    h1 = sb("f_h1", [P, NT, C])
    hf = [sb(f"f_hf{i}", [P, KC, 2 * P]) for i in range(2)]
    h_hi = [sb(f"f_hhi{i}", [P, KC, T], F32R) for i in range(2)]
    h_lo = [sb(f"f_hlo{i}", [P, KC, T], F32R) for i in range(2)]
    stats = sb("f_stats", [P, NT, 6])
    mv = [sb(f"f_mv{i}", [P, NT, 2]) for i in range(2)]
    ve = [sb(f"f_ve{i}", [P, NT]) for i in range(2)]
    rs = [sb(f"f_rs{i}", [P, NT]) for i in range(2)]
    usum = [sb(f"f_usum{i}", [P, 1]) for i in range(2)]
    minus_mean = [sb(f"f_mm{i}", [P, 1]) for i in range(2)]
    usq = [sb(f"f_usq{i}", [P, 1]) for i in range(2)]
    squares = sb("f_squares", [P, HID])
    uve = [sb(f"f_uve{i}", [P, 1]) for i in range(2)]
    urs = [sb(f"f_urs{i}", [P, 1]) for i in range(NT)]
    u_act = [sb(f"f_u{i}", [P, HID]) for i in range(2)]
    u_c = [sb(f"f_uc{i}", [P, HID]) for i in range(2)]
    u_hi = [sb(f"f_uhi{i}", [P, HID], F32R) for i in range(2)]
    u_lo = [sb(f"f_ulo{i}", [P, HID], F32R) for i in range(2)]
    y = [sb(f"f_y{i}", [P, C]) for i in range(2)]
    up_ps = [pb(f"up_ps{i}", 2 * 512) for i in range(2)]
    ut_ps = pb("ut_ps", 2 * 512)
    down_ps = pb("down_ps", 2 * C)
    xt_ps = pb("xt_ps_f", 512)

    passed = [sem(f"f_passed_{e}") for e in ("pool", "dve")]
    x1_in = [sem(f"f_x1_in{i}") for i in range(2)]
    ss_in = [sem(f"f_ss_in{i}") for i in range(2)]
    gate_in = [sem(f"f_gate_in{i}") for i in range(2)]
    out_left = [sem(f"f_out{i}") for i in range(2)]
    st_ok = [sem(f"f_st{i}") for i in range(2)]
    ag_ok = [sem(f"f_ag{i}") for i in range(2)]
    ve_ok = [sem(f"f_ve_ok{i}") for i in range(2)]
    rs_ok = [sem(f"f_rs_ok{i}") for i in range(2)]
    xh_ok, scaled_ok, h0_ok, h1_ok, gc_ok, base_ok = (sem("f_" + n) for n in ("xh", "scaled", "h0", "h1", "gc", "base"))
    xt_ok, hf_ok, hhi_ok, hlo_ok = (sem("f_" + n) for n in ("xt", "hf_ok", "hhi_ok", "hlo_ok"))
    up_ok, gelu_ok, mean_ok, usq_ok, uve_ok, urs_ok, uc_ok, ut_ok, uhi_ok, ulo_ok, down_ok, y_ok, out_ok, pow_ok = (
        sem("f_" + n) for n in ("up", "gelu", "mean", "usq", "uve_ok", "urs_ok", "uc", "ut", "uhi_ok", "ulo_ok", "down", "y_ok", "out_ok", "pow"))

    x1_d = io["x1"].rearrange("b (t p) c -> b p t c", p=P)
    out_d = io["out"].rearrange("b (t p) c -> b p t c", p=P)
    mod_rows = io["mod_rows"]
    FIRST, LAST = 4, NB - 2

    def there(n):
        return not isinstance(n, int) or 0 <= n < NB

    def iterations(eng, body):
        for b in range(-2, FIRST):
            body(b, b // 2, b % 2)
        with eng.Fori(0, (LAST - FIRST) // 2) as i:
            for par in range(2):
                body(i * 2 + (FIRST + par), i + FIRST // 2, par)
        for b in range(LAST, NB + 1):
            body(b, b // 2, b % 2)

    def previous(b, t):
        return (b, t - 1) if t else (b - 1, NT - 1)

    def back(b, t, steps):
        for _ in range(steps):
            b, t = previous(b, t)
        return b, t

    def tile_of(b, t):
        return NT * b + t

    with nc.Block() as block:
        @block.sync
        def _(sp):
            def body(b, hb, par):
                odd = 1 - par
                if there(b + 2):
                    wait(sp, base_ok, b + 1)
                    sp.dma_start(x1[par][:, :, :], x1_d[b + 2]).then_inc(x1_in[par], 16)
                    wait(sp, h0_ok, b + 1)
                    sp.dma_start(shift_scale[par][:, :, :],
                                 mod_rows[b + 2, 3 * C:5 * C].rearrange("(a c) -> a c", a=2).partition_broadcast(P)).then_inc(ss_in[par], 16)
                if there(b + 1):
                    wait(sp, y_ok, NT * b)
                    sp.dma_start(gate[odd][:, :], mod_rows[b + 1, 5 * C:6 * C].partition_broadcast(P)).then_inc(gate_in[odd], 16)
                if there(b - 1):
                    sp.wait_ge(out_ok, NT * b)
                    sp.dma_start(out_d[b - 1], base[odd][:, :, :]).then_inc(out_left[odd], 16)

            iterations(sp, body)
            for i in range(2):
                sp.wait_ge(out_left[i], 16 * (NB // 2))

        @block.gpsimd
        def _(pool):
            pool.memset(half_pow[:, :], -0.5).then_inc(pow_ok, 1)
            pool.wait_ge(pow_ok, 1)

            def rstd(i, n):
                pool.wait_ge(ag_ok[i], n + 1)
                wait_apart(pool, (xh_ok, h1_ok)[i], n, passed[0])
                pool.tensor_scalar(ve[i][:, :], mv[i][:, :, 1], EPS, None, ALU.add).then_inc(ve_ok[i], 1)
                pool.wait_ge(ve_ok[i], n + 1)
                pool.tensor_tensor(rs[i][:, :], ve[i][:, :], half_pow[:, :], ALU.pow).then_inc(rs_ok[i], 1)

            def body(b, hb, par):
                odd = 1 - par
                n = b + 1
                for t in range(NT):
                    if there(b) and t == 1:
                        pool.wait_ge(gate_in[par], 16 * (hb + 1))
                        wait(pool, base_ok, b)
                        pool.tensor_tensor(gated_const[:, :], gate[par][:, :], keep["const_row"][:, :], ALU.mult).then_inc(gc_ok, 1)
                        pool.wait_ge(gc_ok, b + 1)
                        wait(pool, out_left[par], 16 * hb)
                        pool.tensor_tensor(base[par][:, :, :], x1[par][:, :, :],
                                           gated_const[:, :].unsqueeze(1).to_broadcast([P, NT, C]), ALU.add).then_inc(base_ok, 1)
                    mb, mt = previous(b, t)
                    if there(mb):
                        tile = tile_of(mb, mt)
                        pool.wait_ge(usq_ok, tile + 1)
                        wait_apart(pool, y_ok, tile - 3, passed[0])
                        pool.tensor_scalar(uve[mt % 2][:, :], usq[mt % 2][:, :], 1.0 / HID, EPS, ALU.mult, ALU.add).then_inc(uve_ok, 1)
                        pool.wait_ge(uve_ok, tile + 1)
                        pool.tensor_tensor(urs[mt][:, :], uve[mt % 2][:, :], half_pow[:, 0:1], ALU.pow).then_inc(urs_ok, 1)
                    if there(b - 1):
                        pool.wait_ge(y_ok, tile_of(b - 1, t) + 1)
                        pool.tensor_tensor(base[odd][:, t, :], base[odd][:, t, :], y[t % 2][:, :], ALU.add).then_inc(out_ok, 1)
                    if there(n) and t == 0:
                        rstd(1, n)
                    if there(n) and t >= 2:
                        j = t - 2
                        pool.wait_ge(hhi_ok, 2 * n + j + 1)
                        wait(pool, up_ok, NT * (n - 1))
                        pool.tensor_tensor(h_lo[odd][:, :, 2 * P * j:2 * P * j + 2 * P], hf[j][:, :, :],
                                           h_hi[odd][:, :, 2 * P * j:2 * P * j + 2 * P].bitcast(F32),
                                           ALU.subtract).then_inc(hlo_ok, 1)
                    if there(b + 2) and t == 2:
                        rstd(0, b + 2)
                    if there(b + 2) and t == 3:
                        pool.wait_ge(xh_ok, b + 3)
                        pool.wait_ge(ss_in[par], 16 * (hb + 2))
                        wait(pool, h1_ok, b + 2)
                        ss = shift_scale[par]
                        pool.tensor_tensor(h0[:, :, :], xh[:, :, :], ss[:, 1, :].unsqueeze(1).to_broadcast([P, NT, C]),
                                           ALU.mult).then_inc(scaled_ok, 1)
                        pool.wait_ge(scaled_ok, b + 3)
                        pool.tensor_tensor(h0[:, :, :], h0[:, :, :], ss[:, 0, :].unsqueeze(1).to_broadcast([P, NT, C]),
                                           ALU.add).then_inc(h0_ok, 1)

            iterations(pool, body)

        @block.scalar
        def _(act):
            def gain_and_shift(n, j):
                act.wait_ge(xt_ok, 2 * n + j + 1)
                wait(act, hlo_ok, 2 * (n - 1) + j + 1)
                for k in range(KC):
                    ins = act.activation(hf[j][:, k, :].rearrange("p (t c) -> p t c", t=2),
                                         xt_ps[:, :].rearrange("p (t k c) -> p k t c", t=2, k=KC)[:, k],
                                         ACT.Identity, bias=keep["ln1_b"][:, k:k + 1], scale=keep["ln1_g"][:, k:k + 1])
                ins.then_inc(hf_ok, 1)

            def body(b, hb, par):
                odd = 1 - par
                n = b + 1
                for t in range(NT):
                    if t == 2 and there(n):
                        gain_and_shift(n, 0)
                    bb, bt = back(b, t, 2)
                    if there(bb):
                        tile = tile_of(bb, bt)
                        act.wait_ge(ut_ok, tile + 1)
                        wait(act, down_ok, tile - 1)
                        act.activation(u_hi[bt % 2][:, :], ut_ps[:, :], ACT.Copy).then_inc(uhi_ok, 1)
                    mb, mt = previous(b, t)
                    if there(mb):
                        tile = tile_of(mb, mt)
                        act.wait_ge(mean_ok, tile + 1)
                        wait(act, uve_ok, tile - 1)
                        wait(act, usq_ok, tile)
                        act.activation(squares[:, :], u_act[mt % 2][:, :], ACT.Square, bias=minus_mean[mt % 2][:, 0:1],
                                       accum_out=usq[mt % 2][:, 0:1]).then_inc(usq_ok, 1)
                    if there(b):
                        tile = tile_of(b, t)
                        act.wait_ge(up_ok, tile + 1)
                        wait(act, uc_ok, tile - 1)
                        act.activation(u_act[t % 2][:, :], up_ps[t % 2][:, :], ACT.Gelu,
                                       scale=keep["inv_scale"][:, 0:1], accum_out=usum[t % 2][:, 0:1]).then_inc(gelu_ok, 1)
                    if t == 2 and there(n):
                        gain_and_shift(n, 1)

            iterations(act, body)

        @block.vector
        def _(dve):
            def statistics(i, n, src):
                wait(dve, ag_ok[i], n)
                for t in range(NT):
                    ins = dve.bn_stats(stats[:, t, :], src[:, t, :])
                ins.then_inc(st_ok[i], 1)
                wait_apart(dve, st_ok[i], n + 1, passed[1])
                for t in range(NT):
                    ins = dve.bn_aggr(mv[i][:, t, :], stats[:, t, :])
                ins.then_inc(ag_ok[i], 1)

            def normalise(i, n, dst, src, done):
                dve.wait_ge(rs_ok[i], n + 1)
                for t in range(NT):
                    ins = dve.tensor_scalar(dst[:, t, :], src[:, t, :], mv[i][:, t, 0:1], rs[i][:, t:t + 1], ALU.subtract, ALU.mult)
                ins.then_inc(done, 1)

            def body(b, hb, par):
                odd = 1 - par
                n = b + 1
                for t in range(NT):
                    if there(b - 1):
                        tile = tile_of(b - 1, t)
                        dve.wait_ge(down_ok, tile + 1)
                        dve.wait_ge(urs_ok, tile + 1)
                        dve.wait_ge(gate_in[odd], 16 * (hb + (par - 1) // 2 + 1))
                        wait(dve, out_ok, tile - 1)
                        dve.scalar_tensor_tensor(out=y[t % 2][:, :], in0=down_ps[:, C * (t % 2):C * (t % 2) + C],
                                                 scalar=urs[t][:, 0:1], in1=gate[odd][:, :],
                                                 op0=ALU.mult, op1=ALU.mult).then_inc(y_ok, 1)
                    mb, mt = previous(b, t)
                    if there(mb):
                        tile = tile_of(mb, mt)
                        dve.wait_ge(gelu_ok, tile + 1)
                        wait(dve, usq_ok, tile - 1)
                        dve.tensor_scalar(minus_mean[mt % 2][:, :], usum[mt % 2][:, :], -1.0 / HID, None, ALU.mult).then_inc(mean_ok, 1)
                        dve.wait_ge(mean_ok, tile + 1)
                        wait(dve, ut_ok, tile - 1)
                        dve.scalar_tensor_tensor(out=u_c[mt % 2][:, :], in0=u_act[mt % 2][:, :], scalar=minus_mean[mt % 2][:, 0:1],
                                                 in1=keep["gain2"][:, :], op0=ALU.add, op1=ALU.mult).then_inc(uc_ok, 1)
                    bb, bt = back(b, t, 2)
                    if there(bb):
                        tile = tile_of(bb, bt)
                        dve.wait_ge(uhi_ok, tile + 1)
                        wait(dve, down_ok, tile - 1)
                        dve.tensor_tensor(u_lo[bt % 2][:, :], ut_ps[:, :], u_hi[bt % 2][:, :].bitcast(F32),
                                          ALU.subtract).then_inc(ulo_ok, 1)
                    if there(n) and t == 1:
                        wait(dve, xt_ok, 2 * n)
                        normalise(1, n, h1, h0, h1_ok)
                    if there(n) and t >= 2:
                        j = t - 2
                        dve.wait_ge(hf_ok, 2 * n + j + 1)
                        wait(dve, up_ok, NT * (n - 1))
                        dve.tensor_copy(h_hi[odd][:, :, 2 * P * j:2 * P * j + 2 * P], hf[j][:, :, :]).then_inc(hhi_ok, 1)
                    if there(n) and t == 0:
                        dve.wait_ge(h0_ok, n + 1)
                        if not isinstance(n, int) or n > 0:
                            dve.wait_ge(h1_ok, n)
                            dve.wait_ge(ag_ok[0], n + 1)
                        statistics(1, n, h0)
                    if there(b + 2) and t == 2:
                        dve.wait_ge(x1_in[par], 16 * (hb + 2))
                        wait(dve, xh_ok, b + 2)
                        wait(dve, ag_ok[1], b + 2)
                        statistics(0, b + 2, x1[par])
                    if there(b + 2) and t == 3:
                        wait(dve, scaled_ok, b + 2)
                        normalise(0, b + 2, xh, x1[par], xh_ok)

            iterations(dve, body)

        @block.tensor
        def _(pe):
            tern1, tern2 = keep["tern1"], keep["tern2"]

            def transpose_h(n, j):
                pe.wait_ge(h1_ok, n + 1)
                wait(pe, hf_ok, 2 * n + j)
                for tt in range(2):
                    for k in range(KC):
                        ins = pe.transpose(xt_ps[:, P * (KC * tt + k):P * (KC * tt + k) + P],
                                           h1[:, 2 * j + tt, P * k:P * k + P], ident[:, :])
                ins.then_inc(xt_ok, 1)

            def body(b, hb, par):
                odd = 1 - par
                n = b + 1
                for t in range(NT):
                    if t == 2 and there(n):
                        transpose_h(n, 0)
                    bb, bt = back(b, t, 2)
                    if there(bb):
                        tile = tile_of(bb, bt)
                        pe.wait_ge(uc_ok, tile + 1)
                        wait(pe, ulo_ok, tile)
                        for i in range(KH):
                            ins = pe.transpose(ut_ps[:, P * i:P * i + P], u_c[bt % 2][:, P * i:P * i + P], ident[:, :])
                        ins.then_inc(ut_ok, 1)
                    if there(b):
                        tile = NT * b + t
                        pe.wait_ge(hlo_ok, 2 * b + t // 2 + 1)
                        wait(pe, gelu_ok, tile - 1)
                        tok = slice(P * t, P * t + P)
                        for half in range(2):
                            out = up_ps[t % 2][:, 512 * half:512 * half + 512]
                            pe.matmul(out, keep["ones2"][:, :], keep["bias1"][:, 512 * half:512 * half + 512], start=True, stop=False)
                            for k in range(KC):
                                w = tern1[:, HID * k + 512 * half:HID * k + 512 * half + 512]
                                pe.matmul(out, h_lo[par][:, k, tok], w, start=False, stop=False)
                                ins = pe.matmul(out, h_hi[par][:, k, tok], w, start=False, stop=(k == KC - 1))
                        ins.then_inc(up_ok, 1)
                    if t == 2 and there(n):
                        transpose_h(n, 1)
                    bb, bt = back(b, t, 3)
                    if there(bb):
                        tile = tile_of(bb, bt)
                        pe.wait_ge(ulo_ok, tile + 1)
                        wait(pe, y_ok, tile)
                        out = down_ps[:, C * (bt % 2):C * (bt % 2) + C]
                        for i in range(KH):
                            w = tern2[:, C * i:C * i + C]
                            pe.matmul(out, u_lo[bt % 2][:, P * i:P * i + P], w, start=(i == 0), stop=False)
                            ins = pe.matmul(out, u_hi[bt % 2][:, P * i:P * i + P], w, start=False, stop=(i == KH - 1))
                        ins.then_inc(down_ok, 1)

            iterations(pe, body)


def adaln_block(nc, io):
    NB = io["x"].shape[0]
    io["mod_rows"] = nc.dram_tensor("mod_rows", [NB, MODS], F32, kind="Internal").ap()
    io["x1"] = nc.dram_tensor("x1_rows", [NB, T, C], F32, kind="Internal").ap()
    with ExitStack() as whole:
        def sb(name, shape, dt=F32):
            return whole.enter_context(nc.sbuf_tensor(name, shape, dt))

        keep = {"mod_cols": sb("mod_cols", [P, 4, NB]), "ident": sb("ident", [P, P])}
        ident_in = whole.enter_context(nc.semaphore("ident_in"))
        with nc.Block() as block:
            @block.sync
            def _(sp):
                sp.dma_start(keep["ident"][:, :], io["ident"]).then_inc(ident_in, 16)
                sp.wait_ge(ident_in, 16)
        with ExitStack() as ctx:
            setup_phase(nc, io, keep, ctx)
        with ExitStack() as ctx:
            attention_phase(nc, io, keep, ctx)
        keep.update({
            "tern1": sb("tern1", [P, KC * HID], F32R), "tern2": sb("tern2", [P, KH * C], F32R),
            "inv_scale": sb("inv_scale", [P, 2]), "bias1": sb("bias1", [2, HID], F32R), "ones2": sb("ones2", [2, P], F32R),
            "gain2": sb("gain2", [P, HID]), "const_row": sb("const_row", [P, C]),
            "ln1_g": sb("ln1_g", [P, KC]), "ln1_b": sb("ln1_b", [P, KC])})
        with ExitStack() as ctx:
            ternary_phase(nc, io, keep, ctx)
        with ExitStack() as ctx:
            ffn_phase(nc, io, keep, ctx)


def round_12(a):
    m, e = np.frexp(a)
    return np.ldexp(np.rint(np.ldexp(m, 12)), e - 12)


def alibi_rows():
    start = 2.0 ** (-8.0 / HEADS)
    slopes = np.asarray([start * start ** i for i in range(HEADS)], np.float32).astype(np.float64)
    pos = np.arange(T, dtype=np.float64)
    q = np.zeros((P, PAIRS, T))
    k = np.zeros((P, PAIRS, T))
    for head, slope in enumerate(slopes):
        base, pair = 64 * (head % 2), head // 2
        hi = round_12(slope)
        left = -slope * pos
        terms = [(hi + 0 * pos, pos), (slope - hi + 0 * pos, pos)]
        for _ in range(3):
            piece = round_12(left)
            terms.append((piece, 1 + 0 * pos))
            left = left - piece
        for row, (a, b) in enumerate(terms):
            q[base + 4 * row + 3, pair], k[base + 4 * row + 3, pair] = a, b
        k[base + M_ROW, pair] = 1.0
    return q.astype(np.float32), k.astype(np.float32)


def constants():
    q, k = alibi_rows()
    mask = np.where(np.arange(P)[None, :] > np.arange(P)[:, None], MASKED, 0.0).astype(np.float32)
    return {"q_rows": q, "k_rows": k, "mask": np.stack([mask, mask.T], 1), "ident": np.eye(P, dtype=np.float32)}


def by_partition(vector):
    return np.asarray(vector).reshape(-1, P).T


def arrays_of(L0_attn_x, L0_attn_Wqkv, L0_attn_Wout, L0_ffn_ln1_g, L0_ffn_ln1_b, L0_ffn_w1, L0_ffn_b1,
              L0_ffn_ln2_g, L0_ffn_ln2_b, L0_ffn_w2, L0_ffn_b2, L0_c, L0_wmod):
    a = {"x": L0_attn_x, "w_qkv": L0_attn_Wqkv, "w_out": L0_attn_Wout, "ln1_g": by_partition(L0_ffn_ln1_g), "ln1_b": by_partition(L0_ffn_ln1_b),
         "w1": np.asarray(L0_ffn_w1).T, "b1": L0_ffn_b1, "ln2_g": L0_ffn_ln2_g, "ln2_b": by_partition(L0_ffn_ln2_b),
         "w2": np.asarray(L0_ffn_w2).T, "b2": L0_ffn_b2, "c_t": np.asarray(L0_c).T, "w_mod": L0_wmod}
    a = {n: np.ascontiguousarray(v) for n, v in a.items()}
    a.update(constants())
    return a


def kernel(**inputs):
    import concourse.bacc as bacc
    from concourse.bass_utils import run_bass_kernel_spmd

    nc = bacc.Bacc("TRN2", target_bir_lowering=False, num_devices=1)
    arrays = arrays_of(**inputs)
    io = {n: nc.dram_tensor(f"in_{n}", a.shape, mybir.dt.from_np(a.dtype), kind="ExternalInput").ap()
          for n, a in arrays.items()}
    io["out"] = nc.dram_tensor("out", arrays["x"].shape, F32, kind="ExternalOutput").ap()
    adaln_block(nc, io)
    result = run_bass_kernel_spmd(nc, [{f"in_{n}": a for n, a in arrays.items()}], core_ids=[0])
    return result.results[0]["out"]
```

```python
import numpy as np
import concourse.bass as bass
from concourse import mybir
from contextlib import ExitStack

F32 = mybir.dt.float32
F32R = mybir.dt.float32r
BF16 = mybir.dt.bfloat16
ALU = mybir.AluOpType
ACT = mybir.ActivationFunctionType
AX = mybir.AxisListType

P = 128
T = 512
NT = T // P
C = 256
KC = C // P
HEADS = 16
HD = C // HEADS
HG = 4
GROUPS = HEADS // HG
PAIRS = HEADS // 2
UNITS = 10
HID = 1024
KH = HID // P
EPS = 1e-5
MASKED = -1e30
MODS = 6 * C
M_ROW = 63

MISC_USES = (4, 6, 6, 4)
MISC_BEFORE = (0, 2, 5, 8)
MISC_PER_BATCH = 10


def wait(eng, sem, count):
    if isinstance(count, int) and count <= 0:
        return
    eng.wait_ge(sem, count)


def wait_apart(eng, sem, count, passed):
    wait(eng, sem, count)
    eng.sem_inc(passed, 1)


def misc_uses_before(b, slot, order):
    return (b + 1) * MISC_PER_BATCH + MISC_BEFORE[slot] + order // 2


def head_of(group, half, side):
    return HG * group + 2 * half + side


def attention_phase(nc, io, keep, ctx):
    def sb(name, shape, dt=F32):
        return ctx.enter_context(nc.sbuf_tensor(name, shape, dt))

    def pb(name):
        return ctx.enter_context(nc.psum_tensor(name, [P, 512], F32))

    def sem(name):
        return ctx.enter_context(nc.semaphore(name))

    NB = io["x"].shape[0]
    mod_cols, ident = keep["mod_cols"], keep["ident"]
    w_qkv_hi = sb("w_qkv_hi", [P, KC, 3 * C], F32R)
    w_qkv_lo = sb("w_qkv_lo", [P, KC, 3 * C], F32R)
    w_out = sb("w_out", [P, KC, C])
    w_gated = sb("w_gated", [P, C])
    w_gated_hi = sb("w_gated_hi", [P, KC, C], F32R)
    w_gated_lo = sb("w_gated_lo", [P, KC, C], F32R)
    gate = [sb(f"gate{i}", [P, C]) for i in range(2)]
    masks = sb("masks", [P, 2, P], BF16)
    mask, mask_t = masks[:, 0, :], masks[:, 1, :]
    ident_b = sb("ident_b", [P, P], BF16)
    half_pow = sb("half_pow", [P, NT])
    x = [sb(f"x{i}", [P, NT, C]) for i in range(2)]
    stats = sb("stats", [P, NT, 6])
    mean_var = sb("mean_var", [P, NT, 2])
    var_eps = sb("var_eps", [P, NT])
    rstd = sb("rstd", [P, NT])
    h_hi = [sb(f"h_hi{k}", [P, T], F32R) for k in range(KC)]
    h_lo = [sb(f"h_lo{k}", [P, T], F32R) for k in range(KC)]
    dense = {n: sb(f"dense_{n}", [P, 2, T], F32R) for n in ("q_hi", "q_lo", "k_hi", "k_lo")}
    q_st = [sb(f"q_st{i}", [P, PAIRS, T], F32R) for i in range(2)]
    k_st = [sb(f"k_st{i}", [P, PAIRS, T], F32R) for i in range(2)]
    v_ones = [sb(f"v_ones{i}", [P, NT, HEADS, 32]) for i in range(2)]
    probs = [sb(f"probs{i}", [P, UNITS, 512]) for i in range(2)]
    row_max = [sb(f"row_max{i}", [P, 2, 2, NT]) for i in range(2)]
    neg_max = [sb(f"neg_max{i}", [16, P], F32R) for i in range(2)]
    o_sum = [sb(f"o_sum{i}", [P, T]) for i in range(2)]
    recip = sb("recip", [P, 16])
    attn = [sb(f"attn{i}", [P, NT, C]) for i in range(2)]
    attn_hi_all, attn_lo_all = sb("attn_hi", [P, KC * T], F32R), sb("attn_lo", [P, KC * T], F32R)
    attn_hi = [attn_hi_all[:, T * k:T * k + T] for k in range(KC)]
    attn_lo = [attn_lo_all[:, T * k:T * k + T] for k in range(KC)]
    res = [sb(f"res{i}", [P, NT, C]) for i in range(2)]

    mx_bank = [pb(f"mx_bank{i}") for i in range(2)]
    ex_bank = [pb(f"ex_bank{i}") for i in range(2)]
    pv_bank = [pb(f"pv_bank{i}") for i in range(2)]
    misc = [pb(f"misc{i}") for i in range(2)]

    part, mean, clipped, scale = sb("part", [P, 4]), sb("mean", [P, 2]), sb("clipped", [P, 2]), keep["scale"]
    c_in, w_mod_in, w_out_in, raw_in = sem("c_in"), sem("w_mod_in"), sem("w_out_in"), sem("raw_in")
    ident_in, exp_c_ok, silu_ok, mod_ok, mod_cols_ok, rows_ps_ok, rows_in_ok, rows_ok = (
        sem(n) for n in ("ident_in", "exp_c_ok", "silu_ok", "mod_ok", "mod_cols_ok", "rows_ps_ok", "rows_in_ok", "rows_ok"))
    ones_ok, abs_ok, sum_ok, sum_read, tern_ok, chain, setup_out = (
        sem(n) for n in ("ones_ok", "abs_ok", "sum_ok", "sum_read", "tern_ok", "chain", "setup_out"))
    rows_st, tern_out = [sem(f"rows_st{i}") for i in range(2)], [sem(f"tern_out{i}") for i in range(2)]
    const_in, const_ok, dve_const = sem("const_in"), sem("const_ok"), sem("dve_const")
    x_in = [sem(f"x_in{i}") for i in range(2)]
    res_in = [sem(f"res_in{i}") for i in range(2)]
    gate_in = [sem(f"gate_in{i}") for i in range(2)]
    x1_out = [sem(f"x1_out{i}") for i in range(2)]
    stacked = [sem(f"stacked{i}") for i in range(2)]
    max_in = [sem(f"max_in{i}") for i in range(2)]
    stats_ok, aggr_ok, var_ok, rstd_ok, xhat_ok = (sem(n) for n in ("stats_ok", "aggr_ok", "var_ok", "rstd_ok", "xhat_ok"))
    xt_ps, qk_ps, v_ps, mx_ps, ex_ps, pv_ps, ot_ps, mt_ps, at_ps, wo_ps = (
        sem(n) for n in ("xt_ps", "qk_ps", "v_ps", "mx_ps", "ex_ps", "pv_ps", "ot_ps", "mt_ps", "at_ps", "wo_ps"))
    hi_ok, exp_ok, osum_ok = sem("hi_ok"), sem("exp_ok"), sem("osum_ok")
    max_ok, recip_ok = sem("max_ok"), sem("recip_ok")
    hhi_ok, hlo_ok, athi_ok = sem("hhi_ok"), sem("hlo_ok"), sem("athi_ok")
    product_ok, ghi_ok, gated_ok = sem("product_ok"), sem("ghi_ok"), sem("gated_ok")
    passed = [sem(f"passed_{e}") for e in ("pool", "dve")]
    misc_ok = [sem(f"misc_ok{i}") for i in range(2)]

    x_d = io["x"].rearrange("b (t p) c -> b p t c", p=P)
    x1_d = io["x1"].rearrange("b (t p) c -> b p t c", p=P)
    mod_rows = io["mod_rows"]
    FIRST, LAST = 4, NB - 2

    def there(n):
        return not isinstance(n, int) or 0 <= n < NB

    def iterations(eng, body, start):
        for b in range(start, FIRST):
            body(b, b // 2, b % 2)
        with eng.Fori(0, (LAST - FIRST) // 2) as i:
            for par in range(2):
                body(i * 2 + (FIRST + par), i + FIRST // 2, par)
        for b in range(LAST, NB + 2):
            body(b, b // 2, b % 2)

    mask_in = attn[0][:, 0, :].rearrange("p (a j) -> p a j", a=2)
    c_t, e_t, d_t, silu = (attn[0][:, 1, 64 * i:64 * i + KC * NB].rearrange("p (k b) -> p k b", k=KC) for i in range(4))
    w_mod = probs[0][:, 0:6, :].rearrange("p u n -> p (u n)").rearrange("p (k n) -> p k n", k=KC)
    rows = probs[1][0:NB, 0:3, :].rearrange("p u n -> p (u n)")
    sign, neg, mag = o_sum[0][0:NB, 0:C], o_sum[0][0:NB, C:2 * C], o_sum[1][0:NB, 0:C]
    raw = [res[0][:, :, :].rearrange("p t c -> p (t c)"), res[1][:, :, :].rearrange("p t c -> p (t c)"),
           probs[1][:, 4:6, :].rearrange("p u n -> p (u n)"), probs[1][:, 6:8, :].rearrange("p u n -> p (u n)")]
    over = attn[1][:, :, :].rearrange("p t c -> p (t c)")
    under = probs[0][:, 6:8, :].rearrange("p u n -> p (u n)")
    rounded = attn_hi_all[:, :], attn_lo_all[:, :]
    ones = v_ones[1][:, 0, 0:4, :].rearrange("p h d -> p (h d)")
    col_ps = mx_bank[0][:, 0:4 * NB].rearrange("p (j b) -> p j b", j=4)
    row_ps = [a[0:NB, :] for a in (pv_bank[0], pv_bank[1], ex_bank[0])]
    sum_ps = mx_bank[1][:, 0:4]

    def h_t(q, k):
        return x[q][:, :, P * k:P * k + P]

    def tiles_of(a):
        return a[:, :].rearrange("p (t j) -> p t j", j=P)

    def w_qkv_in(k):
        return probs[k][:, PAIRS:UNITS, :].rearrange("p u n -> p (u n)")[:, 0:3 * C]

    EXACT = ((-1, 2), (-1, 3), (0, 0), (0, 1))
    VALUE = ((-1, 1), (-1, 2), (-1, 3), (0, 0))
    MAXT = ((-1, 3), (0, 0), (0, 1), (0, 2))

    def additive_rows(eng, i):
        eng.wait_ge(const_ok, 1)
        for st, src in zip((q_st, k_st), rounded):
            for c in range(NT):
                eng.dma_start(st[i][3:P:4, 2 * c:2 * c + 2, :].bitcast(F32),
                              src[32 * c:32 * c + 32, :].rearrange("p (a n) -> p a n", n=T).bitcast(F32)).then_inc(rows_st[i], 16)

    with nc.Block() as block:
        @block.sync
        def _(sp):
            sp.dma_start(c_t, io["c_t"].rearrange("(k p) b -> p k b", p=P)).then_inc(c_in, 16)
            sp.dma_start(x[0][:, :, :], x_d[0]).then_inc(x_in[0], 16)
            sp.dma_start(w_mod, io["w_mod"].rearrange("(k p) n -> p k n", p=P)).then_inc(w_mod_in, 16)
            sp.dma_start(ident[:, :], io["ident"]).then_inc(ident_in, 16)
            for k in range(KC):
                sp.dma_start(w_qkv_in(k), io["w_qkv"][P * k:P * k + P, :]).then_inc(const_in, 16)
            sp.dma_start(mask_in, io["mask"]).then_inc(const_in, 16)
            for a, n in ((over, "q_rows"), (under, "k_rows")):
                sp.dma_start(a, io[n]).then_inc(const_in, 16)
            for k in range(KC):
                sp.dma_start(raw[k], io["w1"][P * k:P * k + P, :]).then_inc(raw_in, 16)
            w2 = io["w2"].rearrange("(k p) n -> p k n", p=P)
            for i in range(2):
                sp.dma_start(raw[2 + i].rearrange("p (k n) -> p k n", n=C), w2[:, 4 * i:4 * i + 4, :]).then_inc(raw_in, 16)
            sp.dma_start(w_out[:, :, :], io["w_out"].rearrange("(k p) n -> p k n", p=P)).then_inc(w_out_in, 16)

            def body(b, hb, par):
                if isinstance(b, int) and b == -1:
                    additive_rows(sp, 0)
                if isinstance(b, int) and b == 1:
                    sp.wait_ge(setup_out, 16)
                    for i in range(2):
                        sp.wait_ge(tern_out[i], 16 * 2)
                if there(b + 2) and not (isinstance(b, int) and b == -2):
                    wait(sp, hlo_ok, KC * (b + 1))
                    sp.dma_start(x[par][:, :, :], x_d[b + 2]).then_inc(x_in[par], 16)
                n = b - 1
                if there(n):
                    q, half = (par + 1) % 2, hb + (par - 1) // 2
                    wait(sp, x1_out[q], 16 * half)
                    sp.dma_start(res[q][:, :, :], x_d[n]).then_inc(res_in[q], 16)
                    wait(sp, gated_ok, KC * (n - 1))
                    sp.dma_start(gate[q][:, :], mod_rows[n, 2 * C:3 * C].partition_broadcast(P)).then_inc(gate_in[q], 16)
                n = b + 1
                if there(n):
                    q = (par + 1) % 2
                    wait(sp, ex_ps, GROUPS * UNITS * (n - 1))
                    for tile in range(2):
                        for bank in range(2):
                            sp.wait_ge(misc_ok[bank], misc_uses_before(b, 1 + tile, 2 + bank) + 1)
                        for p in range(4):
                            for st, hi, lo, lo_row in ((q_st, "q_hi", "q_lo", 1), (k_st, "k_hi", "k_lo", 2)):
                                for row in range(3):
                                    src = dense[lo if row == lo_row else hi]
                                    sp.dma_start(st[q][row:P:4, 4 * tile + p, :].bitcast(F32),
                                                 src[32 * p:32 * p + 32, tile, :].bitcast(F32)).then_inc(stacked[tile], 16)
                n = b - 2
                if there(n):
                    for bank in range(2):
                        sp.wait_ge(misc_ok[bank], misc_uses_before(b, 2, 4 + bank) + 1)
                    sp.dma_start(x1_d[n], res[par][:, :, :]).then_inc(x1_out[par], 16)

            iterations(sp, body, -2)
            for i in range(2):
                sp.wait_ge(x1_out[i], 16 * (NB // 2))

        @block.gpsimd
        def _(pool):
            pool.memset(half_pow[:, :], -0.5)
            for i in range(2):
                ins = pool.memset(v_ones[i][:, :, :, :], 1.0)
            ins.then_inc(ones_ok, 1)

            def body(b, hb, par):
                if isinstance(b, int) and b == 0:
                    pool.wait_ge(rows_ok, 1)
                    pool.dma_start(mod_rows, rows).then_inc(setup_out, 16)
                    for i in range(4):
                        pool.wait_ge(tern_ok, i + 1)
                        pool.dma_start(io["tern"][:, 1024 * i:1024 * i + 1024],
                                     rounded[i % 2].bitcast(F32)).then_inc(tern_out[i % 2], 16)
                n = b - 2
                if there(n):
                    wait(pool, gate_in[par], 16 * hb)
                    wait(pool, wo_ps, 2 * n)
                    if isinstance(n, int) and n == 0:
                        pool.wait_ge(w_out_in, 16)
                    for k in range(KC):
                        wait(pool, gated_ok, KC * n + k)
                        pool.tensor_tensor(w_gated[:, :], w_out[:, k, :], gate[par][:, :], ALU.mult).then_inc(product_ok, 1)
                        pool.tensor_tensor(w_gated_hi[:, k, :], w_out[:, k, :], gate[par][:, :], ALU.mult).then_inc(ghi_ok, 1)
                        pool.wait_ge(product_ok, KC * n + k + 1)
                        pool.wait_ge(ghi_ok, KC * n + k + 1)
                        pool.tensor_tensor(w_gated_lo[:, k, :], w_gated[:, :], w_gated_hi[:, k, :].bitcast(F32),
                                           ALU.subtract).then_inc(gated_ok, 1)
                for s in range(4):
                    m, mg = MAXT[s]
                    if there(b + m):
                        pool.wait_ge(misc_ok[0], misc_uses_before(b, s, 0) + 1)
                        wait_apart(pool, ex_ps, GROUPS * UNITS * (b + m - 1), passed[0])
                        for half in range(2):
                            pool.dma_start(q_st[(par + m) % 2][M_ROW:P:64, 2 * mg + half, :].bitcast(F32),
                                           neg_max[mg % 2][8 * half:8 * half + 8, :].bitcast(F32)).then_inc(max_in[mg % 2], 16)
                    if s == 0 and there(b + 1):
                        for k in range(KC):
                            pool.wait_ge(hhi_ok, KC * (b + 1) + k + 1)
                            wait(pool, v_ps, 2 * (b + 1))
                            pool.tensor_tensor(tiles_of(h_lo[k]), h_t((par + 1) % 2, k), tiles_of(h_hi[k]).bitcast(F32),
                                               ALU.subtract).then_inc(hlo_ok, 1)
                    if s == 1 and isinstance(b, int) and b == -1:
                        additive_rows(pool, 1)
                    if s == 3 and there(b + 2):
                        pool.wait_ge(aggr_ok, b + 3)
                        wait_apart(pool, xhat_ok, b + 2, passed[0])
                        pool.tensor_scalar(var_eps[:, :], mean_var[:, :, 1], EPS, None, ALU.add).then_inc(var_ok, 1)
                        pool.wait_ge(var_ok, b + 3)
                        pool.tensor_tensor(rstd[:, :], var_eps[:, :], half_pow[:, :], ALU.pow).then_inc(rstd_ok, 1)

            iterations(pool, body, -2)

        @block.scalar
        def _(act):
            act.wait_ge(c_in, 16)
            act.activation(e_t, c_t, ACT.Exp, scale=-1.0).then_inc(exp_c_ok, 1)

            def body(b, hb, par):
                prep = there(b + 1)
                first = isinstance(b, int) and b == -1
                for s in range(4):
                    if first and s == 0:
                        act.wait_ge(rows_ps_ok, 1)
                        for i in range(3):
                            ins = act.activation(rows[:, 512 * i:512 * i + 512], row_ps[i], ACT.Copy)
                        ins.then_inc(rows_in_ok, 1)
                        act.wait_ge(mod_cols_ok, 1)
                    if first and s == 1:
                        act.wait_ge(raw_in, 16 * 4)
                        act.wait_ge(const_ok, 1)
                        for i in range(4):
                            wait(act, abs_ok, i)
                            act.activation(under, raw[i], ACT.Abs, accum_out=part[:, i:i + 1]).then_inc(abs_ok, 1)
                    if isinstance(b, int) and b == 0 and s == 2:
                        act.wait_ge(setup_out, 16)
                        act.wait_ge(tern_ok, 4)
                    e, g = EXACT[s]
                    n = b + e
                    v, vg = VALUE[s]
                    for u in range(UNITS):
                        if there(n):
                            act.wait_ge(ex_ps, GROUPS * UNITS * n + UNITS * g + u + 1)
                            if u == 0:
                                wait(act, pv_ps, GROUPS * n + g - 1)
                            act.activation(probs[g % 2][:, u, :], ex_bank[u % 2][:, :], ACT.Exp).then_inc(exp_ok, 1)
                        if (s, u) in ((0, 6), (1, 0)) and prep:
                            k = s
                            act.wait_ge(xt_ps, KC * (b + 1) + k + 1)
                            act.activation(h_t((par + 1) % 2, k), tiles_of(misc[k]), ACT.Identity,
                                           bias=mod_cols[:, k, bass.ds(b + 1, 1)],
                                           scale=mod_cols[:, 2 + k, bass.ds(b + 1, 1)]).then_inc(misc_ok[k], 1)
                        if s in (1, 2) and u in (4, 6) and prep:
                            which = "q_hi" if u == 4 else "k_hi"
                            use = 4 * (b + 1) + 2 * (s - 1) + (u - 4) // 2
                            act.wait_ge(qk_ps, use + 1)
                            if u == 4:
                                wait(act, stacked[s - 1], 24 * 16 * (b + 1))
                            act.activation(dense[which][:, s - 1, :], misc[(u - 4) // 2][:, :], ACT.Copy).then_inc(hi_ok, 1)
                        if s == 1 and u >= 8 and there(b - 2):
                            k = u - 8
                            act.wait_ge(at_ps, 2 * (b - 2) + k + 1)
                            wait(act, wo_ps, 2 * (b - 2))
                            act.activation(attn_hi[k], misc[k][:, :], ACT.Copy).then_inc(athi_ok, 1)
                        if s == 3 and u in (5, 7) and prep:
                            j = (u - 5) // 2
                            act.wait_ge(v_ps, 2 * (b + 1) + j + 1)
                            wait(act, pv_ps, GROUPS * b)
                            if isinstance(b, int) and b < 1:
                                act.wait_ge(ones_ok, 1)
                                wait(act, sum_ok, b + 1)
                            for t in range(2):
                                ins = act.activation(v_ones[(par + 1) % 2][:, 2 * j + t, :, 0:HD],
                                                     misc[j][:, C * t:C * t + C].rearrange("p (h d) -> p h d", d=HD),
                                                     ACT.Copy)
                            ins.then_inc(misc_ok[j], 1)
                        if u == 9 and there(b + v):
                            n_pv = GROUPS * (b + v) + vg
                            act.wait_ge(pv_ps, n_pv + 1)
                            wait(act, ot_ps, n_pv - 1)
                            act.activation(o_sum[vg % 2][:, :], pv_bank[vg % 2][:, :], ACT.Copy).then_inc(osum_ok, 1)

            iterations(act, body, -1)

        @block.vector
        def _(dve):
            links = 0

            def link(ins):
                nonlocal links
                links += 1
                ins.then_inc(chain, 1)
                dve.wait_ge(chain, links)

            dve.wait_ge(exp_c_ok, 1)
            link(dve.tensor_scalar_add(d_t, e_t, 1.0))
            link(dve.reciprocal(e_t, d_t))
            dve.tensor_tensor(silu, c_t, e_t, ALU.mult).then_inc(silu_ok, 1)

            def constants():
                dve.wait_ge(mod_ok, 1)
                dve.tensor_copy(mod_cols[:, 0:2, :], col_ps[:, 0:2, :])
                dve.tensor_scalar_add(mod_cols[:, 2:4, :], col_ps[:, 2:4, :], 1.0).then_inc(mod_cols_ok, 1)
                dve.wait_ge(ident_in, 16)
                dve.wait_ge(const_in, 16 * 5)
                for k in range(KC):
                    dve.tensor_scalar(w_qkv_hi[:, k, 0:C], w_qkv_in(k)[:, 0:C], HD ** -0.5, None, ALU.mult)
                    dve.tensor_copy(w_qkv_hi[:, k, C:3 * C], w_qkv_in(k)[:, C:3 * C]).then_inc(dve_const, 1)
                    dve.wait_ge(dve_const, k + 1)
                    dve.scalar_tensor_tensor(out=w_qkv_lo[:, k, 0:C], in0=w_qkv_in(k)[:, 0:C], scalar=HD ** -0.5,
                                             in1=w_qkv_hi[:, k, 0:C].bitcast(F32), op0=ALU.mult, op1=ALU.subtract)
                    dve.tensor_tensor(w_qkv_lo[:, k, C:3 * C], w_qkv_in(k)[:, C:3 * C],
                                      w_qkv_hi[:, k, C:3 * C].bitcast(F32), ALU.subtract)
                for a, b_ in zip(rounded, (over, under)):
                    dve.tensor_copy(a, b_)
                dve.tensor_copy(masks[:, :, :], mask_in)
                dve.tensor_copy(ident_b[:, :], ident[:, :]).then_inc(const_ok, 1)

            def modulation_rows():
                dve.wait_ge(rows_in_ok, 1)
                link(dve.tensor_scalar_add(rows[:, 4 * C:5 * C], rows[:, 4 * C:5 * C], 1.0))
                for gate_ in (2, 5):
                    g = rows[:, gate_ * C:gate_ * C + C]
                    link(dve.tensor_scalar(sign, g, 0.0, 2.0, ALU.is_ge, ALU.mult))
                    link(dve.tensor_scalar(neg, g, -1.0, None, ALU.mult))
                    link(dve.tensor_tensor(mag, g, neg, ALU.max))
                    link(dve.tensor_scalar(neg, mag, 0.25, None, ALU.max))
                    link(dve.tensor_scalar(mag, sign, 1.0, None, ALU.subtract))
                    link(dve.tensor_tensor(g, mag, neg, ALU.mult))
                dve.sem_inc(rows_ok, 1)

            def ternary_weights():
                dve.wait_ge(sum_ok, 1)
                sums = sum_ps.rearrange("p (w h) -> p w h", w=2)
                link(dve.reduce_sum(mean[:, :], sums, AX.X))
                link(dve.tensor_scalar(clipped[:, :], mean[:, :], 1.0 / (HID * C), 1e-5, ALU.mult, ALU.max))
                dve.sem_inc(sum_read, 1)
                link(dve.reciprocal(scale[:, :], clipped[:, :]))
                link(dve.reciprocal(keep["inv_scale"][:, :], scale[:, :]))
                for i in range(4):
                    w = i // 2
                    wait(dve, tern_ok, i)
                    if i < 2:
                        for j in range(2):
                            dve.wait_ge(rows_st[j], 16 * 2 * NT)
                    else:
                        dve.wait_ge(tern_out[i % 2], 16)
                    link(dve.tensor_scalar(over, raw[i], scale[:, w:w + 1], 0.5, ALU.mult, ALU.is_gt))
                    link(dve.tensor_scalar(under, raw[i], scale[:, w:w + 1], -0.5, ALU.mult, ALU.is_lt))
                    dve.tensor_tensor(rounded[i % 2], over, under, ALU.subtract).then_inc(tern_ok, 1)

            def normalise_x(n, q, t):
                if t == 0:
                    dve.wait_ge(rstd_ok, n + 1)
                ins = dve.tensor_scalar(x[q][:, t, :], x[q][:, t, :], mean_var[:, t, 0:1], rstd[:, t:t + 1],
                                        ALU.subtract, ALU.mult)
                if t == NT - 1:
                    ins.then_inc(xhat_ok, 1)

            def statistics(n, half, q, t):
                if t == 0:
                    dve.wait_ge(x_in[q], 16 * (half + 1))
                    wait(dve, xhat_ok, n)
                    wait(dve, aggr_ok, n)
                ins = dve.bn_stats(stats[:, t, :], x[q][:, t, :])
                if t == NT - 1:
                    ins.then_inc(stats_ok, 1)

            def mean_and_variance(n):
                wait_apart(dve, stats_ok, n + 1, passed[1])
                for t in range(NT):
                    ins = dve.bn_aggr(mean_var[:, t, :], stats[:, t, :])
                ins.then_inc(aggr_ok, 1)

            def body(b, hb, par):
                prep = there(b + 1)
                if isinstance(b, int) and b == 0:
                    modulation_rows()
                    ternary_weights()
                for s in range(4):
                    m, mg = MAXT[s]
                    for u in range(UNITS):
                        if s == 0 and u < NT and prep:
                            normalise_x(b + 1, (par + 1) % 2, u)
                            if isinstance(b, int) and b == -1 and u == NT - 1:
                                constants()
                        if there(b):
                            side, v = u % 2, u // 2
                            dve.wait_ge(mx_ps, GROUPS * UNITS * b + UNITS * s + u + 1)
                            if u == 0:
                                wait(dve, mt_ps, GROUPS * b + s - 1)
                            bank, out = mx_bank[u % 2], row_max[s % 2]
                            if v in (0, 2):
                                ins = dve.reduce_max(out[:, v // 2, side, 3:4], bank[:, :], AX.X)
                            elif v in (1, 3):
                                dve.reduce_max(out[:, v // 2, side, 0:1], bank[:, 0:P], AX.X)
                                ins = dve.reduce_max(out[:, v // 2, side, 2:3], bank[:, P:512], AX.X)
                            else:
                                ins = dve.reduce_max(out[:, :, side, 1], bank[:, :].rearrange("p (h j) -> p h j", h=2), AX.X)
                            ins.then_inc(max_ok, 1)
                        if u == 2 and there(b + m):
                            n_mt = GROUPS * (b + m) + mg
                            dve.wait_ge(mt_ps, n_mt + 1)
                            wait(dve, max_in[mg % 2], 32 * (2 * (b + m) + mg // 2))
                            dve.tensor_scalar(neg_max[mg % 2][:, :], misc[0][0:16, 0:P], -1.0, None,
                                              ALU.mult).then_inc(misc_ok[0], 1)
                        if u == (4 if s == 0 else 3) and there(b - 1):
                            n_ot = GROUPS * (b - 1) + s
                            dve.wait_ge(ot_ps, n_ot + 1)
                            wait(dve, misc_ok[1], misc_uses_before(b - 1, 3, 1) + 1 if s == 0 else misc_uses_before(b, s - 1, 1) + 1)
                            ot = misc[1][:, :].rearrange("p (a c) -> p a c", c=32)
                            dve.reciprocal(recip[:, :], ot[:, :, HD]).then_inc(recip_ok, 1)
                            dve.wait_ge(recip_ok, n_ot + 1)
                            wait(dve, at_ps, 2 * (b - 2))
                            dve.tensor_tensor(
                                attn[(par + 1) % 2][:, :, 64 * s:64 * s + 64].rearrange("p i (h d) -> p i h d", d=HD),
                                ot[:, :, 0:HD].rearrange("p (i h) d -> p i h d", h=HG),
                                recip[:, :].rearrange("p (i h) -> p i h", h=HG).unsqueeze(3).to_broadcast([P, NT, HG, HD]),
                                ALU.mult).then_inc(misc_ok[1], 1)
                        if (s, u) in ((0, 7), (1, 1)) and prep:
                            k = s
                            dve.wait_ge(misc_ok[k], misc_uses_before(b, 0, 2 + k) + 1)
                            wait(dve, v_ps, 2 * (b + 1))
                            dve.tensor_copy(tiles_of(h_hi[k]), h_t((par + 1) % 2, k)).then_inc(hhi_ok, 1)
                        if (s, u) in ((1, 9), (2, 0)) and there(b - 2):
                            k = s - 1
                            dve.wait_ge(athi_ok, KC * (b - 2) + k + 1)
                            dve.tensor_tensor(attn_lo[k], misc[k][:, :], attn_hi[k].bitcast(F32),
                                              ALU.subtract).then_inc(misc_ok[k], 1)
                        if s in (1, 2) and u in (5, 7) and prep:
                            hi, lo = ("q_hi", "q_lo") if u == 5 else ("k_hi", "k_lo")
                            use = 4 * (b + 1) + 2 * (s - 1) + (u - 5) // 2
                            dve.wait_ge(hi_ok, use + 1)
                            wait(dve, stacked[s - 1], 24 * 16 * (b + 1))
                            dve.tensor_tensor(dense[lo][:, s - 1, :], misc[(u - 5) // 2][:, :],
                                              dense[hi][:, s - 1, :].bitcast(F32), ALU.subtract).then_inc(misc_ok[(u - 5) // 2], 1)
                        if s == 3 and u < 2 and there(b - 2):
                            n, j = b - 2, u
                            dve.wait_ge(wo_ps, 2 * n + j + 1)
                            wait(dve, res_in[par], 16 * hb)
                            dve.tensor_tensor(res[par][:, 2 * j:2 * j + 2, :], res[par][:, 2 * j:2 * j + 2, :],
                                              misc[j][:, :].rearrange("p (t c) -> p t c", t=2), ALU.add).then_inc(misc_ok[j], 1)
                        if s == 3 and 2 <= u < 2 + NT and there(b + 2):
                            statistics(b + 2, hb + 1, par, u - 2)
                        if s == 3 and u == 7 and there(b + 2):
                            mean_and_variance(b + 2)

            iterations(dve, body, -2)

        @block.tensor
        def _(pe):
            pe.wait_ge(w_mod_in, 16)
            pe.wait_ge(silu_ok, 1)
            for j in range(4):
                for k in range(KC):
                    ins = pe.matmul(col_ps[:, j, :], w_mod[:, k, j * P:j * P + P], silu[:, k, :],
                                    start=(k == 0), stop=(k == KC - 1))
            ins.then_inc(mod_ok, 1)
            for i in range(3):
                for k in range(KC):
                    ins = pe.matmul(row_ps[i], silu[:, k, :], w_mod[:, k, 512 * i:512 * i + 512],
                                    start=(k == 0), stop=(k == KC - 1))
            ins.then_inc(rows_ps_ok, 1)
            pe.wait_ge(ident_in, 16)

            def misc_free(b, s, order):
                wait(pe, misc_ok[order % 2], misc_uses_before(b, s, order))
                return misc[order % 2]

            def misc_skip(b, s, order):
                wait(pe, misc_ok[order % 2], misc_uses_before(b, s, order))
                pe.sem_inc(misc_ok[order % 2], 1)

            def product(out, hi, lo, w_hi, w_lo, k):
                pe.matmul(out, lo, w_hi, start=(k == 0), stop=False)
                pe.matmul(out, hi, w_lo, start=False, stop=False)
                return pe.matmul(out, hi, w_hi, start=False, stop=(k == KC - 1))


            def steps(u):
                return 2 if u // 2 in (1, 3) else 1

            def max_scores(n, g, u, q, step):
                side, v, bank = u % 2, u // 2, mx_bank[u % 2]
                rows = slice(64 * side, 64 * side + M_ROW)
                if step == 0:
                    if u == 0 and g % 2 == 0:
                        pe.wait_ge(stacked[g // 2], 24 * 16 * (n + 1))
                        if isinstance(n, int) and n < 2:
                            pe.wait_ge(rows_st[n], 16 * 2 * NT)
                    wait(pe, max_ok, GROUPS * UNITS * n + UNITS * g + u - 1)
                for half in range(2 if v == 4 else 1):
                    pair = 2 * g + (half if v == 4 else v // 2)
                    block_, keys, at = {0: (3, 512, 0), 1: ((0, 256, 0), (2, 384, P))[step], 2: (1, 256, 256 * half)}[
                        2 if v == 4 else v % 2]
                    pe.matmul(bank[:, at:at + keys], q_st[q][rows, pair, P * block_:P * block_ + P],
                              k_st[q][rows, pair, 0:keys], start=(half == 0), stop=False)

            def max_masks(u, step):
                v, bank = u // 2, mx_bank[u % 2]
                if v == 4:
                    ins = add_masks(bank, mask, P, 384)
                else:
                    ins = add_masks(bank, mask, 384 if v % 2 == 0 or step else 0)
                if step == steps(u) - 1:
                    ins.then_inc(mx_ps, 1)

            def exact_scores(n, g, u, q, step):
                side, v, bank = (u + 1) % 2, u // 2, ex_bank[u % 2]
                rows = slice(64 * side, 64 * side + 64)
                if step == 0:
                    if u == 0:
                        pe.wait_ge(max_in[g % 2], 32 * (2 * n + g // 2 + 1))
                    wait(pe, exp_ok, GROUPS * UNITS * n + UNITS * g + u - 1)
                for half in range(2 if v == 4 else 1):
                    pair = 2 * g + (half if v == 4 else v // 2)
                    keys, first, at = {0: (0, 0, 0), 1: ((3, 256, 256), (1, P, 0))[step], 2: (2, 256, 256 * half)}[
                        2 if v == 4 else v % 2]
                    pe.matmul(bank[:, at:at + T - first], k_st[q][rows, pair, P * keys:P * keys + P],
                              q_st[q][rows, pair, first:T], start=(half == 0), stop=False)

            def exact_masks(u, step):
                v, bank = u // 2, ex_bank[u % 2]
                if v == 4:
                    ins = add_masks(bank, mask_t, 0, 256)
                else:
                    ins = add_masks(bank, mask_t, 384 if v % 2 and step == 0 else 0)
                if step == steps(u) - 1:
                    ins.then_inc(ex_ps, 1)

            def add_masks(bank, mask_, first, last=None):
                if last is None:
                    return pe.matmul(bank[:, first:first + P], ident_b[:, :], mask_, start=False, stop=True)
                blocks = bank[:, :].rearrange("p (a j) -> p a j", j=P)[:, first // P:last // P + 1:(last - first) // P]
                return pe.matmul(blocks, ident_b[:, :], mask_.unsqueeze(1).to_broadcast([P, 2, P]), start=False, stop=True)

            def values(n, g, q, keys):
                if keys == 0:
                    pe.wait_ge(exp_ok, GROUPS * UNITS * n + UNITS * (g + 1))
                    wait(pe, osum_ok, GROUPS * n + g - 1)
                for hh in range(HG):
                    half, side = hh // 2, hh % 2
                    odd = 1 - side
                    if keys == 0:
                        moving = probs[g % 2][:, 4 * half + odd, :]
                    elif keys == 1:
                        moving = probs[g % 2][:, 4 * half + 2 + odd, 0:384]
                    elif keys == 3:
                        moving = probs[g % 2][:, 4 * half + 2 + odd, 384:512]
                    else:
                        moving = probs[g % 2][:, 8 + odd, 256 * half:256 * half + 256]
                    ins = pe.matmul(pv_bank[g % 2][32 * hh:32 * hh + 32, P * keys:T],
                                    v_ones[q][:, keys, HG * g + hh, :], moving, start=(keys == 0), stop=(keys == NT - 1))
                if keys == NT - 1:
                    ins.then_inc(pv_ps, 1)

            def body(b, hb, par):
                prep = there(b + 1)
                for s in range(4):
                    e, eg = EXACT[s]
                    v, vg = VALUE[s]
                    m, mg = MAXT[s]
                    if isinstance(b, int) and b == -1 and s == 1:
                        pe.wait_ge(const_ok, 1)
                    if isinstance(b, int) and b == -1 and s == 3:
                        pe.wait_ge(ones_ok, 1)
                        pe.wait_ge(abs_ok, 4)
                        pe.matmul(sum_ps, ones, part[:, :], start=True, stop=True).then_inc(sum_ok, 1)
                    if isinstance(b, int) and b == 0 and s == 0:
                        pe.wait_ge(rows_in_ok, 1)
                        pe.wait_ge(sum_read, 1)
                    for u in range(UNITS):
                        for step in range(steps(u)):
                            if there(b):
                                max_scores(b, s, u, par, step)
                            if there(b + e):
                                exact_scores(b + e, eg, u, (par + e) % 2, step)
                            if there(b):
                                max_masks(u, step)
                            if there(b + e):
                                exact_masks(u, step)
                        if u in (1, 3, 5, 7) and there(b + v):
                            values(b + v, vg, (par + v) % 2, (u - 1) // 2)
                        if u == 1:
                            if there(b + m):
                                bank = misc_free(b, s, 0)
                                pe.wait_ge(max_ok, (GROUPS * (b + m) + mg + 1) * UNITS)
                                pe.matmul(bank[0:16, 0:P], row_max[mg % 2][:, :, :, :].rearrange("p a b c -> p (a b c)"),
                                          ident[:, :], start=True, stop=True).then_inc(mt_ps, 1)
                            else:
                                misc_skip(b, s, 0)
                        if u == (3 if s == 0 else 2):
                            if there(b - 1):
                                bank = misc_free(b, s, 1)
                                pe.wait_ge(osum_ok, GROUPS * (b - 1) + s + 1)
                                for i in range(NT):
                                    ins = pe.transpose(bank[:, P * i:P * i + P], o_sum[s % 2][:, P * i:P * i + P], ident[:, :])
                                ins.then_inc(ot_ps, 1)
                            else:
                                misc_skip(b, s, 1)
                        if s == 0 and u in (5, 9):
                            k = (u - 5) // 4
                            if prep:
                                bank = misc_free(b, s, 2 + k)
                                pe.wait_ge(xhat_ok, b + 2)
                                for t in range(NT):
                                    ins = pe.transpose(bank[:, P * t:P * t + P], x[(par + 1) % 2][:, t, P * k:P * k + P], ident[:, :])
                                ins.then_inc(xt_ps, 1)
                            else:
                                misc_skip(b, s, 2 + k)
                        if s in (1, 2) and u in (3, 5):
                            j = (u - 3) // 2
                            if prep:
                                bank = misc_free(b, s, 2 + j)
                                pe.wait_ge(hlo_ok, KC * (b + 2))
                                col = C * j + P * (s - 1)
                                for k in range(KC):
                                    pe.matmul(bank[:, :], w_qkv_lo[:, k, col:col + P], h_hi[k][:, :], start=(k == 0), stop=False)
                                    pe.matmul(bank[:, :], w_qkv_hi[:, k, col:col + P], h_lo[k][:, :], start=False, stop=False)
                                    ins = pe.matmul(bank[:, :], w_qkv_hi[:, k, col:col + P], h_hi[k][:, :],
                                                    start=False, stop=(k == KC - 1))
                                ins.then_inc(qk_ps, 1)
                            else:
                                misc_skip(b, s, 2 + j)
                        if s == 1 and u in (8, 9):
                            k = u - 8
                            if there(b - 2):
                                bank = misc_free(b, s, 4 + k)
                                pe.wait_ge(misc_ok[1], misc_uses_before(b - 1, 3, 1) + 1)
                                for t in range(NT):
                                    ins = pe.transpose(bank[:, P * t:P * t + P], attn[par][:, t, P * k:P * k + P], ident[:, :])
                                ins.then_inc(at_ps, 1)
                            else:
                                misc_skip(b, s, 4 + k)
                        if s == 2 and u in (7, 9):
                            j = (u - 7) // 2
                            if there(b - 2):
                                bank = misc_free(b, s, 4 + j)
                                for i in range(KC):
                                    pe.wait_ge(misc_ok[i], misc_uses_before(b, 1, 4 + i) + 1)
                                pe.wait_ge(gated_ok, KC * (b - 1))
                                for t in range(2):
                                    for k in range(KC):
                                        tok = P * (2 * j + t)
                                        ins = product(bank[:, C * t:C * t + C], attn_hi[k][:, tok:tok + P], attn_lo[k][:, tok:tok + P],
                                                      w_gated_hi[:, k, :], w_gated_lo[:, k, :], k)
                                ins.then_inc(wo_ps, 1)
                            else:
                                misc_skip(b, s, 4 + j)
                        if s == 3 and u in (4, 6):
                            j = (u - 4) // 2
                            if prep:
                                bank = misc_free(b, s, 2 + j)
                                for t in range(2):
                                    for k in range(KC):
                                        tok = P * (2 * j + t)
                                        ins = product(bank[:, C * t:C * t + C], h_hi[k][:, tok:tok + P], h_lo[k][:, tok:tok + P],
                                                      w_qkv_hi[:, k, 2 * C:3 * C], w_qkv_lo[:, k, 2 * C:3 * C], k)
                                ins.then_inc(v_ps, 1)
                            else:
                                misc_skip(b, s, 2 + j)

            iterations(pe, body, -1)


def ffn_phase(nc, io, keep, ctx):
    def sb(name, shape, dt=F32):
        return ctx.enter_context(nc.sbuf_tensor(name, shape, dt))

    def pb(name, n):
        return ctx.enter_context(nc.psum_tensor(name, [P, n], F32))

    def sem(name):
        return ctx.enter_context(nc.semaphore(name))

    NB = io["x"].shape[0]
    ident = keep["ident"]
    half_pow = sb("f_half_pow", [P, NT])
    x1 = [sb(f"f_x1{i}", [P, NT, C]) for i in range(2)]
    base = [sb(f"f_base{i}", [P, NT, C]) for i in range(2)]
    shift_scale = [sb(f"f_ss{i}", [P, 2, C]) for i in range(2)]
    gate = [sb(f"f_gate{i}", [P, C]) for i in range(2)]
    gated_const = sb("f_gc", [P, C])
    xh = sb("f_xh", [P, NT, C])
    h0 = sb("f_h0", [P, NT, C])
    h1 = sb("f_h1", [P, NT, C])
    hf = [sb(f"f_hf{i}", [P, KC, 2 * P]) for i in range(2)]
    h_hi = [sb(f"f_hhi{i}", [P, KC, T], F32R) for i in range(2)]
    h_lo = [sb(f"f_hlo{i}", [P, KC, T], F32R) for i in range(2)]
    stats = sb("f_stats", [P, NT, 6])
    mv = [sb(f"f_mv{i}", [P, NT, 2]) for i in range(2)]
    ve = [sb(f"f_ve{i}", [P, NT]) for i in range(2)]
    rs = [sb(f"f_rs{i}", [P, NT]) for i in range(2)]
    usum = [sb(f"f_usum{i}", [P, 1]) for i in range(2)]
    minus_mean = [sb(f"f_mm{i}", [P, 1]) for i in range(2)]
    usq = [sb(f"f_usq{i}", [P, 1]) for i in range(2)]
    squares = sb("f_squares", [P, HID])
    uve = [sb(f"f_uve{i}", [P, 1]) for i in range(2)]
    urs = [sb(f"f_urs{i}", [P, 1]) for i in range(NT)]
    u_act = [sb(f"f_u{i}", [P, HID]) for i in range(2)]
    u_c = [sb(f"f_uc{i}", [P, HID]) for i in range(2)]
    u_hi = [sb(f"f_uhi{i}", [P, HID], F32R) for i in range(2)]
    u_lo = [sb(f"f_ulo{i}", [P, HID], F32R) for i in range(2)]
    y = [sb(f"f_y{i}", [P, C]) for i in range(2)]
    tern1, tern2 = sb("tern1", [P, KC * HID], F32R), sb("tern2", [P, KH * C], F32R)
    inv_scale, scale = keep["inv_scale"], keep["scale"]
    b1_two, b1_s, b1_hi, bias1 = sb("b1_two", [2, HID]), sb("b1_s", [2, HID]), sb("b1_hi", [2, HID], F32R), sb("bias1", [2, HID], F32R)
    ones2 = sb("ones2", [2, P], F32R)
    minus_row1 = sb("minus_row1", [2, 1])
    gain2 = sb("gain2", [P, HID])
    ln1_g, ln1_b = sb("ln1_g", [P, KC]), sb("ln1_b", [P, KC])
    g2, ln2_b, b2_all = sb("g2", [P, HID]), sb("ln2_b", [P, KH]), sb("b2_all", [P, C])
    shift_l = sb("shift_l", [P, KH, P])
    tmp_c, const_row = sb("tmp_c", [P, C]), sb("const_row", [P, C])
    up_ps = [pb(f"up_ps{i}", 2 * 512) for i in range(2)]
    ut_ps = pb("ut_ps", 2 * 512)
    down_ps = pb("down_ps", 2 * C)
    xt_ps = pb("xt_ps_f", 512)

    passed = [sem(f"f_passed_{e}") for e in ("pool", "dve")]
    x1_in = [sem(f"f_x1_in{i}") for i in range(2)]
    base_in = [sem(f"f_base_in{i}") for i in range(2)]
    ss_in = [sem(f"f_ss_in{i}") for i in range(2)]
    gate_in = [sem(f"f_gate_in{i}") for i in range(2)]
    out_left = [sem(f"f_out{i}") for i in range(2)]
    st_ok = [sem(f"f_st{i}") for i in range(2)]
    ag_ok = [sem(f"f_ag{i}") for i in range(2)]
    ve_ok = [sem(f"f_ve_ok{i}") for i in range(2)]
    rs_ok = [sem(f"f_rs_ok{i}") for i in range(2)]
    xh_ok, scaled_ok, h0_ok, h1_ok, gc_ok, base_ok = (sem("f_" + n) for n in ("xh", "scaled", "h0", "h1", "gc", "base"))
    xt_ok, hf_ok, hhi_ok, hlo_ok = (sem("f_" + n) for n in ("xt", "hf_ok", "hhi_ok", "hlo_ok"))
    up_ok, gelu_ok, mean_ok, usq_ok, uve_ok, urs_ok, uc_ok, ut_ok, uhi_ok, ulo_ok, down_ok, y_ok, out_ok, pow_ok = (
        sem("f_" + n) for n in ("up", "gelu", "mean", "usq", "uve_ok", "urs_ok", "uc", "ut", "uhi_ok", "ulo_ok", "down", "y_ok", "out_ok", "pow"))

    const_in, tern_in, chain, shift_ok, const_ps_ok, const_ok, row_ok = (
        sem("f_" + n) for n in ("const_in", "tern_in", "chain", "shift", "const_ps", "const", "row"))

    x1_d = io["x1"].rearrange("b (t p) c -> b p t c", p=P)
    out_d = io["out"].rearrange("b (t p) c -> b p t c", p=P)
    mod_rows = io["mod_rows"]
    FIRST, LAST = 4, NB - 2

    def there(n):
        return not isinstance(n, int) or 0 <= n < NB

    def iterations(eng, body):
        for b in range(-2, FIRST):
            body(b, b // 2, b % 2)
        with eng.Fori(0, (LAST - FIRST) // 2) as i:
            for par in range(2):
                body(i * 2 + (FIRST + par), i + FIRST // 2, par)
        for b in range(LAST, NB + 1):
            body(b, b // 2, b % 2)

    def previous(b, t):
        return (b, t - 1) if t else (b - 1, NT - 1)

    def back(b, t, steps):
        for _ in range(steps):
            b, t = previous(b, t)
        return b, t

    def tile_of(b, t):
        return NT * b + t

    with nc.Block() as block:
        @block.sync
        def _(sp):
            def constants():
                for a, n in ((ln1_g, "ln1_g"), (ln1_b, "ln1_b"), (ln2_b, "ln2_b")):
                    sp.dma_start(a[:, :], io[n]).then_inc(const_in, 16)
                sp.dma_start(b1_two[:, :], io["b1"].partition_broadcast(2)).then_inc(const_in, 16)
                sp.dma_start(g2[:, :], io["ln2_g"].partition_broadcast(P)).then_inc(const_in, 16)
                sp.dma_start(b2_all[:, :], io["b2"].partition_broadcast(P)).then_inc(const_in, 16)
                sp.dma_start(tern1[:, :].bitcast(F32), io["tern"][:, 0:KC * HID]).then_inc(tern_in, 16)
                sp.dma_start(tern2[:, :].bitcast(F32), io["tern"][:, KC * HID:]).then_inc(tern_in, 16)

            def body(b, hb, par):
                odd = 1 - par
                if there(b + 2):
                    wait(sp, xh_ok, b + 1)
                    sp.dma_start(x1[par][:, :, :], x1_d[b + 2]).then_inc(x1_in[par], 16)
                    wait(sp, h0_ok, b + 1)
                    sp.dma_start(shift_scale[par][:, :, :],
                                 mod_rows[b + 2, 3 * C:5 * C].rearrange("(a c) -> a c", a=2).partition_broadcast(P)).then_inc(ss_in[par], 16)
                if there(b):
                    wait(sp, out_left[par], 16 * hb)
                    sp.dma_start(base[par][:, :, :], x1_d[b]).then_inc(base_in[par], 16)
                if isinstance(b, int) and b == -2:
                    constants()
                if there(b + 1):
                    wait(sp, y_ok, NT * b)
                    sp.dma_start(gate[odd][:, :], mod_rows[b + 1, 5 * C:6 * C].partition_broadcast(P)).then_inc(gate_in[odd], 16)
                if there(b - 1):
                    sp.wait_ge(out_ok, NT * b)
                    sp.dma_start(out_d[b - 1], base[odd][:, :, :]).then_inc(out_left[odd], 16)

            iterations(sp, body)
            for i in range(2):
                sp.wait_ge(out_left[i], 16 * (NB // 2))

        @block.gpsimd
        def _(pool):
            pool.memset(half_pow[:, :], -0.5).then_inc(pow_ok, 1)
            pool.wait_ge(pow_ok, 1)

            def rstd(i, n):
                pool.wait_ge(ag_ok[i], n + 1)
                wait_apart(pool, (xh_ok, h1_ok)[i], n, passed[0])
                pool.tensor_scalar(ve[i][:, :], mv[i][:, :, 1], EPS, None, ALU.add).then_inc(ve_ok[i], 1)
                pool.wait_ge(ve_ok[i], n + 1)
                pool.tensor_tensor(rs[i][:, :], ve[i][:, :], half_pow[:, :], ALU.pow).then_inc(rs_ok[i], 1)

            def body(b, hb, par):
                odd = 1 - par
                n = b + 1
                for t in range(NT):
                    mb, mt = previous(b, t)
                    if there(mb):
                        tile = tile_of(mb, mt)
                        pool.wait_ge(usq_ok, tile + 1)
                        wait_apart(pool, y_ok, tile - 3, passed[0])
                        pool.tensor_scalar(uve[mt % 2][:, :], usq[mt % 2][:, :], 1.0 / HID, EPS, ALU.mult, ALU.add).then_inc(uve_ok, 1)
                        pool.wait_ge(uve_ok, tile + 1)
                        pool.tensor_tensor(urs[mt][:, :], uve[mt % 2][:, :], half_pow[:, 0:1], ALU.pow).then_inc(urs_ok, 1)
                    if there(b - 1):
                        pool.wait_ge(y_ok, tile_of(b - 1, t) + 1)
                        pool.tensor_tensor(base[odd][:, t, :], base[odd][:, t, :], y[t % 2][:, :], ALU.add).then_inc(out_ok, 1)
                    if there(n) and t == 0:
                        rstd(1, n)
                    if there(n) and t >= 2:
                        j = t - 2
                        pool.wait_ge(hhi_ok, 2 * n + j + 1)
                        wait(pool, up_ok, NT * (n - 1))
                        pool.tensor_tensor(h_lo[odd][:, :, 2 * P * j:2 * P * j + 2 * P], hf[j][:, :, :],
                                           h_hi[odd][:, :, 2 * P * j:2 * P * j + 2 * P].bitcast(F32),
                                           ALU.subtract).then_inc(hlo_ok, 1)
                    if there(b + 2) and t == 1:
                        rstd(0, b + 2)
                    if there(b + 2) and t == 2:
                        pool.wait_ge(xh_ok, b + 3)
                        pool.wait_ge(ss_in[par], 16 * (hb + 2))
                        wait(pool, h1_ok, b + 2)
                        ss = shift_scale[par]
                        pool.tensor_tensor(h0[:, :, :], xh[:, :, :], ss[:, 1, :].unsqueeze(1).to_broadcast([P, NT, C]),
                                           ALU.mult).then_inc(scaled_ok, 1)
                        pool.wait_ge(scaled_ok, b + 3)
                        pool.tensor_tensor(h0[:, :, :], h0[:, :, :], ss[:, 0, :].unsqueeze(1).to_broadcast([P, NT, C]),
                                           ALU.add).then_inc(h0_ok, 1)
                    if there(b) and t == 3:
                        pool.wait_ge(gate_in[par], 16 * (hb + 1))
                        wait(pool, base_ok, b)
                        if isinstance(b, int) and b == 0:
                            pool.wait_ge(row_ok, 1)
                        pool.tensor_tensor(gated_const[:, :], gate[par][:, :], const_row[:, :], ALU.mult).then_inc(gc_ok, 1)
                        pool.wait_ge(gc_ok, b + 1)
                        pool.wait_ge(base_in[par], 16 * (hb + 1))
                        pool.tensor_tensor(base[par][:, :, :], base[par][:, :, :],
                                           gated_const[:, :].unsqueeze(1).to_broadcast([P, NT, C]), ALU.add).then_inc(base_ok, 1)

            iterations(pool, body)

        @block.scalar
        def _(act):
            def gain_and_shift(n, j):
                if isinstance(n, int) and n == 0:
                    act.wait_ge(const_in, 16 * 6)
                act.wait_ge(xt_ok, 2 * n + j + 1)
                wait(act, hlo_ok, 2 * (n - 1) + j + 1)
                for k in range(KC):
                    ins = act.activation(hf[j][:, k, :].rearrange("p (t c) -> p t c", t=2),
                                         xt_ps[:, :].rearrange("p (t k c) -> p k t c", t=2, k=KC)[:, k],
                                         ACT.Identity, bias=ln1_b[:, k:k + 1], scale=ln1_g[:, k:k + 1])
                ins.then_inc(hf_ok, 1)

            def body(b, hb, par):
                odd = 1 - par
                n = b + 1
                for t in range(NT):
                    bb, bt = back(b, t, 2)
                    if there(bb):
                        tile = tile_of(bb, bt)
                        act.wait_ge(ut_ok, tile + 1)
                        wait(act, down_ok, tile - 1)
                        act.activation(u_hi[bt % 2][:, :], ut_ps[:, :], ACT.Copy).then_inc(uhi_ok, 1)
                    if t >= 2 and there(n):
                        gain_and_shift(n, t - 2)
                    mb, mt = previous(b, t)
                    if there(mb):
                        tile = tile_of(mb, mt)
                        act.wait_ge(mean_ok, tile + 1)
                        wait(act, uve_ok, tile - 1)
                        wait(act, usq_ok, tile)
                        act.activation(squares[:, :], u_act[mt % 2][:, :], ACT.Square, bias=minus_mean[mt % 2][:, 0:1],
                                       accum_out=usq[mt % 2][:, 0:1]).then_inc(usq_ok, 1)
                    if there(b):
                        tile = tile_of(b, t)
                        act.wait_ge(up_ok, tile + 1)
                        wait(act, uc_ok, tile - 1)
                        act.activation(u_act[t % 2][:, :], up_ps[t % 2][:, :], ACT.Gelu,
                                       scale=inv_scale[:, 0:1], accum_out=usum[t % 2][:, 0:1]).then_inc(gelu_ok, 1)

            iterations(act, body)

        @block.vector
        def _(dve):
            links = 0

            def link(ins):
                nonlocal links
                links += 1
                ins.then_inc(chain, 1)
                dve.wait_ge(chain, links)

            def constants():
                dve.wait_ge(const_in, 16 * 6)
                dve.tensor_copy(shift_l[:, :, :], ln2_b[:, :].unsqueeze(2).to_broadcast([P, KH, P])).then_inc(shift_ok, 1)
                link(dve.memset(tmp_c[0:2, 0:P], 1.0))
                link(dve.tensor_copy(ones2[:, :], tmp_c[0:2, 0:P]))
                link(dve.tensor_scalar(b1_s[:, :], b1_two[:, :], scale[0:2, 0:1], None, ALU.mult))
                link(dve.tensor_copy(b1_hi[:, :], b1_s[:, :]))
                link(dve.tensor_scalar(minus_row1[:, :], ident[0:2, 1:2], -1.0, None, ALU.mult))
                dve.scalar_tensor_tensor(out=bias1[:, :], in0=b1_hi[:, :].bitcast(F32), scalar=minus_row1[:, 0:1],
                                         in1=b1_s[:, :], op0=ALU.mult, op1=ALU.add)
                dve.tensor_scalar(gain2[:, :], g2[:, :], inv_scale[:, 1:2], None, ALU.mult).then_inc(const_ok, 1)

            def constant_row():
                dve.wait_ge(const_ps_ok, 1)
                link(dve.tensor_scalar(tmp_c[:, :], down_ps[:, 0:C], inv_scale[:, 1:2], None, ALU.mult))
                dve.tensor_tensor(const_row[:, :], tmp_c[:, :], b2_all[:, :], ALU.add).then_inc(row_ok, 1)

            def statistics(i, n, src):
                wait(dve, ag_ok[i], n)
                for t in range(NT):
                    ins = dve.bn_stats(stats[:, t, :], src[:, t, :])
                ins.then_inc(st_ok[i], 1)
                wait_apart(dve, st_ok[i], n + 1, passed[1])
                for t in range(NT):
                    ins = dve.bn_aggr(mv[i][:, t, :], stats[:, t, :])
                ins.then_inc(ag_ok[i], 1)

            def normalise(i, n, dst, src, done):
                dve.wait_ge(rs_ok[i], n + 1)
                for t in range(NT):
                    ins = dve.tensor_scalar(dst[:, t, :], src[:, t, :], mv[i][:, t, 0:1], rs[i][:, t:t + 1], ALU.subtract, ALU.mult)
                ins.then_inc(done, 1)

            def round_h(n, odd, j):
                dve.wait_ge(hf_ok, 2 * n + j + 1)
                wait(dve, up_ok, NT * (n - 1))
                dve.tensor_copy(h_hi[odd][:, :, 2 * P * j:2 * P * j + 2 * P], hf[j][:, :, :]).then_inc(hhi_ok, 1)

            def body(b, hb, par):
                odd = 1 - par
                n = b + 1
                if isinstance(b, int) and b == -1:
                    constants()
                if isinstance(b, int) and b == 0:
                    constant_row()
                for t in range(NT):
                    if there(b - 1):
                        tile = tile_of(b - 1, t)
                        dve.wait_ge(down_ok, tile + 1)
                        dve.wait_ge(urs_ok, tile + 1)
                        dve.wait_ge(gate_in[odd], 16 * (hb + (par - 1) // 2 + 1))
                        wait(dve, out_ok, tile - 1)
                        dve.scalar_tensor_tensor(out=y[t % 2][:, :], in0=down_ps[:, C * (t % 2):C * (t % 2) + C],
                                                 scalar=urs[t][:, 0:1], in1=gate[odd][:, :],
                                                 op0=ALU.mult, op1=ALU.mult).then_inc(y_ok, 1)
                    mb, mt = previous(b, t)
                    if there(mb):
                        tile = tile_of(mb, mt)
                        dve.wait_ge(gelu_ok, tile + 1)
                        wait(dve, usq_ok, tile - 1)
                        dve.tensor_scalar(minus_mean[mt % 2][:, :], usum[mt % 2][:, :], -1.0 / HID, None, ALU.mult).then_inc(mean_ok, 1)
                        dve.wait_ge(mean_ok, tile + 1)
                        wait(dve, ut_ok, tile - 1)
                        dve.scalar_tensor_tensor(out=u_c[mt % 2][:, :], in0=u_act[mt % 2][:, :], scalar=minus_mean[mt % 2][:, 0:1],
                                                 in1=gain2[:, :], op0=ALU.add, op1=ALU.mult).then_inc(uc_ok, 1)
                    bb, bt = back(b, t, 2)
                    if there(bb):
                        tile = tile_of(bb, bt)
                        dve.wait_ge(uhi_ok, tile + 1)
                        wait(dve, down_ok, tile - 1)
                        dve.tensor_tensor(u_lo[bt % 2][:, :], ut_ps[:, :], u_hi[bt % 2][:, :].bitcast(F32),
                                          ALU.subtract).then_inc(ulo_ok, 1)
                    if there(n) and t == 0:
                        dve.wait_ge(h0_ok, n + 1)
                        if not isinstance(n, int) or n > 0:
                            dve.wait_ge(h1_ok, n)
                            dve.wait_ge(ag_ok[0], n + 1)
                        statistics(1, n, h0)
                    if there(n) and t == 1:
                        wait(dve, xt_ok, 2 * n)
                        normalise(1, n, h1, h0, h1_ok)
                    if there(n) and t >= 2:
                        round_h(n, odd, t - 2)
                    if there(b + 2) and t == 1:
                        dve.wait_ge(x1_in[par], 16 * (hb + 2))
                        wait(dve, xh_ok, b + 2)
                        wait(dve, ag_ok[1], b + 2)
                        statistics(0, b + 2, x1[par])
                    if there(b + 2) and t == 2:
                        wait(dve, scaled_ok, b + 2)
                        normalise(0, b + 2, xh, x1[par], xh_ok)

            iterations(dve, body)

        @block.tensor
        def _(pe):
            def transpose_h(n, j):
                pe.wait_ge(h1_ok, n + 1)
                wait(pe, hf_ok, 2 * n + j)
                for tt in range(2):
                    for k in range(KC):
                        ins = pe.transpose(xt_ps[:, P * (KC * tt + k):P * (KC * tt + k) + P],
                                           h1[:, 2 * j + tt, P * k:P * k + P], ident[:, :])
                ins.then_inc(xt_ok, 1)

            def body(b, hb, par):
                odd = 1 - par
                n = b + 1
                if isinstance(b, int) and b == 0:
                    pe.wait_ge(const_ok, 1)
                for t in range(NT):
                    if isinstance(b, int) and b == -1 and t == 1:
                        pe.wait_ge(tern_in, 16 * 2)
                        pe.wait_ge(shift_ok, 1)
                        for k in range(KH):
                            ins = pe.matmul(down_ps[:, 0:C], shift_l[:, k, :], tern2[:, C * k:C * k + C].bitcast(F32),
                                            start=(k == 0), stop=(k == KH - 1))
                        ins.then_inc(const_ps_ok, 1)
                    bb, bt = back(b, t, 2)
                    if there(bb):
                        tile = tile_of(bb, bt)
                        pe.wait_ge(uc_ok, tile + 1)
                        wait(pe, ulo_ok, tile)
                        for i in range(KH):
                            ins = pe.transpose(ut_ps[:, P * i:P * i + P], u_c[bt % 2][:, P * i:P * i + P], ident[:, :])
                        ins.then_inc(ut_ok, 1)
                    if t >= 2 and there(n):
                        transpose_h(n, t - 2)
                    if there(b):
                        tile = NT * b + t
                        pe.wait_ge(hlo_ok, 2 * b + t // 2 + 1)
                        wait(pe, gelu_ok, tile - 1)
                        tok = slice(P * t, P * t + P)
                        for half in range(2):
                            out = up_ps[t % 2][:, 512 * half:512 * half + 512]
                            pe.matmul(out, ones2[:, :], bias1[:, 512 * half:512 * half + 512], start=True, stop=False)
                            for k in range(KC):
                                w = tern1[:, HID * k + 512 * half:HID * k + 512 * half + 512]
                                pe.matmul(out, h_lo[par][:, k, tok], w, start=False, stop=False)
                                ins = pe.matmul(out, h_hi[par][:, k, tok], w, start=False, stop=(k == KC - 1))
                        ins.then_inc(up_ok, 1)
                    bb, bt = back(b, t, 3)
                    if there(bb):
                        tile = tile_of(bb, bt)
                        pe.wait_ge(ulo_ok, tile + 1)
                        if isinstance(bb, int) and tile == 0:
                            pe.wait_ge(row_ok, 1)
                        wait(pe, y_ok, tile)
                        out = down_ps[:, C * (bt % 2):C * (bt % 2) + C]
                        for i in range(KH):
                            w = tern2[:, C * i:C * i + C]
                            pe.matmul(out, u_lo[bt % 2][:, P * i:P * i + P], w, start=(i == 0), stop=False)
                            ins = pe.matmul(out, u_hi[bt % 2][:, P * i:P * i + P], w, start=False, stop=(i == KH - 1))
                        ins.then_inc(down_ok, 1)

            iterations(pe, body)


def adaln_block(nc, io):
    NB = io["x"].shape[0]
    io["mod_rows"] = nc.dram_tensor("mod_rows", [NB, MODS], F32, kind="Internal").ap()
    io["tern"] = nc.dram_tensor("tern", [P, KC * HID + KH * C], F32, kind="Internal").ap()
    io["x1"] = nc.dram_tensor("x1_rows", [NB, T, C], F32, kind="Internal").ap()
    with ExitStack() as whole:
        def sb(name, shape, dt=F32):
            return whole.enter_context(nc.sbuf_tensor(name, shape, dt))

        keep = {"mod_cols": sb("mod_cols", [P, 4, NB]), "ident": sb("ident", [P, P]),
                "scale": sb("scale", [P, 2]), "inv_scale": sb("inv_scale", [P, 2])}
        with ExitStack() as ctx:
            attention_phase(nc, io, keep, ctx)
        with ExitStack() as ctx:
            ffn_phase(nc, io, keep, ctx)


def round_12(a):
    m, e = np.frexp(a)
    return np.ldexp(np.rint(np.ldexp(m, 12)), e - 12)


def alibi_rows():
    start = 2.0 ** (-8.0 / HEADS)
    slopes = np.asarray([start * start ** i for i in range(HEADS)], np.float32).astype(np.float64)
    pos = np.arange(T, dtype=np.float64)
    q = np.zeros((P, PAIRS, T))
    k = np.zeros((P, PAIRS, T))
    for head, slope in enumerate(slopes):
        base, pair = 64 * (head % 2), head // 2
        hi = round_12(slope)
        left = -slope * pos
        terms = [(hi + 0 * pos, pos), (slope - hi + 0 * pos, pos)]
        for _ in range(3):
            piece = round_12(left)
            terms.append((piece, 1 + 0 * pos))
            left = left - piece
        for row, (a, b) in enumerate(terms):
            q[base + 4 * row + 3, pair], k[base + 4 * row + 3, pair] = a, b
        k[base + M_ROW, pair] = 1.0
    return tuple(np.ascontiguousarray(a[3::4].reshape(P // 4, NT, 2 * T).transpose(1, 0, 2)).reshape(P, 2 * T).astype(np.float32)
                 for a in (q, k))


def constants():
    q, k = alibi_rows()
    mask = np.where(np.arange(P)[None, :] > np.arange(P)[:, None], MASKED, 0.0).astype(np.float32)
    return {"q_rows": q, "k_rows": k, "mask": np.stack([mask, mask.T], 1), "ident": np.eye(P, dtype=np.float32)}


def by_partition(vector):
    return np.asarray(vector).reshape(-1, P).T


def arrays_of(L0_attn_x, L0_attn_Wqkv, L0_attn_Wout, L0_ffn_ln1_g, L0_ffn_ln1_b, L0_ffn_w1, L0_ffn_b1,
              L0_ffn_ln2_g, L0_ffn_ln2_b, L0_ffn_w2, L0_ffn_b2, L0_c, L0_wmod):
    a = {"x": L0_attn_x, "w_qkv": L0_attn_Wqkv, "w_out": L0_attn_Wout, "ln1_g": by_partition(L0_ffn_ln1_g), "ln1_b": by_partition(L0_ffn_ln1_b),
         "w1": np.asarray(L0_ffn_w1).T, "b1": L0_ffn_b1, "ln2_g": L0_ffn_ln2_g, "ln2_b": by_partition(L0_ffn_ln2_b),
         "w2": np.asarray(L0_ffn_w2).T, "b2": L0_ffn_b2, "c_t": np.asarray(L0_c).T, "w_mod": L0_wmod}
    a = {n: np.ascontiguousarray(v) for n, v in a.items()}
    a.update(constants())
    return a


def kernel(**inputs):
    import concourse.bacc as bacc
    from concourse.bass_utils import run_bass_kernel_spmd

    nc = bacc.Bacc("TRN2", target_bir_lowering=False, num_devices=1)
    arrays = arrays_of(**inputs)
    io = {n: nc.dram_tensor(f"in_{n}", a.shape, mybir.dt.from_np(a.dtype), kind="ExternalInput").ap()
          for n, a in arrays.items()}
    io["out"] = nc.dram_tensor("out", arrays["x"].shape, F32, kind="ExternalOutput").ap()
    adaln_block(nc, io)
    result = run_bass_kernel_spmd(nc, [{f"in_{n}": a for n, a in arrays.items()}], core_ids=[0])
    return result.results[0]["out"]
```
